# Optimizing a Trainium2 kernel written in Bass

```python
import numpy as np
import jax
import jax.numpy as jnp

def _softmax(x, axis=-1):
    return jax.nn.softmax(x, axis=axis)

def _gelu(x):
    return jax.nn.gelu(x, approximate=True)

def _silu(x):
    return jax.nn.silu(x)

def _sigmoid(x):
    return jax.nn.sigmoid(x)

def _layernorm(x, axis=-1, eps=1e-05):
    m = jnp.mean(x, axis=axis, keepdims=True)
    v = jnp.var(x, axis=axis, keepdims=True)
    return (x - m) / jnp.sqrt(v + eps)

def _scatter_add(tgt, idx, src, axis=0):
    return tgt.at[idx].add(src)

def _segment_sum(src, seg, n):
    return jax.ops.segment_sum(src, seg, n)
kernel_name = 'mk_gnn_resnorm_d4_gnn_r32_95d23c'

def setup_inputs(seed: int=0):
    np.random.seed(seed)
    _w = jnp.asarray

    def _rec_inputs():
        import jax
        import jax.numpy as jnp
        _gk = jax.random.key(seed)
        x = -0.000202 + 1 * jax.random.normal(jax.random.fold_in(_gk, 1), (3125, 128), jnp.float32)
        src = jax.random.randint(jax.random.fold_in(_gk, 2), (100000,), 0, 3125, jnp.int32)
        dst = jnp.minimum((3125 * jax.random.uniform(jax.random.fold_in(_gk, 3), (100000,)) ** 2.0).astype(jnp.int32), 99999)
        _o = jnp.argsort(dst, stable=True)
        src = src[_o]
        dst = dst[_o]
        return (x, src, dst)
    x, src, dst = _rec_inputs()

    def _L0_gnn_setup():
        import jax, jax.numpy as jnp
        import numpy as np
        BN_EPS = 1e-05

        def _batchnorm(h, gamma, beta):
            mean = jnp.mean(h, axis=0)
            var = jnp.var(h, axis=0)
            return (h - mean) * jax.lax.rsqrt(var + BN_EPS) * gamma + beta
        N, E, D_IN, D_OUT = (50000, 25000, 128, 128)
        key = jax.random.key(seed)
        ks = jax.random.split(key, 6)
        x = jax.random.normal(ks[0], (N, D_IN), dtype=jnp.float32)
        edge_index = jax.random.randint(ks[1], (2, E), 0, N, dtype=jnp.int32)
        lim1 = 1.0 / np.sqrt(2 * D_IN)
        lim2 = 1.0 / np.sqrt(D_OUT)
        W1 = jax.random.uniform(ks[2], (D_OUT, 2 * D_IN), jnp.float32, -lim1, lim1)
        b1 = jax.random.uniform(ks[3], (D_OUT,), jnp.float32, -lim1, lim1)
        W2 = jax.random.uniform(ks[4], (D_OUT, D_OUT), jnp.float32, -lim2, lim2)
        b2 = jax.random.uniform(ks[5], (D_OUT,), jnp.float32, -lim2, lim2)
        g1 = jnp.ones((D_OUT,), jnp.float32)
        be1 = jnp.zeros((D_OUT,), jnp.float32)
        g2 = jnp.ones((D_OUT,), jnp.float32)
        be2 = jnp.zeros((D_OUT,), jnp.float32)
        return {'x': x, 'edge_index': edge_index, 'W1': W1, 'b1': b1, 'g1': g1, 'be1': be1, 'W2': W2, 'b2': b2, 'g2': g2, 'be2': be2}
    _L0_gnn_all = _L0_gnn_setup()
    _L0_gnn_in = {k: v for k, v in _L0_gnn_all.items() if k in ('W1', 'b1', 'g1', 'be1', 'W2', 'b2', 'g2', 'be2')}
    del _L0_gnn_all

    def _L1_gnn_setup():
        import jax, jax.numpy as jnp
        import numpy as np
        N, E, DIN, DOUT = (50000, 625000, 128, 128)

        def gcn_conv(x, W, b, src, dst, n):
            loops = jnp.arange(n, dtype=src.dtype)
            src2 = jnp.concatenate([src, loops])
            dst2 = jnp.concatenate([dst, loops])
            ones = jnp.ones(src2.shape[0], dtype=x.dtype)
            deg = jax.ops.segment_sum(ones, dst2, num_segments=n)
            dinv = jnp.where(deg > 0, jax.lax.rsqrt(deg), 0.0)
            norm = dinv[src2] * dinv[dst2]
            h = x @ W
            msgs = h[src2] * norm[:, None]
            out = jax.ops.segment_sum(msgs, dst2, num_segments=n)
            return out + b
        key = jax.random.key(seed)
        k = jax.random.split(key, 4)
        x = jax.random.normal(k[0], (N, DIN), dtype=jnp.float32)
        edge_index = jax.random.randint(k[1], (2, E), 0, N, dtype=jnp.int32)
        s = 1.0 / np.sqrt(DIN)
        W_fwd = jax.random.uniform(k[2], (DIN, DOUT), jnp.float32, -s, s)
        W_bwd = jax.random.uniform(k[3], (DIN, DOUT), jnp.float32, -s, s)
        b_fwd = jnp.zeros((DOUT,), jnp.float32)
        b_bwd = jnp.zeros((DOUT,), jnp.float32)
        return {'x': x, 'edge_index': edge_index, 'W_fwd': W_fwd, 'b_fwd': b_fwd, 'W_bwd': W_bwd, 'b_bwd': b_bwd}
    _L1_gnn_all = _L1_gnn_setup()
    _L1_gnn_in = {k: v for k, v in _L1_gnn_all.items() if k in ('W_fwd', 'b_fwd', 'W_bwd', 'b_bwd')}
    del _L1_gnn_all

    def _L2_gnn_setup():
        import jax, jax.numpy as jnp
        import numpy as np
        N_NODES = 3125
        N_EDGES = 50000
        HIDDEN = 128
        IN_CH = 128

        def _pairwise_weight(Wp):
            W0 = jnp.triu(Wp[:, :-2], 1)
            W0 = W0 + W0.T
            q = Wp[:, -2]
            r = Wp[:, -1]
            return W0 + jnp.diag(q * jnp.sum(jnp.abs(W0), axis=1) + r)
        key = jax.random.key(seed)
        ks = jax.random.split(key, 7)
        x = jax.random.normal(ks[0], (N_NODES, IN_CH), dtype=jnp.float32)
        row = jax.random.randint(ks[1], (N_EDGES,), 0, N_NODES)
        off = jax.random.randint(ks[2], (N_EDGES,), 1, N_NODES)
        col = (row + off) % N_NODES
        edge_index = jnp.stack([row, col], axis=0).astype(jnp.int64)
        Wi = jax.random.normal(ks[3], (HIDDEN, IN_CH), dtype=jnp.float32) * (1.0 / np.sqrt(IN_CH))
        bi = jax.random.normal(ks[4], (HIDDEN,), dtype=jnp.float32) * 0.01
        A = jax.random.normal(ks[5], (HIDDEN, HIDDEN), dtype=jnp.float32) * (1.0 / np.sqrt(HIDDEN))
        Wp = jax.random.normal(ks[6], (HIDDEN, HIDDEN + 2), dtype=jnp.float32) * (1.0 / np.sqrt(HIDDEN))
        return {'x': x, 'edge_index': edge_index, 'Wi': Wi, 'bi': bi, 'A': A, 'Wp': Wp, 'num_layers': 4}
    _L2_gnn_all = _L2_gnn_setup()
    _L2_gnn_in = {k: v for k, v in _L2_gnn_all.items() if k in ('Wi', 'bi', 'A', 'Wp')}
    del _L2_gnn_all

    def _L3_gnn_setup():
        import jax, jax.numpy as jnp
        import numpy as np
        DIM = 128
        NUM_HEADS = 8
        HEAD_DIM = DIM // NUM_HEADS
        N_NODES = 50000
        N_EDGES = 25000
        key = jax.random.key(seed)
        ks = jax.random.split(key, 10)
        scale = 1.0 / np.sqrt(DIM)
        x = jax.random.normal(ks[0], (N_NODES, DIM), dtype=jnp.float32)
        edge_index = jax.random.randint(ks[1], (2, N_EDGES), 0, N_NODES, dtype=jnp.int64)
        Wq = jax.random.normal(ks[2], (DIM, DIM), dtype=jnp.float32) * scale
        bq = jnp.zeros((DIM,), dtype=jnp.float32)
        Wk = jax.random.normal(ks[3], (DIM, DIM), dtype=jnp.float32) * scale
        bk = jnp.zeros((DIM,), dtype=jnp.float32)
        Wv = jax.random.normal(ks[4], (DIM, DIM), dtype=jnp.float32) * scale
        bv = jnp.zeros((DIM,), dtype=jnp.float32)
        Wo = jax.random.normal(ks[5], (DIM, DIM), dtype=jnp.float32) * scale
        bo = jnp.zeros((DIM,), dtype=jnp.float32)
        return {'x': x, 'edge_index': edge_index, 'Wq': Wq, 'bq': bq, 'Wk': Wk, 'bk': bk, 'Wv': Wv, 'bv': bv, 'Wo': Wo, 'bo': bo}
    _L3_gnn_all = _L3_gnn_setup()
    _L3_gnn_in = {k: v for k, v in _L3_gnn_all.items() if k in ('Wq', 'bq', 'Wk', 'bk', 'Wv', 'bv', 'Wo', 'bo')}
    del _L3_gnn_all
    return {'x': x, 'src': src, 'dst': dst, 'L0_gnn_W1': _L0_gnn_in['W1'], 'L0_gnn_b1': _L0_gnn_in['b1'], 'L0_gnn_g1': _L0_gnn_in['g1'], 'L0_gnn_be1': _L0_gnn_in['be1'], 'L0_gnn_W2': _L0_gnn_in['W2'], 'L0_gnn_b2': _L0_gnn_in['b2'], 'L0_gnn_g2': _L0_gnn_in['g2'], 'L0_gnn_be2': _L0_gnn_in['be2'], 'L1_gnn_W_fwd': _L1_gnn_in['W_fwd'], 'L1_gnn_b_fwd': _L1_gnn_in['b_fwd'], 'L1_gnn_W_bwd': _L1_gnn_in['W_bwd'], 'L1_gnn_b_bwd': _L1_gnn_in['b_bwd'], 'L2_gnn_Wi': _L2_gnn_in['Wi'], 'L2_gnn_bi': _L2_gnn_in['bi'], 'L2_gnn_A': _L2_gnn_in['A'], 'L2_gnn_Wp': _L2_gnn_in['Wp'], 'L3_gnn_Wq': _L3_gnn_in['Wq'], 'L3_gnn_bq': _L3_gnn_in['bq'], 'L3_gnn_Wk': _L3_gnn_in['Wk'], 'L3_gnn_bk': _L3_gnn_in['bk'], 'L3_gnn_Wv': _L3_gnn_in['Wv'], 'L3_gnn_bv': _L3_gnn_in['bv'], 'L3_gnn_Wo': _L3_gnn_in['Wo'], 'L3_gnn_bo': _L3_gnn_in['bo']}

def reference(x, src, dst, L0_gnn_W1, L0_gnn_b1, L0_gnn_g1, L0_gnn_be1, L0_gnn_W2, L0_gnn_b2, L0_gnn_g2, L0_gnn_be2, L1_gnn_W_fwd, L1_gnn_b_fwd, L1_gnn_W_bwd, L1_gnn_b_bwd, L2_gnn_Wi, L2_gnn_bi, L2_gnn_A, L2_gnn_Wp, L3_gnn_Wq, L3_gnn_bq, L3_gnn_Wk, L3_gnn_bk, L3_gnn_Wv, L3_gnn_bv, L3_gnn_Wo, L3_gnn_bo):
    import jax
    import jax.numpy as jnp

    def _L0_gnn_ref(x, edge_index, W1, b1, g1, be1, W2, b2, g2, be2):
        import jax, jax.numpy as jnp
        import numpy as np
        BN_EPS = 1e-05

        def _batchnorm(h, gamma, beta):
            mean = jnp.mean(h, axis=0)
            var = jnp.var(h, axis=0)
            return (h - mean) * jax.lax.rsqrt(var + BN_EPS) * gamma + beta
        src, dst = (edge_index[0], edge_index[1])
        edge_features = jnp.concatenate([x[src], x[dst]], axis=1)
        h = edge_features @ W1.T + b1
        h = jax.nn.relu(_batchnorm(h, g1, be1))
        h = h @ W2.T + b2
        edge_updates = jax.nn.relu(_batchnorm(h, g2, be2))
        x_out = jax.ops.segment_sum(edge_updates, dst, num_segments=x.shape[0])
        return x_out

    def _L1_gnn_ref(x, edge_index, W_fwd, b_fwd, W_bwd, b_bwd):
        import jax, jax.numpy as jnp
        import numpy as np
        N, E, DIN, DOUT = (50000, 625000, 128, 128)

        def gcn_conv(x, W, b, src, dst, n):
            loops = jnp.arange(n, dtype=src.dtype)
            src2 = jnp.concatenate([src, loops])
            dst2 = jnp.concatenate([dst, loops])
            ones = jnp.ones(src2.shape[0], dtype=x.dtype)
            deg = jax.ops.segment_sum(ones, dst2, num_segments=n)
            dinv = jnp.where(deg > 0, jax.lax.rsqrt(deg), 0.0)
            norm = dinv[src2] * dinv[dst2]
            h = x @ W
            msgs = h[src2] * norm[:, None]
            out = jax.ops.segment_sum(msgs, dst2, num_segments=n)
            return out + b
        src, dst = (edge_index[0], edge_index[1])
        n = x.shape[0]
        x_forward = gcn_conv(x, W_fwd, b_fwd, src, dst, n)
        x_backward = gcn_conv(x, W_bwd, b_bwd, dst, src, n)
        return jax.nn.relu(x_forward + x_backward)

    def _L2_gnn_ref(x, edge_index, Wi, bi, A, Wp, num_layers):
        import jax, jax.numpy as jnp
        import numpy as np
        N_NODES = 3125
        N_EDGES = 50000
        HIDDEN = 128
        IN_CH = 128

        def _pairwise_weight(Wp):
            W0 = jnp.triu(Wp[:, :-2], 1)
            W0 = W0 + W0.T
            q = Wp[:, -2]
            r = Wp[:, -1]
            return W0 + jnp.diag(q * jnp.sum(jnp.abs(W0), axis=1) + r)
        n = x.shape[0]
        row, col = (edge_index[0], edge_index[1])
        deg = jax.ops.segment_sum(jnp.ones_like(col, dtype=x.dtype), col, num_segments=n)
        dinv = jnp.where(deg > 0, jax.lax.rsqrt(jnp.maximum(deg, 1.0)), 0.0)
        norm = dinv[row] * dinv[col]
        Weff = _pairwise_weight(Wp)
        Asym = A - A.T
        h = jax.nn.relu(x @ Wi.T + bi)
        for _ in range(num_layers):
            out = h @ Weff.T
            msg = norm[:, None] * out[row]
            agg = jax.ops.segment_sum(msg, col, num_segments=n)
            delta = agg - jax.nn.relu(h @ Asym.T)
            h = h + jax.nn.relu(jnp.tanh(delta))
        return h

    def _L3_gnn_ref(x, edge_index, Wq, bq, Wk, bk, Wv, bv, Wo, bo):
        import jax, jax.numpy as jnp
        import numpy as np
        DIM = 128
        NUM_HEADS = 8
        HEAD_DIM = DIM // NUM_HEADS
        N_NODES = 50000
        N_EDGES = 25000
        n = x.shape[0]
        tgt = edge_index[0]
        src = edge_index[1]
        q = (x @ Wq.T + bq).reshape(n, NUM_HEADS, HEAD_DIM)
        k = (x @ Wk.T + bk).reshape(n, NUM_HEADS, HEAD_DIM)
        v = (x @ Wv.T + bv).reshape(n, NUM_HEADS, HEAD_DIM)
        scores = jnp.einsum('ehd,ehd->eh', q[src], k[tgt]) / np.sqrt(HEAD_DIM).astype(np.float32)
        m = jax.ops.segment_max(scores, tgt, num_segments=n)
        m = jax.lax.stop_gradient(m)
        p = jnp.exp(scores - m[tgt])
        s = jax.ops.segment_sum(p, tgt, num_segments=n)
        probs = p / s[tgt]
        weighted = v[src] * probs[..., None]
        agg = jax.ops.segment_sum(weighted, tgt, num_segments=n)
        out = agg.reshape(n, DIM) @ Wo.T + bo
        return out
    edge_index = jnp.stack([src, dst])
    x = _layernorm(x + _L0_gnn_ref(x, edge_index, L0_gnn_W1, L0_gnn_b1, L0_gnn_g1, L0_gnn_be1, L0_gnn_W2, L0_gnn_b2, L0_gnn_g2, L0_gnn_be2), axis=-1)
    x = _layernorm(x + _L1_gnn_ref(x, edge_index, L1_gnn_W_fwd, L1_gnn_b_fwd, L1_gnn_W_bwd, L1_gnn_b_bwd), axis=-1)
    x = _layernorm(x + _L2_gnn_ref(x, edge_index, L2_gnn_Wi, L2_gnn_bi, L2_gnn_A, L2_gnn_Wp, 4), axis=-1)
    x = _layernorm(x + _L3_gnn_ref(x, edge_index, L3_gnn_Wq, L3_gnn_bq, L3_gnn_Wk, L3_gnn_bk, L3_gnn_Wv, L3_gnn_bv, L3_gnn_Wo, L3_gnn_bo), axis=-1)
    return x

_drawn_inputs = setup_inputs


def setup_inputs(seed=0):
    import zlib

    import numpy as np

    out = dict(_drawn_inputs(seed))
    spreads = {'L0_gnn_g1': (1.0, 0.2),
     'L0_gnn_be1': (0.0, 0.1),
     'L0_gnn_g2': (1.0, 0.2),
     'L0_gnn_be2': (0.0, 0.1),
     'L1_gnn_b_fwd': (0.0, 0.1),
     'L1_gnn_b_bwd': (0.0, 0.1),
     'L3_gnn_bq': (0.0, 0.8),
     'L3_gnn_bk': (0.0, 0.8),
     'L3_gnn_bv': (0.0, 0.1),
     'L3_gnn_bo': (0.0, 0.1)}
    factors = {'L0_gnn_b1': 8.0, 'L0_gnn_b2': 8.0, 'L2_gnn_bi': 4.623}
    for name, (base, spread) in spreads.items():
        noise = np.random.default_rng([zlib.crc32(name.encode()), seed]).standard_normal(out[name].shape)
        drawn = base * np.exp(spread * noise) if base else spread * noise
        out[name] = jnp.asarray(drawn.astype(out[name].dtype))
    for name, factor in factors.items():
        out[name] = (out[name] * factor).astype(out[name].dtype)
    return out
```

```python
import concourse.bass as bass
from concourse import mybir
from contextlib import ExitStack

P = 128
N = 3125
NB = -(-N // P)
NP = NB * P
E = 100000
GE = 512
NG = -(-E // GE)
EP = NG * GE
NT = EP // P
PE_EDGES = 256
NPAIR = EP // PE_EDGES
WP = 98
LAST = E - (NG - 1) * GE
EPS = 1e-5
CENTER = NP // 2
CW = 400
NC = NP // CW
BANK = 512
CHUNKS = [(c, min(BANK, NP - c)) for c in range(0, NP, BANK)]
H = 8
HD = P // H
QUADS = 2
HQ = H // QUADS
HW = 32
QK_SLOTS = ((0, 0), (0, 1), (1, 0), (1, 1), (0, 2), (2, 0))
KQK = len(QK_SLOTS) * HD
MASKED = -1e30
SC = 5
GNN_LAYERS = 4
PAIR0 = 512
VISIT0 = 64
RING = 5
STAGES = 7


def gnn(nc, ins, out, stages=9):
    f32, bf16, f16, i32 = mybir.dt.float32, mybir.dt.bfloat16, mybir.dt.float16, mybir.dt.int32
    ALU = mybir.AluOpType
    ACT = mybir.ActivationFunctionType
    AX = mybir.AxisListType
    ds = bass.ds

    a_table = nc.dram_tensor("a_table", (NP, P), f32).ap()
    a_edges = nc.dram_tensor("a_edges", (NG, P, GE), f32).ap()
    h1_edges = nc.dram_tensor("h1_edges", (P, EP), f32).ap()
    c_parts = nc.dram_tensor("c_parts", (2 * NP, NP), bf16).ap()
    pair_rows = nc.dram_tensor("pair_rows", (2, WP, NPAIR // WP), i32).ap()
    group_rows = nc.dram_tensor("group_rows", (2, WP, NG // WP), i32).ap()
    block_rows = nc.dram_tensor("block_rows", (2, NB), i32).ap()
    qk_parts = nc.dram_tensor("qk_parts", (6, P, NP), bf16).ap()
    head_sums = nc.dram_tensor("head_sums", (QUADS, P, NP), f32).ap()
    flag_row = nc.dram_tensor("flag_row", (P, 1), f32).ap()
    pairs_flat = pair_rows.rearrange("a p g -> a (p g)")
    groups_flat = group_rows.rearrange("a p g -> a (p g)")

    ctx = ExitStack()
    with ctx:
        def sem(name):
            return ctx.enter_context(nc.semaphore(name))

        at = [-(-nc.sbuf_base // 64) * 64]
        size = {f32: 4, i32: 4, bf16: 2, f16: 2}

        def sb(name, shape, dt):
            n = size[dt]
            for s in shape[1:]:
                n *= s
            t = nc.alloc_sbuf_tensor_at(name, shape, dt, offset=at[0])
            at[0] += -(-n // 64) * 64
            assert at[0] <= nc.sbuf_usable_end, (name, at[0])
            return t

        x = sb("x", [P, NP], f32)
        y = sb("y", [P, NP], f32)
        z = sb("z", [P, NP], f32)
        W = {n: sb(n, [P, a.shape[1]], f32) for n, a in ins.items() if n[0] == "W"}
        V = {n: sb(n, [P, 1], f32) for n, a in ins.items() if n[0] == "v"}
        identf = sb("identf", [P, P], f32)
        identb = sb("identb", [P, P], bf16)
        onesf = sb("onesf", [P, P], f32)
        meanf = sb("meanf", [P, P], f32)
        onesb = sb("onesb", [P, BANK], bf16)
        zerosb = sb("zerosb", [P, BANK], bf16)
        eps1 = sb("eps1", [P, 1], f32)
        iota = sb("iota", [P, NP], f16)
        nodeid = sb("nodeid", [P, NB], f32)
        src_i = sb("src_i", [P, NT], i32)
        dst_i = sb("dst_i", [P, NT], i32)
        src_c = sb("src_c", [P, NT], f32)
        dst_c = sb("dst_c", [P, NT], f32)
        group_tab = sb("group_tab", [1, 4, NG], i32)
        block_tab = sb("block_tab", [1, 4, NB], i32)
        parts_tab = sb("parts_tab", [1, 8], i32)
        vec = sb("vec", [P, 32], f32)
        col_b = sb("col_b", [P, 4], bf16)
        col_f = sb("col_f", [P, 8], f32)
        b1_parts = sb("b1_parts", [3, P], bf16)
        row3 = sb("row3", [3, GE], bf16)
        base = at[0]

        b_rows = sb("b_rows", [P, NP], f32)
        a_rows = sb("a_rows", [P, NP], f32)
        edge_order = sb("edge_order", [WP, EP // WP], i32)
        pair_lim = sb("pair_lim", [WP, 2, NPAIR // WP], i32)
        group_lim = sb("group_lim", [WP, 2, NG // WP], i32)
        pair_bc = sb("pair_bc", [NB, 2, NPAIR], i32)
        win = sb("win", [NB, 6, NPAIR], f32)
        edge_w = sb("edge_w", [NB, 8], f32)
        rowf = sb("rowf", [1, 8, NG], f32)
        lim_i = sb("lim_i", [NB, 2], i32)
        b_parts = sb("b_parts", [P, 3, NP], bf16)
        after_b = at[0]

        at[0] = base
        one_src = sb("one_src", [P, 2, NP], bf16)
        one_dst = sb("one_dst", [P, 2, P], bf16)
        c_hi = sb("c_hi", [P, NP], bf16)
        c_lo = sb("c_lo", [P, NP], bf16)
        over = sb("over", [P, NB], f32)
        over_out = sb("over_out", [P, NP], bf16)
        over1 = sb("over1", [P, 1], f32)
        overrow = sb("overrow", [1, P], f32)
        gat = sb("gat", [P, 4, GE], f32)
        gidx = sb("gidx", [P, 4, 4], i32)
        assert at[0] <= after_b - 3 * NP * 2

        at[0] = base
        a_in = sb("a_in", [P, 2, GE], f32)
        dst_bc = sb("dst_bc", [P, 2, GE], i32)
        oht = sb("oht", [P, 2, GE], bf16)
        h1 = sb("h1", [P, 4, GE], f32)
        r1 = sb("r1", [P, 2, GE], f32)
        u = sb("u", [P, 2, GE], f32)
        ohd = sb("ohd", [P, 2, GE], f32)
        stats = sb("stats", [P, NG, 6], f32)
        w2s = sb("w2s", [P, P], f32)
        w2t = sb("w2t", [P, P], f32)
        assert at[0] <= after_b - 3 * NP * 2

        at[0] = base
        c_ring = sb("c_ring", [P, RING, NP], bf16)
        hp = sb("hp", [P, 3, NP], bf16)
        hn = sb("hn", [P, NP], f32)
        dd = sb("dd", [P, NP], f32)
        dsr = sb("dsr", [P, NP], f32)
        q2 = sb("q2", [P, NP], f32)
        hT = sb("hT", [P, NP], f32)
        nd = sb("nd", [P, 3, NB], f32)
        weff = sb("weff", [P, P], f32)
        wtmp = sb("wtmp", [P, 4, P], f32)
        gcn_end = at[0]

        at[0] = base
        selh = sb("selh", [H, P], f32)
        bv_bc = sb("bv_bc", [P, P], f32)
        qp = sb("qp", [P, HQ, NP], bf16)
        kp = sb("kp", [P, HQ, NP], bf16)
        vaug = sb("vaug", [P, NB, H, HW], f32)
        attn = at[0]
        parts3 = sb("parts3", [P, 3, NP], bf16)
        parts3k = sb("parts3k", [P, 3, NP], bf16)
        at[0] = attn
        mask = sb("mask", [P, RING, NP], bf16)
        masked = sb("masked", [P, 4 * CW], bf16)
        mx = sb("mx", [P, 2 * HQ], f32)
        mxs = sb("mxs", [P, NB, HQ], f32)
        mtmp = sb("mtmp", [P, NB, HQ], f32)
        mb = sb("mb", [P, NB, HQ], bf16)
        m_parts = sb("m_parts", [P, NB, HQ, 3], f32)
        m_rows = sb("m_rows", [HQ * 3, NP], bf16)
        at[0] = attn
        c_raw = sb("c_raw", [P, 2, 2, SC, CW], bf16)
        c_full = sb("c_full", [P, 2, SC, CW], f32)
        ex = sb("ex", [P, 3, 2 * CW], f32)
        pw = sb("pw", [P, 4, 2 * CW], f32)
        o_sb = sb("o_sb", [P, CW], f32)

        psum = ctx.enter_context(nc.psum_tensor("psum", [P, 8 * BANK], f32))

        def bank(j, n=BANK):
            return psum[:, j * BANK:j * BANK + n]

        done = {e: sem(f"{e}_stages") for e in ("sp", "pool", "act", "dve", "pe")}
        loaded = sem("loaded")
        step = {e: sem(f"{e}_steps") for e in ("act", "dve", "pe", "pool")}
        held = {e: sem(f"{e}_held") for e in ("act", "dve", "pe", "pool", "sp")}
        steps = dict.fromkeys(step, 0)
        passed = dict.fromkeys(done, 0)
        names = ("root_asked root_made ln_dve ln_sq ln_psum lims_ready lims_stored rows_back windows_ready "
                 "windows_stored windows_back ab_taken a_stored over1_ready over_stored over_back h1_psum bv_back "
                 "qk_parts_ready qk_stored mask_used m_rows_ready m_rows_stored full_ready sums_back out_sb "
                 "out_stored consts_ready row_sb vaug_ready mask_ready pw_ready ab_ready vec_psum slot_free "
                 "c_made c_stored chunk_free over_ready h1_counted h1_ready bn1_ready w2_psum bn2_ready agg_done "
                 "node_psum node_taken nd_psum nd_sb gcn_sum gcn_relu weff_sum weff_abs hT_psum hT_ready "
                 "asym_psum asym_taken delta_ready tanh_ready bq_ready qk_psum qk_scaled m_rows_psum ex_ready "
                 "sc_psum pw_free o_ready pv_taken o_stored x_ready vec_ready one_ready visit_free visit_ready "
                 "w2_ready agg_ready agg_psum agg_added deg_psum deg_taken h_parts agg_sum weff_ready hT_next "
                 "s_free s_psum m_parts_ready attn_ready attn_psum wo_psum out_psum").split()
        S = {n: sem(n) for n in names}
        gathered = [sem(f"gathered{s}") for s in range(4)]
        a_staged = [sem(f"a_staged{s}") for s in range(4)]
        gat_free = [sem(f"gat_free{s}") for s in range(4)]
        a_loaded = [sem(f"a_loaded{s}") for s in range(2)]
        dst_loaded = [sem(f"dst_loaded{s}") for s in range(2)]
        dst_used = [sem(f"dst_used{s}") for s in range(2)]
        h1_stored = [sem(f"h1_stored{s}") for s in range(2)]
        r1_made = {n: sem(f"r1_made{n}") for n in (3, 4)}
        h1_loaded = {n: [sem(f"h1_loaded{n}{s}") for s in range(2)] for n in (3, 4)}
        h2_psum = {n: sem(f"h2_psum{n}") for n in (3, 4)}
        h2_taken = {n: sem(f"h2_taken{n}") for n in (3, 4)}
        packed = sem("packed")
        mask_loaded = [sem(f"mask_loaded{r}") for r in range(RING)]
        raw_loaded = [sem(f"raw_loaded{r}") for r in range(2)]
        c_loaded = [sem(f"c_loaded{s}") for s in range(RING)]
        S["c_used"] = sem("c_used")

        def after(eng, s, n):
            if not (isinstance(n, int) and n <= 0):
                eng.wait_ge(s, n)

        def hold(name, eng, s, n):
            eng.wait_ge(s, n)
            eng.sem_inc(held[name], 1)

        def slot_again(n, slots, j, u):
            before = u - slots if u >= slots else max(w for w in range(n) if w % slots == u % slots) - n
            return j * n + (before + 1 + n)

        def stepped(name, eng, i):
            steps[name] += 1
            i.then_inc(step[name], 1)
            eng.wait_ge(step[name], steps[name])

        def stage_end(name, eng, last):
            if last is None:
                eng.sem_inc(done[name], 1)
            else:
                last.then_inc(done[name], 1)

        def stage_start(name, eng):
            passed[name] += 1
            for e in done:
                eng.wait_ge(done[e], passed[name])

        roots = dict(act=0, dve=0)

        def root_act(act, to, of, bias):
            n = roots["act"] = roots["act"] + 1
            act.wait_ge(S["root_asked"], n)
            nc.scalar.activation(to, of, ACT.Sqrt, bias=bias).then_inc(S["root_made"], 1)

        def root_dve(dve, to):
            n = roots["dve"] = roots["dve"] + 1
            dve.sem_inc(S["root_asked"], 1)
            dve.wait_ge(S["root_made"], n)
            stepped("dve", dve, nc.vector.reciprocal(to, to))

        norms = dict(pe=0, act=0, dve=0)

        def norm_pe(pe):
            n = norms["pe"] = norms["pe"] + 1
            for k, (operand, ready) in enumerate(((y, S["ln_dve"]), (z, S["ln_sq"]))):
                pe.wait_ge(ready, 2 * n - 1 if operand is y else n)
                if operand is z:
                    pe.wait_ge(S["ln_dve"], 2 * n)
                for c, w in CHUNKS:
                    last = nc.tensor.matmul(psum[:, c:c + w], meanf[:, :], operand[:, c:c + w], start=True, stop=True)
                last.then_inc(S["ln_psum"], 1)

        def norm_act(act):
            n = norms["act"] = norms["act"] + 1
            act.wait_ge(S["ln_dve"], 2 * n)
            nc.scalar.activation(z[:, :], y[:, :], ACT.Square).then_inc(S["ln_sq"], 1)
            act.wait_ge(S["ln_psum"], 2 * n)
            root_act(act, z[:, :], psum[:, 0:NP], eps1[:, 0:1])

        def norm_dve(dve):
            n = norms["dve"] = norms["dve"] + 1
            dve.sem_inc(S["ln_dve"], 1)
            dve.wait_ge(S["ln_psum"], 2 * n - 1)
            nc.vector.tensor_tensor(y[:, :], y[:, :], psum[:, 0:NP], ALU.subtract).then_inc(S["ln_dve"], 1)
            dve.wait_ge(S["ln_psum"], 2 * n)
            root_dve(dve, z[:, :])
            nc.vector.tensor_tensor(x[:, :], y[:, :], z[:, :], ALU.mult).then_inc(done["dve"], 1)

        block = ctx.enter_context(nc.Block())

        @block.sync
        def _(sp):
            n = 0
            sp.dma_start(x[:, 0:N], ins["xT"]).then_inc(loaded, 16)
            for name in list(W) + list(V):
                sp.dma_start((W if name in W else V)[name][:, :], ins[name]).then_inc(loaded, 16)
            sp.dma_start(src_i[:, :], ins["src_cols"]).then_inc(loaded, 16)
            sp.dma_start(dst_i[:, :], ins["dst_cols"]).then_inc(loaded, 16)
            sp.dma_start(edge_order[:, :], ins["dst_rows"].rearrange("a (p e) -> (a p) e", p=WP)).then_inc(loaded, 16)
            sp.wait_ge(S["lims_ready"], 1)
            for a in range(2):
                sp.dma_start(pair_rows[a], pair_lim[:, a, :]).then_inc(S["lims_stored"], 16)
                sp.dma_start(group_rows[a], group_lim[:, a, :]).then_inc(S["lims_stored"], 16)
            sp.wait_ge(S["lims_stored"], 64)
            for a in range(2):
                sp.dma_start(pair_bc[:, a, :],
                             pairs_flat[a:a + 1, :].broadcast_to([NB, NPAIR])).then_inc(S["rows_back"], 16)
                sp.dma_start(group_tab[:, a, :], groups_flat[a:a + 1, :]).then_inc(S["rows_back"], 16)
            sp.wait_ge(S["windows_ready"], 1)
            with nc.allow_non_contiguous_dma(reason="two columns of 25 numbers"):
                sp.dma_start(block_rows.rearrange("a b -> b a"), lim_i[:, :]).then_inc(S["windows_stored"], 16)
            sp.wait_ge(S["windows_stored"], 16)
            sp.dma_start(block_tab[:, 0:2, :], block_rows.rearrange("(o a) b -> o a b", o=1)).then_inc(S["windows_back"], 16)
            sp.wait_ge(S["ab_taken"], 25)
            sp.dma_start(a_table.rearrange("(b p) f -> p b f", p=P),
                         a_rows[:, :].rearrange("p (b f) -> p b f", f=P)).then_inc(S["a_stored"], 16)
            sp.wait_ge(S["a_stored"], 16)
            stage_end("sp", sp, None)
            if stages >= 1:
                stage_start("sp", sp)
                with sp.Fori(0, NG // 4) as i:
                    for s in range(4):
                        sp.wait_ge(gathered[s], 64 * i + 64)
                        sp.dma_start(a_edges[ds(4 * i + s, 1)].rearrange("o p e -> (o p) e"),
                                     gat[:, s, :]).then_inc(a_staged[s], 16)
                        if s:
                            sp.wait_ge(a_staged[s - 1], 16 * i + 16)
                            sp.sem_inc(gat_free[s - 1], 1)
                    sp.wait_ge(a_staged[3], 16 * i + 16)
                    sp.sem_inc(gat_free[3], 1)
                sp.wait_ge(S["over1_ready"], 1)
                with nc.allow_non_contiguous_dma(reason="a column of 128 numbers"):
                    sp.dma_start(flag_row, over1[:, :]).then_inc(S["over_stored"], 16)
                sp.wait_ge(S["over_stored"], 16)
                sp.dma_start(overrow[:, :], flag_row.rearrange("p o -> o p")).then_inc(S["over_back"], 16)
                stage_end("sp", sp, None)
            if stages >= 2:
                stage_start("sp", sp)

                def fetch(i):
                    for s in range(2):
                        after(sp, S["h1_psum"], 2 * i + s - 1)
                        sp.dma_start(a_in[:, s, :], a_edges[ds(2 * i + s, 1)].rearrange("o p e -> (o p) e")
                                     ).then_inc(a_loaded[s], 16)
                        after(sp, dst_used[s], i)
                        sp.dma_start(dst_bc[:, s, :], ins["dst_rows"][:, ds((2 * i + s) * GE, GE)].broadcast_to([P, GE])
                                     ).then_inc(dst_loaded[s], 16)

                fetch(0)
                with sp.Fori(1, NG // 2) as i:
                    fetch(i)
                stage_end("sp", sp, None)
            for n in (3, 4):
                if stages >= n:
                    stage_start("sp", sp)

                    def fetch_h1(i):
                        for s in range(2):
                            after(sp, r1_made[n], 2 * i + s - 1)
                            sp.dma_start(a_in[:, s, :], h1_edges[:, ds((2 * i + s) * GE, GE)]).then_inc(h1_loaded[n][s], 16)

                    fetch_h1(0)
                    with sp.Fori(1, NG // 2) as i:
                        fetch_h1(i)
                    stage_end("sp", sp, None)
            def load_counts(q, transposed):

                with sp.Fori(0, steps_sp) as i:
                    for r in range(RING):
                        hold("sp", sp, S["c_used"], steps_sp * (RING * q) + i * RING + (r + 1))
                        if transposed:
                            sp.dma_start_transpose(
                                c_ring[:, r, :],
                                c_parts[ds((i // RING) * NP, NP), ds((i % RING) * (RING * P) + r * P, P)]
                            ).then_inc(c_loaded[r], 16)
                        else:
                            sp.dma_start(c_ring[:, r, :], c_parts[ds(i * (RING * P) + r * P, P), :]
                                         ).then_inc(c_loaded[r], 16)

            if stages >= 5:
                stage_start("sp", sp)
                steps_sp = sp.value_load(parts_tab[0:1, 0:1], min_val=RING, max_val=2 * RING)
                load_counts(0, False)
                load_counts(1, True)
                load_counts(2, True)
                load_counts(3, False)
                stage_end("sp", sp, None)
            if stages >= 6:
                stage_start("sp", sp)
                for q in range(4, 4 + GNN_LAYERS):
                    load_counts(q, True)
                stage_end("sp", sp, None)
            if stages >= 7:
                stage_start("sp", sp)
                sp.dma_start(bv_bc[:, :], ins["v_bv"].rearrange("p o -> o p").broadcast_to([P, P])).then_inc(S["bv_back"], 16)
                sp.wait_ge(S["qk_parts_ready"], 1)
                for m in range(3):
                    sp.dma_start(qk_parts[m], parts3[:, m, :]).then_inc(S["qk_stored"], 16)
                    sp.dma_start(qk_parts[3 + m], parts3k[:, m, :]).then_inc(S["qk_stored"], 16)
                sp.wait_ge(S["qk_stored"], 96)
                stage_end("sp", sp, None)
                for quad in range(QUADS):
                    stage_start("sp", sp)
                    rows = slice(quad * HQ * HD, (quad + 1) * HQ * HD)
                    for n, (mq, mk) in enumerate(QK_SLOTS):
                        for pack, m in ((qp, mq), (kp, 3 + mk)):
                            sp.dma_start(pack[n * HD:(n + 1) * HD, :, :],
                                         qk_parts[m][rows, :].rearrange("(h d) n -> d h n", d=HD)).then_inc(packed, 16)
                    with sp.Fori(0, NB // RING) as i:
                        for r in range(RING):
                            hold("sp", sp, S["mask_used"], i * RING + r + 1 + quad * NB)
                            sp.dma_start_transpose(mask[:, r, :], c_parts[0:NP, ds(i * (RING * P) + r * P, P)]
                                                   ).then_inc(mask_loaded[r], 16)
                    sp.wait_ge(S["m_rows_ready"], quad + 1)
                    for hh in range(HQ):
                        sp.dma_start(kp[KQK:KQK + 3, hh, :], m_rows[3 * hh:3 * hh + 3, :]).then_inc(S["m_rows_stored"], 16)
                    sp.wait_ge(S["m_rows_stored"], 16 * HQ * (quad + 1))
                    stage_end("sp", sp, None)
                    stage_start("sp", sp)
                    with sp.Fori(0, NC) as j:
                        for w in range(NB // SC):
                            hold("sp", sp, S["full_ready"], slot_again(NB // SC, 2, j, w) + quad * NC * (NB // SC))
                            for part in range(2):
                                first = part * NP + w * SC * P
                                sp.dma_start(c_raw[:, w % 2, part, :, :],
                                             c_parts[first:first + SC * P, ds(j * CW, CW)].rearrange(
                                                 "(k p) t -> p k t", p=P)).then_inc(raw_loaded[w % 2], 16)
                    stage_end("sp", sp, None)
                stage_start("sp", sp)
                for h in range(H):
                    quad, row = h // HQ, (h % HQ) * HW
                    sp.dma_start(y[h * HD:(h + 1) * HD, :], head_sums[quad, row:row + HD, :]).then_inc(S["sums_back"], 16)
                    sp.dma_start(z[h:h + 1, :], head_sums[quad, row + HD:row + HD + 1, :]).then_inc(S["sums_back"], 16)
                stage_end("sp", sp, None)
            stage_start("sp", sp)
            for b in range(NB):
                rows = min(P, N - b * P)
                sp.wait_ge(S["out_sb"], b + 1)
                sp.dma_start(out[b * P:b * P + rows, :], y[0:rows, b * P:(b + 1) * P]).then_inc(S["out_stored"], 16)
            sp.wait_ge(S["out_stored"], 16 * NB)

        @block.gpsimd
        def _(pool):
            g = nc.gpsimd
            stepped("pool", pool, g.memset(identf[:, :], 0.0))
            stepped("pool", pool, g.memset(identb[:, :], 0.0))
            for m in (identf, identb):
                g.affine_select(out=m[:, :], in_=m[:, :], compare_op=ALU.not_equal, fill=1.0, base=0,
                                pattern=[[-1, P]], channel_multiplier=1)
            pool.wait_ge(loaded, 16 * len(ins))
            for m, sign in ((W["Wp"], 1), (W["WpT"], -1)):
                g.affine_select(out=m[:, :], in_=m[:, :], compare_op=ALU.is_ge, fill=0.0, base=-1,
                                pattern=[[sign, P]], channel_multiplier=-sign)
            g.memset(onesf[:, :], 1.0)
            g.memset(meanf[:, :], 1.0 / P)
            g.memset(onesb[:, :], 1.0)
            g.memset(zerosb[:, :], 0.0)
            g.memset(eps1[:, :], EPS)
            g.iota(nodeid[:, :], pattern=[[P, NB]], base=0, channel_multiplier=1,
                   allow_small_or_imprecise_dtypes=True)
            g.iota(win[:, 0, :], pattern=[[-1, NPAIR]], base=NPAIR, channel_multiplier=0,
                   allow_small_or_imprecise_dtypes=True)
            g.iota(win[:, 1, :], pattern=[[1, NPAIR]], base=1, channel_multiplier=0,
                   allow_small_or_imprecise_dtypes=True)
            g.iota(iota[:, :], pattern=[[1, NP]], base=-CENTER, channel_multiplier=0,
                   allow_small_or_imprecise_dtypes=True).then_inc(S["consts_ready"], 1)
            stage_end("pool", pool, None)
            if stages >= 1:
                stage_start("pool", pool)

                def gather(i):
                    for s in range(4):
                        after(pool, gat_free[s], i)
                        g.tensor_copy(gidx[:, s, :], src_i[:, ds(16 * i + 4 * s, 4)]).then_inc(S["row_sb"], 1)
                        hold("pool", pool, S["row_sb"], 4 * i + s + 1)
                        for k in range(4):
                            g.indirect_dma_start(gat[:, s, k * P:(k + 1) * P], None, a_table,
                                                 bass.IndirectOffsetOnAxis(ap=gidx[:, s, k:k + 1], axis=0)
                                                 ).then_inc(gathered[s], 16)

                gather(0)
                with pool.Fori(1, NG // 4) as i:
                    gather(i)
                stage_end("pool", pool, None)
            for n in range(2, min(stages, 6) + 1):
                stage_start("pool", pool)
                stage_end("pool", pool, None)
            if stages >= 7:
                stage_start("pool", pool)
                stepped("pool", pool, g.memset(selh[:, :], 1.0))
                stepped("pool", pool, g.affine_select(out=selh[:, :], in_=selh[:, :], compare_op=ALU.is_ge, fill=0.0,
                                                      base=0, pattern=[[1, P]], channel_multiplier=-HD))
                stepped("pool", pool, g.affine_select(out=selh[:, :], in_=selh[:, :], compare_op=ALU.is_ge, fill=0.0,
                                                      base=HD - 1, pattern=[[-1, P]], channel_multiplier=HD))
                stepped("pool", pool, g.memset(qp[KQK:P, :, :], 1.0))
                stepped("pool", pool, g.memset(vaug[:, :, :, :], 0.0))
                g.memset(vaug[:, :, :, HD:HD + 1], 1.0).then_inc(S["vaug_ready"], 1)
                stage_end("pool", pool, None)
                for quad in range(QUADS):
                    stage_start("pool", pool)
                    with pool.Fori(0, NB // RING) as i:
                        for r in range(RING):
                            hold("pool", pool, mask_loaded[r], 16 * i + 16 + quad * (16 * NB // RING))
                            g.tensor_scalar(mask[:, r, :], mask[:, r, :], 0.0, MASKED, ALU.is_equal,
                                            ALU.mult).then_inc(S["mask_ready"], 1)
                    stage_end("pool", pool, None)
                    stage_start("pool", pool)
                    if not quad:
                        pool.sem_inc(S["full_ready"], NB // SC)
                    with pool.Fori(0, NC) as j:
                        for w in range(NB // SC):
                            uses = sum(1 for k in range(NB // SC) if k % 2 == w % 2)
                            hold("pool", pool, raw_loaded[w % 2], j * (32 * uses) + 32 * (w // 2 + 1) + quad * NC * 32 * uses)
                            hold("pool", pool, S["pw_ready"],
                                 slot_again(NB // SC, 2, j, w) * (2 * SC) + quad * NC * 2 * NB)
                            g.tensor_tensor(c_full[:, w % 2, :, :], c_raw[:, w % 2, 0, :, :], c_raw[:, w % 2, 1, :, :],
                                            ALU.add).then_inc(S["full_ready"], 1)
                    stage_end("pool", pool, None)
                stage_start("pool", pool)
                stage_end("pool", pool, None)
            stage_start("pool", pool)

        @block.scalar
        def _(act):
            a = nc.scalar
            for b in range(NB):
                act.wait_ge(S["ab_ready"], b + 1)
                o = (b % 4) * BANK
                a.activation(a_rows[:, b * P:(b + 1) * P], psum[:, o:o + P], ACT.Copy)
                last = a.activation(b_rows[:, b * P:(b + 1) * P], psum[:, o + P:o + 2 * P], ACT.Copy)
                last.then_inc(S["ab_taken"], 1)
            act.wait_ge(S["vec_psum"], 1)
            a.activation(b1_parts[:, :], bank(4)[0:3, 0:P], ACT.Copy).then_inc(done["act"], 1)
            if stages >= 1:
                stage_start("act", act)
                with act.Fori(0, NB) as b:
                    before = act.value_load(block_tab[0:1, 2, ds(b, 1)], min_val=0, max_val=PAIR0 + NB * NPAIR)
                    end = act.value_load(block_tab[0:1, 1, ds(b, 1)], min_val=1, max_val=NPAIR)
                    act.wait_ge(S["slot_free"], (before + end) * 2 + 2)
                    for j in range(NC):
                        a.activation(c_hi[:, j * CW:(j + 1) * CW], bank(j, CW), ACT.Copy).then_inc(S["c_made"], 1)
                    act.wait_ge(S["c_made"], 8 * b + 8)
                    act.dma_start(c_parts[ds(b * P, P), :], c_hi[:, :]).then_inc(S["c_stored"], 16)
                    act.wait_ge(S["chunk_free"], 8 * b + 8)
                    act.dma_start(c_parts[ds(b * P + NP, P), :], c_lo[:, :]).then_inc(S["c_stored"], 16)
                    a.activation(over_out[:, :], c_lo[:, :], ACT.Square, accum_out=over[:, ds(b, 1)]
                                 ).then_inc(S["over_ready"], 1)
                    act.wait_ge(S["over_ready"], b + 1)
                    act.wait_ge(S["c_stored"], 32 * b + 32)
                stage_end("act", act, None)
            if stages >= 2:
                stage_start("act", act)

                def keep_h1(i):
                    for s in range(2):
                        after(act, h1_stored[s], 16 * i)
                        after(act, S["h1_counted"], 2 * i + s - 1)
                        act.wait_ge(S["h1_psum"], 2 * i + s + 1)
                        a.activation(h1[:, s, :], bank(s), ACT.Copy).then_inc(S["h1_ready"], 1)
                        act.wait_ge(S["h1_ready"], 2 * i + s + 1)
                        act.dma_start(h1_edges[:, ds((2 * i + s) * GE, GE)], h1[:, s, :]).then_inc(h1_stored[s], 16)

                keep_h1(0)
                with act.Fori(1, NG // 2) as i:
                    keep_h1(i)
                for s in range(2):
                    act.wait_ge(h1_stored[s], 16 * (NG // 2))
                stage_end("act", act, None)
            if stages >= 3:
                stage_start("act", act)
                root_act(act, vec[:, 3:4], vec[:, 3:4], eps1[:, 0:1])
                act.wait_ge(S["bn1_ready"], 1)

                def relu1(n, i, s):
                    after(act, h2_psum[n], 2 * i + s - 1)
                    act.wait_ge(h1_loaded[n][s], 16 * i + 16)
                    return a.activation(r1[:, s, :], a_in[:, s, :], ACT.Relu, scale=vec[:, 4:5],
                                        bias=vec[:, 5:6]).then_inc(r1_made[n], 1)

                relu1(3, 0, 0)
                relu1(3, 0, 1)
                with act.Fori(1, NG // 2) as i:
                    relu1(3, i, 0)
                    relu1(3, i, 1)
                stage_end("act", act, None)
            if stages >= 4:
                stage_start("act", act)
                root_act(act, vec[:, 3:4], vec[:, 3:4], eps1[:, 0:1])
                act.wait_ge(S["w2_psum"], 1)
                a.activation(w2s[:, :], bank(6, P), ACT.Copy)
                for k in range(GE // P):
                    last = a.activation(row3[:, k * P:(k + 1) * P], bank(7)[0:3, 0:P], ACT.Copy)
                last.then_inc(S["bn2_ready"], 1)

                def relu2(i, s):
                    after(act, S["agg_done"], 2 * i + s - 1)
                    act.wait_ge(h2_psum[4], 2 * i + s + 1)
                    a.activation(u[:, s, :], bank(s), ACT.Relu).then_inc(h2_taken[4], 1)

                relu1(4, 0, 0)
                relu1(4, 0, 1)
                relu2(0, 0)
                with act.Fori(1, NG // 2) as i:
                    relu1(4, i, 0)
                    relu2(i + -1, 1)
                    relu1(4, i, 1)
                    relu2(i, 0)
                relu2(NG // 2 - 1, 1)
                norm_act(act)
                stage_end("act", act, None)

            def messages(q, width, scales):
                for b in range(NB):
                    act.wait_ge(S["node_psum"], q * NB + b + 1)
                    for m, (to, factor) in enumerate(scales):
                        o = (b % 4) * BANK + m * P
                        last = a.activation(to[:, b * P:(b + 1) * P], psum[:, o:o + P], ACT.Copy,
                                            scale=nd[:, factor, b:b + 1])
                    last.then_inc(S["node_taken"], 1)

            if stages >= 5:
                stage_start("act", act)
                root_act(act, dsr[:, :], dsr[:, :], 0.0)
                root_act(act, dd[:, :], dd[:, :], 0.0)
                root_act(act, q2[:, :], q2[:, :], 0.0)
                act.wait_ge(S["nd_psum"], 1)
                a.activation(nd[:, :, :].rearrange("p j b -> p (j b)"), bank(7, 3 * NB), ACT.Copy
                             ).then_inc(S["nd_sb"], 1)
                act.wait_ge(S["nd_sb"], 1)
                messages(0, 2 * P, ((hn, 0), (hT, 1)))
                act.wait_ge(S["gcn_sum"], 1)
                a.activation(y[:, :], y[:, :], ACT.Relu, bias=vec[:, 8:9]).then_inc(S["gcn_relu"], 1)
                norm_act(act)
                stage_end("act", act, None)
            if stages >= 6:
                stage_start("act", act)
                act.wait_ge(S["weff_sum"], 1)
                a.activation(wtmp[:, 0, :], weff[:, :], ACT.Abs, accum_out=vec[:, 9:10]).then_inc(S["weff_abs"], 1)
                act.wait_ge(S["hT_psum"], 1)
                a.activation(hT[:, :], psum[:, 0:NP], ACT.Relu, bias=V["v_bi"][:, 0:1]).then_inc(S["hT_ready"], 1)
                for k in range(GNN_LAYERS):
                    act.wait_ge(S["asym_psum"], k + 1)
                    a.activation(y[:, :], psum[:, 0:NP], ACT.Relu).then_inc(S["asym_taken"], 1)
                    messages(1 + k, P, ((hn, 2),))
                    act.wait_ge(S["delta_ready"], k + 1)
                    a.activation(z[:, :], z[:, :], ACT.Tanh).then_inc(S["tanh_ready"], 1)
                norm_act(act)
                stage_end("act", act, None)

            if stages >= 7:
                stage_start("act", act)
                act.wait_ge(S["bq_ready"], 1)
                act.wait_ge(S["qk_psum"], 1)
                a.activation(y[:, :], psum[:, 0:NP], ACT.Identity, scale=HD ** -0.5, bias=vec[:, 10:11]
                             ).then_inc(S["qk_scaled"], 1)
                act.wait_ge(S["qk_psum"], 2)
                a.activation(z[:, :], psum[:, 0:NP], ACT.Identity, bias=V["v_bk"][:, 0:1]).then_inc(S["qk_scaled"], 1)
                stage_end("act", act, None)
                for quad in range(QUADS):
                    stage_start("act", act)
                    act.wait_ge(S["m_rows_psum"], quad + 1)
                    a.activation(m_rows[:, :], psum[0:HQ * 3, 0:NP], ACT.Copy).then_inc(S["m_rows_ready"], 1)
                    stage_end("act", act, None)
                    stage_start("act", act)
                    pairs = 2 * NB
                    if not quad:
                        act.sem_inc(S["ex_ready"], pairs)
                    with act.Fori(0, NC) as j:
                        for n in range(pairs):
                            act.wait_ge(S["sc_psum"], j * pairs + n + 1 + quad * NC * pairs)
                            act.wait_ge(S["pw_ready"], slot_again(pairs, 3, j, n) + quad * NC * pairs)
                            o = 2 * (n % 3) * BANK
                            a.activation(ex[:, n % 3, :].rearrange("p (h t) -> p h t", h=2),
                                         psum[:, o:o + 2 * BANK].rearrange("p (h t) -> p h t", h=2)[:, :, 0:CW],
                                         ACT.Exp).then_inc(S["ex_ready"], 1)
                        act.wait_ge(S["pw_free"], j * pairs + (2 + quad * NC) * pairs)
                        a.activation(o_sb[:, :], bank(6, CW), ACT.Copy).then_inc(S["o_ready"], 1)
                        hold("act", act, S["o_ready"], j + 1 + quad * NC)
                        act.sem_inc(S["pv_taken"], 1)
                        act.dma_start(head_sums[quad, :, ds(j * CW, CW)], o_sb[:, :]).then_inc(S["o_stored"], 16)
                        hold("act", act, S["o_stored"], 16 * j + 16 + 16 * quad * NC)
                    stage_end("act", act, None)
                stage_start("act", act)
                norm_act(act)
                stage_end("act", act, None)

        @block.vector
        def _(dve):
            v = nc.vector

            def do(i):
                stepped("dve", dve, i)

            def split_col(col):
                do(v.tensor_copy(col_b[:, 0:1], col))
                do(v.tensor_tensor(col_f[:, 4:5], col, col_b[:, 0:1], ALU.subtract))
                do(v.tensor_copy(col_b[:, 1:2], col_f[:, 4:5]))
                do(v.tensor_tensor(col_f[:, 5:6], col_f[:, 4:5], col_b[:, 1:2], ALU.subtract))
                do(v.tensor_copy(col_b[:, 2:3], col_f[:, 5:6]))
                do(v.tensor_copy(col_f[:, 0:3], col_b[:, 0:3]))

            def split(parts, whole):
                do(v.tensor_copy(parts[:, 0, :], whole))
                do(v.tensor_tensor(whole, whole, parts[:, 0, :], ALU.subtract))
                do(v.tensor_copy(parts[:, 1, :], whole))
                do(v.tensor_tensor(whole, whole, parts[:, 1, :], ALU.subtract))
                do(v.tensor_copy(parts[:, 2, :], whole))

            dve.wait_ge(loaded, 16 * len(ins))
            do(v.memset(x[:, N:NP], 0.0))
            dve.sem_inc(S["x_ready"], 1)
            v.tensor_scalar(src_c[:, :], src_i[:, :], float(-CENTER), None, ALU.add)
            v.tensor_scalar(dst_c[:, :], dst_i[:, :], float(-CENTER), None, ALU.add)
            for k, op in enumerate((ALU.min, ALU.max)):
                do(v.tensor_reduce(out=pair_lim[:, k, :], in_=edge_order[:, :].rearrange("p (g e) -> p g e", e=PE_EDGES),
                                   op=op, axis=AX.X))
                do(v.tensor_single_scalar(pair_lim[:, k, :], pair_lim[:, k, :], 7, op=ALU.arith_shift_right))
                do(v.tensor_reduce(out=group_lim[:, k, :], in_=pair_lim[:, k, :].rearrange("p (g e) -> p g e", e=2),
                                   op=op, axis=AX.X))
            dve.sem_inc(S["lims_ready"], 1)
            dve.wait_ge(S["rows_back"], 64)
            dve.wait_ge(S["consts_ready"], 1)
            do(v.tensor_scalar(win[:, 2, :], pair_bc[:, 0, :], nodeid[0:NB, 0:1], None, ALU.is_le))
            do(v.tensor_scalar(win[:, 3, :], pair_bc[:, 1, :], nodeid[0:NB, 0:1], None, ALU.is_ge))
            do(v.tensor_tensor(win[:, 2, :], win[:, 2, :], win[:, 3, :], ALU.mult))
            do(v.tensor_tensor(win[:, 4, :], win[:, 2, :], win[:, 0, :], ALU.mult))
            do(v.tensor_tensor(win[:, 5, :], win[:, 2, :], win[:, 1, :], ALU.mult))
            do(v.tensor_reduce(out=edge_w[:, 0:2], in_=win[:, 4:6, :], op=ALU.max, axis=AX.X))
            do(v.tensor_scalar(edge_w[:, 2:3], edge_w[:, 0:1], -1.0, float(NPAIR), ALU.mult, ALU.add))
            do(v.tensor_scalar(edge_w[:, 2:3], edge_w[:, 2:3], float(NPAIR - 2), None, ALU.min))
            do(v.tensor_scalar(edge_w[:, 4:5], edge_w[:, 2:3], 2.0, None, ALU.add))
            do(v.tensor_tensor(edge_w[:, 3:4], edge_w[:, 1:2], edge_w[:, 4:5], ALU.max))
            do(v.tensor_copy(lim_i[:, :], edge_w[:, 2:4]))
            dve.sem_inc(S["windows_ready"], 1)

            def visits(tab, n, start):
                do(v.memset(rowf[:, 0, 0:n], 1.0))
                do(v.tensor_tensor(rowf[:, 1, 0:n], tab[:, 1, :], tab[:, 0, :], ALU.subtract))
                do(v.tensor_tensor_scan(rowf[:, 2, 0:n], rowf[:, 0, 0:n], rowf[:, 1, 0:n], 0.0, ALU.mult, ALU.add))
                do(v.tensor_tensor(rowf[:, 3, 0:n], rowf[:, 2, 0:n], tab[:, 1, :], ALU.subtract))
                do(v.tensor_scalar(tab[:, 2, :], rowf[:, 3, 0:n], float(start), None, ALU.add))

            do(v.tensor_scalar(group_tab[:, 1, :], group_tab[:, 1, :], 1.0, None, ALU.add))
            visits(group_tab, NG, VISIT0)
            dve.wait_ge(S["windows_back"], 16)
            visits(block_tab, NB, PAIR0)
            split_col(V["v_b1"][:, 0:1])
            dve.sem_inc(S["vec_ready"], 1)
            dve.wait_ge(S["ab_taken"], NB)
            split(b_parts, b_rows[:, :])
            stage_end("dve", dve, None)

            if stages >= 1:
                stage_start("dve", dve)
                dve.sem_inc(S["one_ready"], 2 * PAIR0)

                def one_hots(b, p, before):
                    for t in range(2):
                        dve.wait_ge(S["slot_free"], (before + p) * 2 + t + 1)
                        v.tensor_scalar(one_src[:, t, :], iota[:, :], src_c[:, ds(p * 2 + t, 1)], None, ALU.is_equal)
                        v.tensor_scalar(one_dst[:, t, :], iota[:, ds(b * P, P)], dst_c[:, ds(p * 2 + t, 1)], None,
                                        ALU.is_equal).then_inc(S["one_ready"], 1)

                def window(eng, b):
                    first = eng.value_load(block_tab[0:1, 0, ds(b, 1)], min_val=0, max_val=NPAIR - 2)
                    end = eng.value_load(block_tab[0:1, 1, ds(b, 1)], min_val=2, max_val=NPAIR)
                    before = eng.value_load(block_tab[0:1, 2, ds(b, 1)], min_val=0, max_val=PAIR0 + NB * NPAIR)
                    return first, end, before

                def rest_of_counts(b):
                    for j in range(NC):
                        dve.wait_ge(S["c_made"], 8 * b + j + 1)
                        v.tensor_tensor(c_lo[:, j * CW:(j + 1) * CW], bank(j, CW), c_hi[:, j * CW:(j + 1) * CW],
                                        ALU.subtract).then_inc(S["chunk_free"], 1)

                def count_block(b):
                    first, end, before = window(dve, b)
                    one_hots(b, first, before)
                    if not isinstance(b, int):
                        rest_of_counts(b + -1)
                    with dve.Fori(first + 1, end) as p:
                        one_hots(b, p, before)

                count_block(0)
                with dve.Fori(1, NB) as b:
                    count_block(b)
                rest_of_counts(NB - 1)
                dve.wait_ge(S["over_ready"], NB)
                do(v.tensor_reduce(out=over1[:, :], in_=over[:, :], op=ALU.max, axis=AX.X))
                dve.sem_inc(S["over1_ready"], 1)
                dve.wait_ge(S["over_back"], 16)
                do(v.tensor_reduce(out=overrow[:, 0:1], in_=overrow[:, :], op=ALU.max, axis=AX.X))
                do(v.tensor_scalar(overrow[:, 0:1], overrow[:, 0:1], 0.0, 5.0, ALU.is_gt, ALU.mult))
                v.tensor_scalar(parts_tab[:, 0:1], overrow[:, 0:1], 5.0, None, ALU.add).then_inc(done["dve"], 1)
            def group(eng, g):
                first = eng.value_load(group_tab[0:1, 0, ds(g, 1)], min_val=0, max_val=NB - 1)
                end = eng.value_load(group_tab[0:1, 1, ds(g, 1)], min_val=1, max_val=NB)
                before = eng.value_load(group_tab[0:1, 2, ds(g, 1)], min_val=0, max_val=VISIT0 + NB * NG)
                return first, end, before

            def count1(g, n=GE, i=None):
                v.bn_stats(stats[:, ds(g, 1), :].rearrange("p o s -> p (o s)"), h1[:, i, 0:n]
                           ).then_inc(S["h1_counted"], 1)

            if stages >= 2:
                stage_start("dve", dve)

                def pass1(i):
                    for s in range(2):
                        g = 2 * i + s
                        first, end, before = group(dve, g)
                        hold("dve", dve, dst_loaded[s], 16 * i + 16)
                        with dve.Fori(first, end) as b:
                            dve.wait_ge(S["visit_free"], before + b + 1)
                            v.tensor_scalar(oht[:, ds((before + b) & 1, 1), :].rearrange("p o e -> p (o e)"),
                                            dst_bc[:, s, :], nodeid[:, ds(b, 1)], None,
                                            ALU.is_equal).then_inc(S["visit_ready"], 1)
                        after(dve, dst_used[s], i)
                        v.memset(vec[:, 30 + s:31 + s], 0.0).then_inc(dst_used[s], 1)
                        if not (isinstance(i, int) and i == 0 and s == 0):
                            dve.wait_ge(S["h1_ready"], 2 * i + s)
                            count1(2 * i + (s - 1), GE, (s + 1) % 2)

                dve.sem_inc(S["visit_ready"], VISIT0)
                pass1(0)
                with dve.Fori(1, NG // 2) as i:
                    pass1(i)
                dve.wait_ge(S["h1_ready"], NG)
                count1(NG - 1, LAST, 1)
                stage_end("dve", dve, None)

            def batch_norm(gain, shift, bias, to):
                do(v.bn_aggr(vec[:, 2:4], stats[:, :, :].rearrange("p g s -> p (g s)")))
                root_dve(dve, vec[:, 3:4])
                do(v.tensor_copy(vec[:, to:to + 1], vec[:, 3:4]))
                do(v.tensor_tensor(vec[:, to:to + 1], vec[:, to:to + 1], gain, ALU.mult))
                if bias is not None:
                    do(v.tensor_tensor(vec[:, 2:3], vec[:, 2:3], bias, ALU.add))
                    do(v.tensor_tensor(vec[:, 2:3], bias, vec[:, 2:3], ALU.subtract))
                    do(v.tensor_tensor(vec[:, 2:3], vec[:, 2:3], vec[:, to:to + 1], ALU.mult))
                    do(v.tensor_tensor(vec[:, to + 1:to + 2], shift, vec[:, 2:3], ALU.add))
                else:
                    do(v.tensor_tensor(vec[:, 2:3], vec[:, 2:3], vec[:, to:to + 1], ALU.mult))
                    do(v.tensor_tensor(vec[:, to + 1:to + 2], shift, vec[:, 2:3], ALU.subtract))

            if stages >= 3:
                stage_start("dve", dve)
                dve.wait_ge(S["h1_counted"], NG)
                batch_norm(V["v_g1"][:, 0:1], V["v_be1"][:, 0:1], None, 4)
                dve.sem_inc(S["bn1_ready"], 1)

                def count2(g, k, s, n=GE):
                    dve.wait_ge(h2_psum[3], k + 1)
                    v.bn_stats(stats[:, ds(g, 1), :].rearrange("p o s -> p (o s)"), bank(s, n)
                               ).then_inc(h2_taken[3], 1)

                with dve.Fori(0, NG // 2 - 1) as i:
                    count2(2 * i, 2 * i, 0)
                    count2(2 * i + 1, 2 * i + 1, 1)
                count2(NG - 2, NG - 2, 0)
                count2(NG - 1, NG - 1, 1, LAST)
                stage_end("dve", dve, None)
            if stages >= 4:
                stage_start("dve", dve)
                dve.wait_ge(h2_taken[3], NG)
                batch_norm(V["v_g2"][:, 0:1], V["v_be2"][:, 0:1], V["v_b2"][:, 0:1], 6)
                do(v.tensor_scalar(w2t[:, :], W["W2"][:, :], vec[:, 6:7], None, ALU.mult))
                split_col(vec[:, 7:8])
                do(v.memset(y[:, :], 0.0))
                dve.sem_inc(S["w2_ready"], 1)
                dve.sem_inc(S["agg_ready"], VISIT0)

                def pass3(i):
                    for s in range(2):
                        g = 2 * i + s
                        first, end, before = group(dve, g)
                        with dve.Fori(first, end) as b:
                            for k in range(GE // P):
                                last = v.tensor_scalar(ohd[:, s, k * P:(k + 1) * P], iota[:, ds(b * P, P)],
                                                       dst_c[:, ds(g * 4 + k, 1)], None, ALU.is_equal)
                            last.then_inc(S["agg_ready"], 1)
                            dve.wait_ge(S["agg_psum"], before + b + 1)
                            v.tensor_tensor(y[:, ds(b * P, P)], y[:, ds(b * P, P)], bank(2 + s, P),
                                            ALU.add).then_inc(S["agg_added"], 1)
                            dve.wait_ge(S["agg_added"], before + b + 1)

                dve.sem_inc(S["agg_added"], VISIT0)
                pass3(0)
                with dve.Fori(1, NG // 2) as i:
                    pass3(i)
                do(v.tensor_tensor(y[:, :], y[:, :], x[:, :], ALU.add))
                norm_dve(dve)
            if stages >= 5:
                stage_start("dve", dve)
                dve.wait_ge(S["deg_psum"], 1)
                do(v.tensor_scalar(dsr[:, :], psum[:, 0:NP], 1.0, None, ALU.add))
                dve.sem_inc(S["deg_taken"], 1)
                root_dve(dve, dsr[:, :])
                dve.wait_ge(S["deg_psum"], 2)
                do(v.tensor_scalar(dd[:, :], psum[:, 0:NP], 1.0, None, ALU.add))
                root_dve(dve, dd[:, :])
                do(v.tensor_scalar(q2[:, :], psum[:, 0:NP], 1.0, None, ALU.max))
                root_dve(dve, q2[:, :])
                do(v.tensor_scalar(z[:, :], psum[:, 0:NP], 0.0, None, ALU.is_gt))
                do(v.tensor_tensor(q2[:, :], q2[:, :], z[:, :], ALU.mult))
                do(v.tensor_tensor(vec[:, 8:9], V["v_bf"][:, 0:1], V["v_bb"][:, 0:1], ALU.add))
                dve.sem_inc(S["deg_taken"], 1)
                dve.wait_ge(S["node_taken"], NB)
                split(hp, hn[:, :])
                dve.sem_inc(S["h_parts"], 1)
                dve.wait_ge(S["agg_sum"], 1)
                do(v.tensor_tensor(y[:, :], psum[:, 0:NP], dd[:, :], ALU.mult))
                split(hp, hT[:, :])
                dve.sem_inc(S["h_parts"], 1)
                dve.wait_ge(S["agg_sum"], 2)
                do(v.tensor_tensor(z[:, :], psum[:, 0:NP], dsr[:, :], ALU.mult))
                do(v.tensor_tensor(y[:, :], y[:, :], z[:, :], ALU.add))
                dve.sem_inc(S["gcn_sum"], 1)
                dve.wait_ge(S["gcn_relu"], 1)
                do(v.tensor_tensor(y[:, :], y[:, :], x[:, :], ALU.add))
                norm_dve(dve)
            if stages >= 6:
                stage_start("dve", dve)
                do(v.tensor_tensor(weff[:, :], W["Wp"][:, :], W["WpT"][:, :], ALU.add))
                dve.sem_inc(S["weff_sum"], 1)
                do(v.tensor_tensor(W["WAT"][:, :], W["WAT"][:, :], W["WA"][:, :], ALU.subtract))
                dve.wait_ge(S["weff_abs"], 1)
                do(v.tensor_tensor(vec[:, 9:10], vec[:, 9:10], V["v_q"][:, 0:1], ALU.mult))
                do(v.tensor_tensor(vec[:, 9:10], vec[:, 9:10], V["v_r"][:, 0:1], ALU.add))
                do(v.tensor_scalar(wtmp[:, 1, :], identf[:, :], vec[:, 9:10], None, ALU.mult))
                do(v.tensor_tensor(weff[:, :], weff[:, :], wtmp[:, 1, :], ALU.add))
                dve.sem_inc(S["weff_ready"], 1)
                for k in range(GNN_LAYERS):
                    dve.wait_ge(S["node_taken"], (2 + k) * NB)
                    split(hp, hn[:, :])
                    dve.sem_inc(S["h_parts"], 1)
                    dve.wait_ge(S["agg_sum"], 3 + k)
                    do(v.tensor_tensor(z[:, :], psum[:, 0:NP], q2[:, :], ALU.mult))
                    do(v.tensor_tensor(z[:, :], z[:, :], y[:, :], ALU.subtract))
                    dve.sem_inc(S["delta_ready"], 1)
                    dve.wait_ge(S["tanh_ready"], k + 1)
                    do(v.scalar_tensor_tensor(hT[:, :], z[:, :], 0.0, hT[:, :], ALU.max, ALU.add))
                    dve.sem_inc(S["hT_next"], 1)
                do(v.tensor_tensor(y[:, :], hT[:, :], x[:, :], ALU.add))
                norm_dve(dve)
            if stages >= 7:
                stage_start("dve", dve)
                do(v.tensor_scalar(vec[:, 10:11], V["v_bq"][:, 0:1], HD ** -0.5, None, ALU.mult))
                dve.sem_inc(S["bq_ready"], 1)
                dve.wait_ge(S["qk_scaled"], 2)
                split(parts3, y[:, :])
                split(parts3k, z[:, :])
                dve.sem_inc(S["qk_parts_ready"], 1)
                dve.wait_ge(S["bv_back"], 16)
                dve.wait_ge(S["vaug_ready"], 1)
                for b in range(NB):
                    dve.wait_ge(S["node_psum"], (1 + GNN_LAYERS) * NB + b + 1)
                    last = v.tensor_tensor(vaug[:, b, :, 0:HD], bank(b % 4, P).rearrange("p (h d) -> p h d", h=H),
                                           bv_bc[:, :].rearrange("p (h d) -> p h d", h=H), ALU.add)
                    last.then_inc(S["node_taken"], 1)
                dve.wait_ge(S["node_taken"], (2 + GNN_LAYERS) * NB)
                stage_end("dve", dve, None)
                for quad in range(QUADS):
                    stage_start("dve", dve)
                    if not quad:
                        dve.sem_inc(S["mask_used"], RING)
                        dve.sem_inc(S["s_free"], 2)
                    halves = 2 * HQ
                    with dve.Fori(0, NB // RING) as i:
                        for r in range(RING):
                            hold("dve", dve, S["mask_ready"], i * RING + r + 1 + quad * NB)
                            for n in range(halves):
                                o = (n % 2) * 4 * BANK
                                hold("dve", dve, S["s_psum"], i * (RING * halves) + r * halves + n + 1 + quad * NB * halves)
                                v.tensor_tensor_reduce(
                                    out=masked[:, :].rearrange("p (c t) -> p c t", c=4),
                                    in0=psum[:, o:o + 4 * BANK].rearrange("p (c t) -> p c t", c=4)[:, :, 0:CW],
                                    in1=mask[:, r, (n % 2) * 4 * CW:(n % 2 + 1) * 4 * CW].rearrange("p (c t) -> p c t", c=4),
                                    scale=1.0, scalar=-3e38, op0=ALU.add, op1=ALU.max,
                                    accum_out=mx[:, n:n + 1]).then_inc(S["s_free"], 1)
                                hold("dve", dve, S["s_free"], i * (RING * halves) + r * halves + n + 3 + quad * NB * halves)
                            v.tensor_reduce(out=mxs[:, ds(i * RING + r, 1), :].rearrange("p o h -> p (o h)"),
                                            in_=mx[:, :].rearrange("p (h c) -> p h c", c=2), op=ALU.max,
                                            axis=AX.X).then_inc(S["mask_used"], 1)
                            hold("dve", dve, S["mask_used"], i * RING + r + 1 + RING + quad * NB)
                    do(v.tensor_scalar(mtmp[:, :, :], mxs[:, :, :], MASKED / 2, -1.0, ALU.is_gt, ALU.mult))
                    do(v.tensor_tensor(mxs[:, :, :], mxs[:, :, :], mtmp[:, :, :], ALU.mult))
                    for m in range(3):
                        do(v.tensor_copy(mb[:, :, :], mxs[:, :, :]))
                        do(v.tensor_copy(m_parts[:, :, :, m:m + 1].rearrange("p b h o -> p b (h o)"), mb[:, :, :]))
                        if m < 2:
                            do(v.tensor_tensor(mxs[:, :, :], mxs[:, :, :], mb[:, :, :], ALU.subtract))
                    dve.sem_inc(S["m_parts_ready"], 1)
                    stage_end("dve", dve, None)
                    stage_start("dve", dve)
                    pairs = 2 * NB
                    if not quad:
                        dve.sem_inc(S["pw_ready"], pairs)
                    with dve.Fori(0, NC) as j:
                        for n in range(pairs):
                            w = (n // 2) // SC
                            if n % (2 * SC) == 0:
                                dve.wait_ge(S["full_ready"], j * (NB // SC) + w + 1 + (quad * NC + 1) * (NB // SC))
                            dve.wait_ge(S["ex_ready"], j * pairs + n + 1 + (quad * NC + 1) * pairs)
                            dve.wait_ge(S["pw_free"], slot_again(pairs, 4, j, n) + quad * NC * pairs)
                            last = v.scalar_tensor_tensor(
                                pw[:, n % 4, :].rearrange("p (h t) -> p h t", h=2),
                                ex[:, n % 3, :].rearrange("p (h t) -> p h t", h=2), -MASKED,
                                c_full[:, w % 2, (n // 2) % SC:(n // 2) % SC + 1, :].broadcast_to([P, 2, CW]),
                                ALU.min, ALU.mult)
                            last.then_inc(S["pw_ready"], 1)
                    stage_end("dve", dve, None)
                stage_start("dve", dve)
                dve.wait_ge(S["sums_back"], 16 * 2 * H)
                do(v.tensor_scalar(z[0:H, :], z[0:H, :], 0.5, None, ALU.max))
                do(v.reciprocal(z[0:H, :], z[0:H, :]))
                dve.sem_inc(S["attn_ready"], 1)
                dve.wait_ge(S["attn_psum"], 1)
                do(v.tensor_tensor(y[:, :], y[:, :], psum[:, 0:NP], ALU.mult))
                dve.sem_inc(S["attn_ready"], 1)
                dve.wait_ge(S["wo_psum"], 1)
                do(v.scalar_tensor_tensor(y[:, :], psum[:, 0:NP], V["v_bo"][:, 0:1], x[:, :], ALU.add, ALU.add))
                norm_dve(dve)
            stage_start("dve", dve)
            for b in range(NB):
                dve.wait_ge(S["out_psum"], b + 1)
                v.tensor_copy(y[:, b * P:(b + 1) * P], bank(b % 4, P)).then_inc(S["out_sb"], 1)

        @block.tensor
        def _(pe):
            t = nc.tensor
            pe.wait_ge(loaded, 16 * len(ins))
            pe.wait_ge(S["x_ready"], 1)
            for b in range(NB):
                after(pe, S["ab_taken"], b - 3)
                o = (b % 4) * BANK
                t.matmul(psum[:, o:o + 2 * P], x[:, b * P:(b + 1) * P], W["W1"][:, :],
                         start=True, stop=True).then_inc(S["ab_ready"], 1)
            pe.wait_ge(S["vec_ready"], 1)
            pe.wait_ge(S["consts_ready"], 1)
            t.transpose(bank(4)[0:3, 0:P], col_f[:, 0:3], identf[:, :]).then_inc(S["vec_psum"], 1)
            stage_end("pe", pe, None)
            if stages >= 1:
                stage_start("pe", pe)
                pe.sem_inc(S["slot_free"], 2 * PAIR0 + 2)

                def window_pe(b):
                    first = pe.value_load(block_tab[0:1, 0, ds(b, 1)], min_val=0, max_val=NPAIR - 2)
                    end = pe.value_load(block_tab[0:1, 1, ds(b, 1)], min_val=2, max_val=NPAIR)
                    before = pe.value_load(block_tab[0:1, 2, ds(b, 1)], min_val=0, max_val=PAIR0 + NB * NPAIR)
                    return first, end, before

                def count_pe(b):
                    first, end, before = window_pe(b)
                    for j in range(NC):
                        if not isinstance(b, int):
                            pe.wait_ge(S["chunk_free"], 8 * (b + -1) + j + 1)
                        t.matmul(bank(j, CW), zerosb[:, 0:P], zerosb[:, 0:CW], start=True, stop=True)
                    with pe.Fori(first, end) as p:
                        for s in range(2):
                            pe.wait_ge(S["one_ready"], (before + p) * 2 + s + 1)
                            for j in range(NC):
                                last = t.matmul(bank(j, CW), one_dst[:, s, :], one_src[:, s, j * CW:(j + 1) * CW],
                                                start=False, stop=True, skip_group_check=True)
                            last.then_inc(S["slot_free"], 1)

                count_pe(0)
                with pe.Fori(1, NB) as b:
                    count_pe(b)
                stage_end("pe", pe, None)

            def group_pe(g):
                first = pe.value_load(group_tab[0:1, 0, ds(g, 1)], min_val=0, max_val=NB - 1)
                end = pe.value_load(group_tab[0:1, 1, ds(g, 1)], min_val=1, max_val=NB)
                before = pe.value_load(group_tab[0:1, 2, ds(g, 1)], min_val=0, max_val=VISIT0 + NB * NG)
                return first, end, before

            if stages >= 2:
                stage_start("pe", pe)
                pe.sem_inc(S["visit_free"], VISIT0 + 2)

                def pass1_pe(i):
                    for s in range(2):
                        first, end, before = group_pe(2 * i + s)
                        after(pe, S["h1_ready"], 2 * i + s - 1)
                        t.matmul(bank(s), b1_parts[:, :], onesb[0:3, :], start=True, stop=True)
                        with pe.Fori(first, end) as b:
                            pe.wait_ge(S["visit_ready"], before + b + 1)
                            for m in range(3):
                                last = t.matmul(bank(s), b_parts[:, m, ds(b * P, P)],
                                                oht[:, ds((before + b) & 1, 1), :].rearrange("p o e -> p (o e)"),
                                                start=False, stop=True, skip_group_check=True)
                            last.then_inc(S["visit_free"], 1)
                        pe.wait_ge(a_loaded[s], 16 * i + 16)
                        for k in range(GE // P):
                            last = t.matmul(bank(s)[:, k * P:(k + 1) * P], a_in[:, s, k * P:(k + 1) * P],
                                            identf[:, :], start=False, stop=True, skip_group_check=True)
                        last.then_inc(S["h1_psum"], 1)

                pass1_pe(0)
                with pe.Fori(1, NG // 2) as i:
                    pass1_pe(i)
                stage_end("pe", pe, None)
            if stages >= 3:
                stage_start("pe", pe)

                def layer2(i):
                    for s in range(2):
                        pe.wait_ge(r1_made[3], 2 * i + s + 1)
                        after(pe, h2_taken[3], 2 * i + s - 1)
                        t.matmul(bank(s), W["W2T"][:, :], r1[:, s, :], start=True, stop=True).then_inc(h2_psum[3], 1)

                layer2(0)
                with pe.Fori(1, NG // 2) as i:
                    layer2(i)
                stage_end("pe", pe, None)
            if stages >= 4:
                stage_start("pe", pe)
                pe.wait_ge(S["w2_ready"], 1)
                t.transpose(bank(6, P), w2t[:, :], identf[:, :])
                t.transpose(bank(7)[0:3, 0:P], col_f[:, 0:3], identf[:, :]).then_inc(S["w2_psum"], 1)
                pe.wait_ge(S["bn2_ready"], 1)
                pe.sem_inc(S["agg_psum"], VISIT0)

                def layer2_rows(i, s):
                    pe.wait_ge(r1_made[4], 2 * i + s + 1)
                    after(pe, h2_taken[4], 2 * i + s - 1)
                    t.matmul(bank(s), onesb[0:3, 0:P], row3[:, :], start=True, stop=True)
                    for k in range(GE // P):
                        last = t.matmul(bank(s)[:, k * P:(k + 1) * P], r1[:, s, k * P:(k + 1) * P], w2s[:, :],
                                        start=False, stop=True, skip_group_check=True)
                    last.then_inc(h2_psum[4], 1)

                def sum_edges(i, s):
                    first, end, before = group_pe(2 * i + s)
                    hold("pe", pe, h2_taken[4], 2 * i + s + 1)
                    with pe.Fori(first, end) as b:
                        pe.wait_ge(S["agg_ready"], before + b + 1)
                        for k in range(GE // P):
                            last = t.matmul(bank(2 + s, P), u[:, s, k * P:(k + 1) * P], ohd[:, s, k * P:(k + 1) * P],
                                            start=(k == 0), stop=(k == GE // P - 1))
                        last.then_inc(S["agg_psum"], 1)
                    t.matmul(bank(5, 1), zerosb[:, 0:P], zerosb[:, 0:1], start=True, stop=True
                             ).then_inc(S["agg_done"], 1)

                layer2_rows(0, 0)
                layer2_rows(0, 1)
                sum_edges(0, 0)
                with pe.Fori(1, NG // 2) as i:
                    layer2_rows(i, 0)
                    sum_edges(i + -1, 1)
                    layer2_rows(i, 1)
                    sum_edges(i, 0)
                sum_edges(NG // 2 - 1, 1)
                norm_pe(pe)
                stage_end("pe", pe, None)
            def aggregate(q, parts):

                def chunk(i):
                    for r in range(RING):
                        pe.wait_ge(c_loaded[r], steps_pe * (16 * q) + (i * 16 + 16))
                        first = r * P if isinstance(i, int) else (i % RING) * (RING * P) + r * P
                        new = isinstance(i, int) and r == 0
                        for m in range(len(parts)):
                            weights = parts[m][:, ds(first, P)] if len(parts) > 1 else parts[m]
                            for c, w in CHUNKS:
                                last = t.matmul(psum[:, c:c + w], weights, c_ring[:, r, c:c + w],
                                                start=new and m == 0, stop=True, skip_group_check=not (new and m == 0))
                        last.then_inc(S["c_used"], 1)

                chunk(0)
                with pe.Fori(1, steps_pe) as i:
                    chunk(i)

            def node_rows(q, features, weights, width, taken):
                for b in range(NB):
                    after(pe, S["node_taken"], q * NB + b - 3 if b > 3 else 0)
                    o = (b % 4) * BANK
                    t.matmul(psum[:, o:o + width], features[:, b * P:(b + 1) * P], weights[:, 0:width],
                             start=True, stop=True).then_inc(S["node_psum"], 1)

            def feature_rows(weights, features, ready):
                for c, w in CHUNKS:
                    last = t.matmul(psum[:, c:c + w], weights[:, :], features[:, c:c + w], start=True, stop=True)
                last.then_inc(ready, 1)

            if stages >= 5:
                stage_start("pe", pe)
                steps_pe = pe.value_load(parts_tab[0:1, 0:1], min_val=RING, max_val=2 * RING)
                pe.sem_inc(S["c_used"], RING)
                for q in range(2):
                    after(pe, S["deg_taken"], q)
                    aggregate(q, [onesb[:, 0:P]])
                    pe.drain().then_inc(S["deg_psum"], 1)
                pe.wait_ge(S["deg_taken"], 2)
                for j, rows in enumerate((dd, dsr, q2)):
                    for b in range(NB):
                        last = t.matmul(bank(7)[:, j * NB + b:j * NB + b + 1], rows[0:1, b * P:(b + 1) * P],
                                        onesf[0:1, 0:1], start=True, stop=True)
                last.then_inc(S["nd_psum"], 1)
                node_rows(0, x, W["Wfb"], 2 * P, None)
                parts = [hp[:, m, :] for m in range(3)]
                for k, q in enumerate((2, 3)):
                    pe.wait_ge(S["h_parts"], k + 1)
                    if not k:
                        pe.wait_ge(S["node_taken"], NB)
                    aggregate(q, parts)
                    for b in range(NB):
                        for m in range(3):
                            last = t.matmul(psum[:, b * P:(b + 1) * P], hp[:, m, b * P:(b + 1) * P], identb[:, :],
                                            start=False, stop=True, skip_group_check=True)
                    last.then_inc(S["agg_sum"], 1)
                norm_pe(pe)
                stage_end("pe", pe, None)
            if stages >= 6:
                stage_start("pe", pe)
                feature_rows(W["WiT"], x, S["hT_psum"])
                pe.wait_ge(S["weff_ready"], 1)
                pe.wait_ge(S["hT_ready"], 1)
                for k in range(GNN_LAYERS):
                    after(pe, S["hT_next"], k)
                    feature_rows(W["WAT"], hT, S["asym_psum"])
                    pe.wait_ge(S["asym_taken"], k + 1)
                    node_rows(1 + k, hT, weff, P, None)
                    pe.wait_ge(S["h_parts"], 3 + k)
                    aggregate(4 + k, parts)
                    pe.drain().then_inc(S["agg_sum"], 1)
                norm_pe(pe)
                stage_end("pe", pe, None)
            if stages >= 7:
                stage_start("pe", pe)
                feature_rows(W["WqT"], x, S["qk_psum"])
                pe.wait_ge(S["qk_scaled"], 1)
                feature_rows(W["WkT"], x, S["qk_psum"])
                pe.wait_ge(S["qk_scaled"], 2)
                node_rows(1 + GNN_LAYERS, x, W["WvT"], P, None)
                stage_end("pe", pe, None)
                for quad in range(QUADS):
                    stage_start("pe", pe)
                    pe.wait_ge(packed, 16 * 2 * len(QK_SLOTS) * (quad + 1))
                    halves = 2 * HQ
                    with pe.Fori(0, NB) as b:
                        for n in range(halves):
                            hold("pe", pe, S["s_free"], b * halves + n + 1 + quad * NB * halves)
                            for c in range(4):
                                last = t.matmul(bank((n % 2) * 4 + c, CW), kp[0:KQK, n // 2, ds(b * P, P)],
                                                qp[0:KQK, n // 2, ((n % 2) * 4 + c) * CW:((n % 2) * 4 + c + 1) * CW],
                                                start=True, stop=True)
                            last.then_inc(S["s_psum"], 1)
                    pe.wait_ge(S["m_parts_ready"], quad + 1)
                    for b in range(NB):
                        last = t.transpose(psum[0:HQ * 3, b * P:(b + 1) * P],
                                           m_parts[:, b, :, :].rearrange("p h m -> p (h m)"), identf[:, :])
                    last.then_inc(S["m_rows_psum"], 1)
                    stage_end("pe", pe, None)
                    stage_start("pe", pe)
                    pairs = 2 * NB
                    if not quad:
                        pe.sem_inc(S["pw_free"], pairs)
                        pe.sem_inc(S["pv_taken"], 1)

                    def scores(j, n):
                        pe.wait_ge(S["ex_ready"], slot_again(pairs, 3, j, n) + quad * NC * pairs)
                        s0 = (n // 2) * P
                        for e in range(2):
                            hh = (n % 2) * 2 + e
                            last = t.matmul(bank(2 * (n % 3) + e, CW), qp[0:KQK + 3, hh, s0:s0 + P],
                                            kp[0:KQK + 3, hh, ds(j * CW, CW)], start=True, stop=True)
                        last.then_inc(S["sc_psum"], 1)

                    with pe.Fori(0, NC) as j:
                        scores(j, 0)
                        scores(j, 1)
                        for k in range(NB):
                            if k + 1 < NB:
                                scores(j, 2 * k + 2)
                                scores(j, 2 * k + 3)
                            if k == 0:
                                hold("pe", pe, S["pv_taken"], j + 1 + quad * NC)
                            pe.wait_ge(S["pw_ready"], j * pairs + 2 * k + 2 + (quad * NC + 1) * pairs)
                            for hh in range(HQ):
                                last = t.matmul(psum[hh * HW:(hh + 1) * HW, 6 * BANK:6 * BANK + CW],
                                                vaug[:, k, quad * HQ + hh, :],
                                                pw[:, (2 * k + hh // 2) % 4, (hh % 2) * CW:(hh % 2 + 1) * CW],
                                                start=(k == 0), stop=(k == NB - 1))
                            last.then_inc(S["pw_free"], 2)
                    stage_end("pe", pe, None)
                stage_start("pe", pe)
                pe.wait_ge(S["attn_ready"], 1)
                for c, w in CHUNKS:
                    last = t.matmul(psum[:, c:c + w], selh[:, :], z[0:H, c:c + w], start=True, stop=True)
                last.then_inc(S["attn_psum"], 1)
                pe.wait_ge(S["attn_ready"], 2)
                feature_rows(W["WoT"], y, S["wo_psum"])
                norm_pe(pe)
                stage_end("pe", pe, None)
            stage_start("pe", pe)
            for b in range(NB):
                after(pe, S["out_sb"], b - 3)
                t.transpose(bank(b % 4, P), x[:, b * P:(b + 1) * P], identf[:, :]).then_inc(S["out_psum"], 1)


_INS = ["x", "src", "dst", "L0_gnn_W1", "L0_gnn_b1", "L0_gnn_g1", "L0_gnn_be1", "L0_gnn_W2", "L0_gnn_b2", "L0_gnn_g2",
        "L0_gnn_be2", "L1_gnn_W_fwd", "L1_gnn_b_fwd", "L1_gnn_W_bwd", "L1_gnn_b_bwd", "L2_gnn_Wi", "L2_gnn_bi",
        "L2_gnn_A", "L2_gnn_Wp", "L3_gnn_Wq", "L3_gnn_bq", "L3_gnn_Wk", "L3_gnn_bk", "L3_gnn_Wv", "L3_gnn_bv",
        "L3_gnn_Wo", "L3_gnn_bo"]


def kernel(**inputs):
    import numpy as _np
    import concourse.bacc as _bacc
    from concourse import mybir as _mybir
    from concourse.bass_utils import run_bass_kernel_spmd as _run

    a = {n: _np.asarray(inputs[n]) for n in _INS}

    def edges(e):
        padded = _np.full((EP,), NP - 1, e.dtype)
        padded[:E] = e
        return padded

    src, dst = edges(a["src"]), edges(a["dst"])
    wp = a["L2_gnn_Wp"]
    laid = {
        "xT": a["x"].T,
        "src_cols": src.reshape(NT, P).T,
        "dst_cols": dst.reshape(NT, P).T,
        "dst_rows": dst.reshape(1, EP),
        "W1": a["L0_gnn_W1"].T.reshape(2, P, P).transpose(1, 0, 2).reshape(P, 2 * P),
        "W2": a["L0_gnn_W2"],
        "W2T": a["L0_gnn_W2"].T,
        "Wfb": _np.concatenate([a["L1_gnn_W_fwd"], a["L1_gnn_W_bwd"]], axis=1),
        "WiT": a["L2_gnn_Wi"].T,
        "WA": a["L2_gnn_A"],
        "WAT": a["L2_gnn_A"].T,
        "Wp": wp[:, :P],
        "WpT": wp[:, :P].T,
        "WqT": a["L3_gnn_Wq"].T,
        "WkT": a["L3_gnn_Wk"].T,
        "WvT": a["L3_gnn_Wv"].T,
        "WoT": a["L3_gnn_Wo"].T,
        "v_b1": a["L0_gnn_b1"].reshape(P, 1), "v_g1": a["L0_gnn_g1"].reshape(P, 1),
        "v_be1": a["L0_gnn_be1"].reshape(P, 1), "v_b2": a["L0_gnn_b2"].reshape(P, 1),
        "v_g2": a["L0_gnn_g2"].reshape(P, 1), "v_be2": a["L0_gnn_be2"].reshape(P, 1),
        "v_bf": a["L1_gnn_b_fwd"].reshape(P, 1), "v_bb": a["L1_gnn_b_bwd"].reshape(P, 1),
        "v_bi": a["L2_gnn_bi"].reshape(P, 1), "v_q": wp[:, P:P + 1], "v_r": wp[:, P + 1:P + 2],
        "v_bq": a["L3_gnn_bq"].reshape(P, 1), "v_bk": a["L3_gnn_bk"].reshape(P, 1),
        "v_bv": a["L3_gnn_bv"].reshape(P, 1), "v_bo": a["L3_gnn_bo"].reshape(P, 1),
    }
    nc = _bacc.Bacc("TRN2", target_bir_lowering=False, num_devices=1)
    arrays, ins = {}, {}
    for name, array in laid.items():
        array = _np.ascontiguousarray(array)
        arrays[f"in_{name}"] = array
        ins[name] = nc.dram_tensor(f"in_{name}", array.shape, _mybir.dt.from_np(array.dtype), kind="ExternalInput").ap()
    out = nc.dram_tensor("out_x", (N, P), _mybir.dt.float32, kind="ExternalOutput").ap()
    gnn(nc, ins, out, STAGES)
    r = _run(nc, [arrays], core_ids=[0])
    return r.results[0]["out_x"]
```

```python
import concourse.bass as bass
from concourse import mybir
from contextlib import ExitStack

P = 128
N = 3125
NB = -(-N // P)
NP = NB * P
E = 100000
GE = 512
NG = -(-E // GE)
EP = NG * GE
NT = EP // P
UE = 2 * GE
NU = EP // UE
PE_EDGES = 256
NPAIR = EP // PE_EDGES
WP = 98
LAST = E - (NG - 1) * GE
EPS = 1e-5
CENTER = NP // 2
CW = 400
NC = NP // CW
BANK = 512
CHUNKS = [(c, min(BANK, NP - c)) for c in range(0, NP, BANK)]
H = 8
HD = P // H
QUADS = 2
HQ = H // QUADS
HW = 32
QK_SLOTS = ((0, 0), (0, 1), (1, 0), (1, 1), (0, 2), (2, 0))
KQK = len(QK_SLOTS) * HD
MASKED = -1e30
SC = 5
GNN_LAYERS = 4
PAIR0 = 512
VISIT0 = 64
RING = 5
STAGES = 7


def gnn(nc, ins, out, stages=9):
    f32, bf16, f16, i32 = mybir.dt.float32, mybir.dt.bfloat16, mybir.dt.float16, mybir.dt.int32
    ALU = mybir.AluOpType
    ACT = mybir.ActivationFunctionType
    AX = mybir.AxisListType
    ds = bass.ds

    a_table = nc.dram_tensor("a_table", (NP, P), f32).ap()
    a_edges = nc.dram_tensor("a_edges", (NG, P, GE), f32).ap()
    r1_edges = nc.dram_tensor("r1_edges", (P, EP), f32).ap()
    c_parts = nc.dram_tensor("c_parts", (2 * NP, NP), bf16).ap()
    pair_rows = nc.dram_tensor("pair_rows", (2, WP, NPAIR // WP), i32).ap()
    unit_rows = nc.dram_tensor("unit_rows", (2, WP, NU // WP), i32).ap()
    block_rows = nc.dram_tensor("block_rows", (2, NB), i32).ap()
    qk_parts = nc.dram_tensor("qk_parts", (6, P, NP), bf16).ap()
    head_sums = nc.dram_tensor("head_sums", (QUADS, P, NP), f32).ap()
    flag_row = nc.dram_tensor("flag_row", (P, 1), f32).ap()
    pairs_flat = pair_rows.rearrange("a p g -> a (p g)")
    units_flat = unit_rows.rearrange("a p g -> a (p g)")

    ctx = ExitStack()
    with ctx:
        def sem(name):
            return ctx.enter_context(nc.semaphore(name))

        at = [-(-nc.sbuf_base // 64) * 64]
        size = {f32: 4, i32: 4, bf16: 2, f16: 2}

        def sb(name, shape, dt):
            n = size[dt]
            for s in shape[1:]:
                n *= s
            t = nc.alloc_sbuf_tensor_at(name, shape, dt, offset=at[0])
            at[0] += -(-n // 64) * 64
            assert at[0] <= nc.sbuf_usable_end, (name, at[0])
            return t

        x = sb("x", [P, NP], f32)
        y = sb("y", [P, NP], f32)
        z = sb("z", [P, NP], f32)
        W = {n: sb(n, [P, a.shape[1]], f32) for n, a in ins.items() if n[0] == "W"}
        V = {n: sb(n, [P, 1], f32) for n, a in ins.items() if n[0] == "v"}
        identf = sb("identf", [P, P], f32)
        identb = sb("identb", [P, P], bf16)
        onesf = sb("onesf", [P, P], f32)
        meanf = sb("meanf", [P, P], f32)
        onesb = sb("onesb", [P, BANK], bf16)
        zerosb = sb("zerosb", [P, BANK], bf16)
        eps1 = sb("eps1", [P, 1], f32)
        iota = sb("iota", [P, NP], f16)
        nodeid = sb("nodeid", [P, NB], f32)
        src_i = sb("src_i", [P, NT], i32)
        dst_i = sb("dst_i", [P, NT], i32)
        src_c = sb("src_c", [P, NT], f32)
        dst_c = sb("dst_c", [P, NT], f32)
        unit_tab = sb("unit_tab", [1, 4, NU], i32)
        block_tab = sb("block_tab", [1, 4, NB], i32)
        parts_tab = sb("parts_tab", [1, 8], i32)
        vec = sb("vec", [P, 32], f32)
        col_b = sb("col_b", [P, 4], bf16)
        col_f = sb("col_f", [P, 8], f32)
        row3 = sb("row3", [3, GE], bf16)
        base = at[0]

        b_rows = sb("b_rows", [P, NP], f32)
        a_rows = sb("a_rows", [P, NP], f32)
        edge_order = sb("edge_order", [WP, EP // WP], i32)
        pair_lim = sb("pair_lim", [WP, 2, NPAIR // WP], i32)
        unit_lim = sb("unit_lim", [WP, 2, NU // WP], i32)
        pair_bc = sb("pair_bc", [NB, 2, NPAIR], i32)
        win = sb("win", [NB, 6, NPAIR], f32)
        edge_w = sb("edge_w", [NB, 8], f32)
        rowf = sb("rowf", [1, 8, NU], f32)
        lim_i = sb("lim_i", [NB, 2], i32)
        b_parts = sb("b_parts", [P, 3, NP], bf16)
        after_b = at[0]

        at[0] = base
        one_src = sb("one_src", [P, 2, NP], bf16)
        one_dst = sb("one_dst", [P, 2, P], bf16)
        c_hi = sb("c_hi", [P, NP], bf16)
        c_lo = sb("c_lo", [P, NP], bf16)
        over = sb("over", [P, NB], f32)
        over_out = sb("over_out", [P, NP], bf16)
        over1 = sb("over1", [P, 1], f32)
        overrow = sb("overrow", [1, P], f32)
        gat = sb("gat", [P, 4, GE], f32)
        gidx = sb("gidx", [P, 4, 4], i32)
        assert at[0] <= after_b - 3 * NP * 2

        at[0] = base
        a_in = sb("a_in", [P, 2, UE], f32)
        r1 = sb("r1", [P, 2, UE], f32)
        stats = sb("stats", [P, NG, 6], f32)
        w2s = sb("w2s", [P, P], f32)
        w2t = sb("w2t", [P, P], f32)
        shared = at[0]
        dst_bc = sb("dst_bc", [P, 2, UE], i32)
        oht = sb("oht", [P, 2, UE], bf16)
        assert at[0] <= after_b - 3 * NP * 2
        at[0] = shared
        u = sb("u", [P, 2, UE], f32)
        ohd = sb("ohd", [P, 2, UE], f32)
        assert at[0] <= after_b

        at[0] = base
        c_ring = sb("c_ring", [P, RING, NP], bf16)
        c_ring_end = at[0]
        hp = sb("hp", [P, 3, NP], bf16)
        hn = sb("hn", [P, NP], f32)
        nd = sb("nd", [P, 3, NB], f32)
        weff = sb("weff", [P, P], f32)
        wtmp = sb("wtmp", [P, 4, P], f32)
        hT_start = at[0]
        hT = sb("hT", [P, NP], f32)
        assert c_ring_end <= after_b - 3 * NP * 2 and hT_start >= after_b
        dd = sb("dd", [P, NP], f32)
        dsr = sb("dsr", [P, NP], f32)
        q2 = sb("q2", [P, NP], f32)

        at[0] = base
        selh = sb("selh", [H, P], f32)
        bv_bc = sb("bv_bc", [P, P], f32)
        qp = sb("qp", [P, HQ, NP], bf16)
        kp = sb("kp", [P, HQ, NP], bf16)
        vaug = sb("vaug", [P, NB, H, HW], f32)
        attn = at[0]
        parts3 = sb("parts3", [P, 3, NP], bf16)
        parts3k = sb("parts3k", [P, 3, NP], bf16)
        at[0] = attn
        mask = sb("mask", [P, RING, NP], bf16)
        masked = sb("masked", [P, 4 * CW], bf16)
        mx = sb("mx", [P, 2 * HQ], f32)
        mxs = sb("mxs", [P, NB, HQ], f32)
        mtmp = sb("mtmp", [P, NB, HQ], f32)
        mb = sb("mb", [P, NB, HQ], bf16)
        m_parts = sb("m_parts", [P, NB, HQ, 3], f32)
        m_rows = sb("m_rows", [HQ * 3, NP], bf16)
        at[0] = attn
        c_raw = sb("c_raw", [P, 2, 2, SC, CW], bf16)
        c_full = sb("c_full", [P, 2, SC, CW], f32)
        ex = sb("ex", [P, 3, 2 * CW], f32)
        pw = sb("pw", [P, 4, 2 * CW], f32)
        o_sb = sb("o_sb", [P, CW], f32)

        psum = ctx.enter_context(nc.psum_tensor("psum", [P, 8 * BANK], f32))

        def bank(j, n=BANK):
            return psum[:, j * BANK:j * BANK + n]

        done = {e: sem(f"{e}_stages") for e in ("sp", "pool", "act", "dve", "pe")}
        loaded = sem("loaded")
        step = {e: sem(f"{e}_steps") for e in ("act", "dve", "pe", "pool")}
        held = {e: sem(f"{e}_held") for e in ("act", "dve", "pe", "pool", "sp")}
        steps = dict.fromkeys(step, 0)
        passed = dict.fromkeys(done, 0)
        names = ("root_asked root_made ln_dve ln_sq ln_psum lims_ready lims_stored rows_back windows_ready "
                 "windows_stored windows_back ab_taken a_stored over1_ready over_stored over_back h1_psum bv_back "
                 "qk_parts_ready qk_stored mask_used m_rows_ready m_rows_stored full_ready sums_back out_sb "
                 "out_stored consts_ready row_sb r1_made vaug_ready mask_ready pw_ready ab_ready slot_free c_made "
                 "c_stored chunk_free over_ready halves_psum halves_taken bn1_ready w2_psum bn2_ready agg_done "
                 "node_psum node_taken nd_psum nd_sb gcn_sum gcn_relu weff_sum weff_abs hT_psum hT_ready "
                 "asym_psum asym_taken delta_ready tanh_ready bq_ready qk_psum qk_scaled m_rows_psum ex_ready "
                 "sc_psum pw_free o_ready pv_taken o_stored x_ready one_ready deg_psum deg_taken visit_free "
                 "visit_ready w2_ready agg_ready agg_added agg_psum h_parts agg_sum weff_ready hT_next s_free "
                 "s_psum m_parts_ready attn_ready attn_psum wo_psum out_psum").split()
        S = {n: sem(n) for n in names}
        gathered = [sem(f"gathered{s}") for s in range(4)]
        a_staged = [sem(f"a_staged{s}") for s in range(4)]
        gat_free = [sem(f"gat_free{s}") for s in range(4)]
        a_loaded = [sem(f"a_loaded{s}") for s in range(2)]
        dst_loaded = [sem(f"dst_loaded{s}") for s in range(2)]
        dst_used = [sem(f"dst_used{s}") for s in range(2)]
        r1_stored = [sem(f"r1_stored{s}") for s in range(2)]
        r1_loaded = [sem(f"r1_loaded{s}") for s in range(2)]
        h2_psum = {n: sem(f"h2_psum{n}") for n in (3, 4)}
        h2_taken = {n: sem(f"h2_taken{n}") for n in (3, 4)}
        packed = sem("packed")
        mask_loaded = [sem(f"mask_loaded{r}") for r in range(RING)]
        raw_loaded = [sem(f"raw_loaded{r}") for r in range(2)]
        c_loaded = [sem(f"c_loaded{s}") for s in range(RING)]
        S["c_used"] = sem("c_used")

        def after(eng, s, n):
            if not (isinstance(n, int) and n <= 0):
                eng.wait_ge(s, n)

        def hold(name, eng, s, n):
            eng.wait_ge(s, n)
            eng.sem_inc(held[name], 1)

        def unit(eng, g):
            word = eng.value_load(unit_tab[0:1, 3, ds(g, 1)], min_val=0, max_val=(VISIT0 + NB * NU) * 1024)
            def number(value, least, most):
                return nc.s_assert_within(eng.snap(value), least, most)

            return (number(word & 31, 0, NB - 1), number((word >> 5) & 31, 1, NB),
                    number(word >> 10, 0, VISIT0 + NB * NU))

        def slot_again(n, slots, j, u):
            before = u - slots if u >= slots else max(w for w in range(n) if w % slots == u % slots) - n
            return j * n + (before + 1 + n)

        def stepped(name, eng, i):
            steps[name] += 1
            i.then_inc(step[name], 1)
            eng.wait_ge(step[name], steps[name])

        def stage_end(name, eng, last):
            if last is None:
                eng.sem_inc(done[name], 1)
            else:
                last.then_inc(done[name], 1)

        def stage_start(name, eng):
            passed[name] += 1
            for e in done:
                eng.wait_ge(done[e], passed[name])

        roots = dict(act=0, dve=0)

        def root_act(act, to, of, bias):
            n = roots["act"] = roots["act"] + 1
            act.wait_ge(S["root_asked"], n)
            nc.scalar.activation(to, of, ACT.Sqrt, bias=bias).then_inc(S["root_made"], 1)

        def root_dve(dve, to):
            n = roots["dve"] = roots["dve"] + 1
            dve.sem_inc(S["root_asked"], 1)
            dve.wait_ge(S["root_made"], n)
            stepped("dve", dve, nc.vector.reciprocal(to, to))

        norms = dict(pe=0, act=0, dve=0)

        def norm_pe(pe):
            n = norms["pe"] = norms["pe"] + 1
            for k, (operand, ready) in enumerate(((y, S["ln_dve"]), (z, S["ln_sq"]))):
                pe.wait_ge(ready, 2 * n - 1 if operand is y else n)
                if operand is z:
                    pe.wait_ge(S["ln_dve"], 2 * n)
                for c, w in CHUNKS:
                    last = nc.tensor.matmul(psum[:, c:c + w], meanf[:, :], operand[:, c:c + w], start=True, stop=True)
                last.then_inc(S["ln_psum"], 1)

        def norm_act(act):
            n = norms["act"] = norms["act"] + 1
            act.wait_ge(S["ln_dve"], 2 * n)
            nc.scalar.activation(z[:, :], y[:, :], ACT.Square).then_inc(S["ln_sq"], 1)
            act.wait_ge(S["ln_psum"], 2 * n)
            root_act(act, z[:, :], psum[:, 0:NP], eps1[:, 0:1])

        def norm_dve(dve):
            n = norms["dve"] = norms["dve"] + 1
            dve.sem_inc(S["ln_dve"], 1)
            dve.wait_ge(S["ln_psum"], 2 * n - 1)
            nc.vector.tensor_tensor(y[:, :], y[:, :], psum[:, 0:NP], ALU.subtract).then_inc(S["ln_dve"], 1)
            dve.wait_ge(S["ln_psum"], 2 * n)
            root_dve(dve, z[:, :])
            nc.vector.tensor_tensor(x[:, :], y[:, :], z[:, :], ALU.mult).then_inc(done["dve"], 1)

        block = ctx.enter_context(nc.Block())

        @block.sync
        def _(sp):
            n = 0
            sp.dma_start(x[:, 0:N], ins["xT"]).then_inc(loaded, 16)
            for name in list(W) + list(V):
                sp.dma_start((W if name in W else V)[name][:, :], ins[name]).then_inc(loaded, 16)
            sp.dma_start(src_i[:, :], ins["src_cols"]).then_inc(loaded, 16)
            sp.dma_start(dst_i[:, :], ins["dst_cols"]).then_inc(loaded, 16)
            sp.dma_start(edge_order[:, :], ins["dst_rows"].rearrange("a (p e) -> (a p) e", p=WP)).then_inc(loaded, 16)
            sp.wait_ge(S["lims_ready"], 1)
            for a in range(2):
                sp.dma_start(pair_rows[a], pair_lim[:, a, :]).then_inc(S["lims_stored"], 16)
                sp.dma_start(unit_rows[a], unit_lim[:, a, :]).then_inc(S["lims_stored"], 16)
            sp.wait_ge(S["lims_stored"], 64)
            for a in range(2):
                sp.dma_start(pair_bc[:, a, :],
                             pairs_flat[a:a + 1, :].broadcast_to([NB, NPAIR])).then_inc(S["rows_back"], 16)
                sp.dma_start(unit_tab[:, a, :], units_flat[a:a + 1, :]).then_inc(S["rows_back"], 16)
            sp.wait_ge(S["windows_ready"], 1)
            with nc.allow_non_contiguous_dma(reason="two columns of 25 numbers"):
                sp.dma_start(block_rows.rearrange("a b -> b a"), lim_i[:, :]).then_inc(S["windows_stored"], 16)
            sp.wait_ge(S["windows_stored"], 16)
            sp.dma_start(block_tab[:, 0:2, :], block_rows.rearrange("(o a) b -> o a b", o=1)).then_inc(S["windows_back"], 16)
            sp.wait_ge(S["ab_taken"], 25)
            sp.dma_start(a_table.rearrange("(b p) f -> p b f", p=P),
                         a_rows[:, :].rearrange("p (b f) -> p b f", f=P)).then_inc(S["a_stored"], 16)
            sp.wait_ge(S["a_stored"], 16)
            stage_end("sp", sp, None)
            if stages >= 1:
                stage_start("sp", sp)
                with sp.Fori(0, NG // 4) as i:
                    for s in range(4):
                        sp.wait_ge(gathered[s], 64 * i + 64)
                        sp.dma_start(a_edges[ds(4 * i + s, 1)].rearrange("o p e -> (o p) e"),
                                     gat[:, s, :]).then_inc(a_staged[s], 16)
                        if s:
                            sp.wait_ge(a_staged[s - 1], 16 * i + 16)
                            sp.sem_inc(gat_free[s - 1], 1)
                    sp.wait_ge(a_staged[3], 16 * i + 16)
                    sp.sem_inc(gat_free[3], 1)
                sp.wait_ge(S["over1_ready"], 1)
                with nc.allow_non_contiguous_dma(reason="a column of 128 numbers"):
                    sp.dma_start(flag_row, over1[:, :]).then_inc(S["over_stored"], 16)
                sp.wait_ge(S["over_stored"], 16)
                sp.dma_start(overrow[:, :], flag_row.rearrange("p o -> o p")).then_inc(S["over_back"], 16)
                stage_end("sp", sp, None)
            def load_counts(q, transposed):

                with sp.Fori(0, steps_sp) as i:
                    for r in range(RING):
                        hold("sp", sp, S["c_used"], steps_sp * (RING * q) + i * RING + (r + 1))
                        if transposed:
                            sp.dma_start_transpose(
                                c_ring[:, r, :],
                                c_parts[ds((i // RING) * NP, NP), ds((i % RING) * (RING * P) + r * P, P)]
                            ).then_inc(c_loaded[r], 16)
                        else:
                            sp.dma_start(c_ring[:, r, :], c_parts[ds(i * (RING * P) + r * P, P), :]
                                         ).then_inc(c_loaded[r], 16)

            if stages >= 2:
                stage_start("sp", sp)
                steps_sp = sp.value_load(parts_tab[0:1, 0:1], min_val=RING, max_val=2 * RING)
                load_counts(0, False)
                load_counts(1, True)
                load_counts(2, False)
                stage_end("sp", sp, None)
            if stages >= 3:
                stage_start("sp", sp)

                def fetch(i):
                    for s in range(2):
                        after(sp, S["h1_psum"], 2 * i + s - 1)
                        sp.dma_start(a_in[:, s, :].rearrange("p (o e) -> p o e", o=2),
                                     a_edges[ds(4 * i + 2 * s, 2)].rearrange("o p e -> p o e")).then_inc(a_loaded[s], 16)
                        after(sp, dst_used[s], i)
                        sp.dma_start(dst_bc[:, s, :], ins["dst_rows"][:, ds((2 * i + s) * UE, UE)].broadcast_to([P, UE])
                                     ).then_inc(dst_loaded[s], 16)

                fetch(0)
                with sp.Fori(1, NU // 2) as i:
                    fetch(i)
                stage_end("sp", sp, None)
            if stages >= 4:
                stage_start("sp", sp)

                def fetch_r1(i):
                    for s in range(2):
                        after(sp, h2_psum[4], 2 * i + s - 1)
                        sp.dma_start(a_in[:, s, :], r1_edges[:, ds((2 * i + s) * UE, UE)]).then_inc(r1_loaded[s], 16)

                fetch_r1(0)
                with sp.Fori(1, NU // 2) as i:
                    fetch_r1(i)
                stage_end("sp", sp, None)
            if stages >= 5:
                stage_start("sp", sp)
                load_counts(3, True)
                load_counts(4, False)
                stage_end("sp", sp, None)
            if stages >= 6:
                stage_start("sp", sp)
                for q in range(5, 5 + GNN_LAYERS):
                    load_counts(q, True)
                stage_end("sp", sp, None)
            if stages >= 7:
                stage_start("sp", sp)
                sp.dma_start(bv_bc[:, :], ins["v_bv"].rearrange("p o -> o p").broadcast_to([P, P])).then_inc(S["bv_back"], 16)
                sp.wait_ge(S["qk_parts_ready"], 1)
                for m in range(3):
                    sp.dma_start(qk_parts[m], parts3[:, m, :]).then_inc(S["qk_stored"], 16)
                    sp.dma_start(qk_parts[3 + m], parts3k[:, m, :]).then_inc(S["qk_stored"], 16)
                sp.wait_ge(S["qk_stored"], 96)
                stage_end("sp", sp, None)
                for quad in range(QUADS):
                    stage_start("sp", sp)
                    rows = slice(quad * HQ * HD, (quad + 1) * HQ * HD)
                    for n, (mq, mk) in enumerate(QK_SLOTS):
                        for pack, m in ((qp, mq), (kp, 3 + mk)):
                            sp.dma_start(pack[n * HD:(n + 1) * HD, :, :],
                                         qk_parts[m][rows, :].rearrange("(h d) n -> d h n", d=HD)).then_inc(packed, 16)
                    with sp.Fori(0, NB // RING) as i:
                        for r in range(RING):
                            hold("sp", sp, S["mask_used"], i * RING + r + 1 + quad * NB)
                            sp.dma_start_transpose(mask[:, r, :], c_parts[0:NP, ds(i * (RING * P) + r * P, P)]
                                                   ).then_inc(mask_loaded[r], 16)
                    sp.wait_ge(S["m_rows_ready"], quad + 1)
                    for hh in range(HQ):
                        sp.dma_start(kp[KQK:KQK + 3, hh, :], m_rows[3 * hh:3 * hh + 3, :]).then_inc(S["m_rows_stored"], 16)
                    sp.wait_ge(S["m_rows_stored"], 16 * HQ * (quad + 1))
                    stage_end("sp", sp, None)
                    stage_start("sp", sp)
                    with sp.Fori(0, NC) as j:
                        for w in range(NB // SC):
                            hold("sp", sp, S["full_ready"], slot_again(NB // SC, 2, j, w) + quad * NC * (NB // SC))
                            for part in range(2):
                                first = part * NP + w * SC * P
                                sp.dma_start(c_raw[:, w % 2, part, :, :],
                                             c_parts[first:first + SC * P, ds(j * CW, CW)].rearrange(
                                                 "(k p) t -> p k t", p=P)).then_inc(raw_loaded[w % 2], 16)
                    stage_end("sp", sp, None)
                stage_start("sp", sp)
                for h in range(H):
                    quad, row = h // HQ, (h % HQ) * HW
                    sp.dma_start(y[h * HD:(h + 1) * HD, :], head_sums[quad, row:row + HD, :]).then_inc(S["sums_back"], 16)
                    sp.dma_start(z[h:h + 1, :], head_sums[quad, row + HD:row + HD + 1, :]).then_inc(S["sums_back"], 16)
                stage_end("sp", sp, None)
            stage_start("sp", sp)
            for b in range(NB):
                rows = min(P, N - b * P)
                sp.wait_ge(S["out_sb"], b + 1)
                sp.dma_start(out[b * P:b * P + rows, :], y[0:rows, b * P:(b + 1) * P]).then_inc(S["out_stored"], 16)
            sp.wait_ge(S["out_stored"], 16 * NB)

        @block.gpsimd
        def _(pool):
            g = nc.gpsimd
            stepped("pool", pool, g.memset(identf[:, :], 0.0))
            stepped("pool", pool, g.memset(identb[:, :], 0.0))
            for m in (identf, identb):
                g.affine_select(out=m[:, :], in_=m[:, :], compare_op=ALU.not_equal, fill=1.0, base=0,
                                pattern=[[-1, P]], channel_multiplier=1)
            pool.wait_ge(loaded, 16 * len(ins))
            for m, sign in ((W["Wp"], 1), (W["WpT"], -1)):
                g.affine_select(out=m[:, :], in_=m[:, :], compare_op=ALU.is_ge, fill=0.0, base=-1,
                                pattern=[[sign, P]], channel_multiplier=-sign)
            g.memset(onesf[:, :], 1.0)
            g.memset(meanf[:, :], 1.0 / P)
            g.memset(onesb[:, :], 1.0)
            g.memset(zerosb[:, :], 0.0)
            g.memset(eps1[:, :], EPS)
            g.iota(nodeid[:, :], pattern=[[P, NB]], base=0, channel_multiplier=1,
                   allow_small_or_imprecise_dtypes=True)
            g.iota(win[:, 0, :], pattern=[[-1, NPAIR]], base=NPAIR, channel_multiplier=0,
                   allow_small_or_imprecise_dtypes=True)
            g.iota(win[:, 1, :], pattern=[[1, NPAIR]], base=1, channel_multiplier=0,
                   allow_small_or_imprecise_dtypes=True)
            g.iota(iota[:, :], pattern=[[1, NP]], base=-CENTER, channel_multiplier=0,
                   allow_small_or_imprecise_dtypes=True).then_inc(S["consts_ready"], 1)
            stage_end("pool", pool, None)
            if stages >= 1:
                stage_start("pool", pool)

                def gather(i):
                    for s in range(4):
                        after(pool, gat_free[s], i)
                        g.tensor_copy(gidx[:, s, :], src_i[:, ds(16 * i + 4 * s, 4)]).then_inc(S["row_sb"], 1)
                        hold("pool", pool, S["row_sb"], 4 * i + s + 1)
                        for k in range(4):
                            g.indirect_dma_start(gat[:, s, k * P:(k + 1) * P], None, a_table,
                                                 bass.IndirectOffsetOnAxis(ap=gidx[:, s, k:k + 1], axis=0)
                                                 ).then_inc(gathered[s], 16)

                gather(0)
                with pool.Fori(1, NG // 4) as i:
                    gather(i)
                stage_end("pool", pool, None)
            for n in range(2, min(stages, 6) + 1):
                stage_start("pool", pool)
                if n == 3:
                    def keep_r1(i):
                        for s in range(2):
                            hold("pool", pool, S["r1_made"], 2 * i + s + 1)
                            pool.dma_start(r1_edges[:, ds((2 * i + s) * UE, UE)], r1[:, s, :]).then_inc(r1_stored[s], 16)

                    with pool.Fori(0, NU // 2) as i:
                        keep_r1(i)
                    for s in range(2):
                        pool.wait_ge(r1_stored[s], 16 * (NU // 2))
                stage_end("pool", pool, None)
            if stages >= 7:
                stage_start("pool", pool)
                stepped("pool", pool, g.memset(selh[:, :], 1.0))
                stepped("pool", pool, g.affine_select(out=selh[:, :], in_=selh[:, :], compare_op=ALU.is_ge, fill=0.0,
                                                      base=0, pattern=[[1, P]], channel_multiplier=-HD))
                stepped("pool", pool, g.affine_select(out=selh[:, :], in_=selh[:, :], compare_op=ALU.is_ge, fill=0.0,
                                                      base=HD - 1, pattern=[[-1, P]], channel_multiplier=HD))
                stepped("pool", pool, g.memset(qp[KQK:P, :, :], 1.0))
                stepped("pool", pool, g.memset(vaug[:, :, :, :], 0.0))
                g.memset(vaug[:, :, :, HD:HD + 1], 1.0).then_inc(S["vaug_ready"], 1)
                stage_end("pool", pool, None)
                for quad in range(QUADS):
                    stage_start("pool", pool)
                    with pool.Fori(0, NB // RING) as i:
                        for r in range(RING):
                            hold("pool", pool, mask_loaded[r], 16 * i + 16 + quad * (16 * NB // RING))
                            g.tensor_scalar(mask[:, r, :], mask[:, r, :], 0.0, MASKED, ALU.is_equal,
                                            ALU.mult).then_inc(S["mask_ready"], 1)
                    stage_end("pool", pool, None)
                    stage_start("pool", pool)
                    if not quad:
                        pool.sem_inc(S["full_ready"], NB // SC)
                    with pool.Fori(0, NC) as j:
                        for w in range(NB // SC):
                            uses = sum(1 for k in range(NB // SC) if k % 2 == w % 2)
                            hold("pool", pool, raw_loaded[w % 2], j * (32 * uses) + 32 * (w // 2 + 1) + quad * NC * 32 * uses)
                            hold("pool", pool, S["pw_ready"],
                                 slot_again(NB // SC, 2, j, w) * (2 * SC) + quad * NC * 2 * NB)
                            g.tensor_tensor(c_full[:, w % 2, :, :], c_raw[:, w % 2, 0, :, :], c_raw[:, w % 2, 1, :, :],
                                            ALU.add).then_inc(S["full_ready"], 1)
                    stage_end("pool", pool, None)
                stage_start("pool", pool)
                stage_end("pool", pool, None)
            stage_start("pool", pool)

        @block.scalar
        def _(act):
            a = nc.scalar
            for b in range(NB):
                act.wait_ge(S["ab_ready"], b + 1)
                o = (b % 4) * BANK
                a.activation(a_rows[:, b * P:(b + 1) * P], psum[:, o:o + P], ACT.Copy)
                last = a.activation(b_rows[:, b * P:(b + 1) * P], psum[:, o + P:o + 2 * P], ACT.Copy)
                last.then_inc(S["ab_taken"], 1)
            act.wait_ge(S["ab_taken"], NB)
            stage_end("act", act, None)
            if stages >= 1:
                stage_start("act", act)
                with act.Fori(0, NB) as b:
                    before = act.value_load(block_tab[0:1, 2, ds(b, 1)], min_val=PAIR0 - NPAIR, max_val=PAIR0 + NB * NPAIR)
                    end = act.value_load(block_tab[0:1, 1, ds(b, 1)], min_val=1, max_val=NPAIR)
                    act.wait_ge(S["slot_free"], (before + end) * 2 + 2)
                    for j in range(NC):
                        a.activation(c_hi[:, j * CW:(j + 1) * CW], bank(j, CW), ACT.Copy).then_inc(S["c_made"], 1)
                    act.wait_ge(S["c_made"], 8 * b + 8)
                    act.dma_start(c_parts[ds(b * P, P), :], c_hi[:, :]).then_inc(S["c_stored"], 16)
                    act.wait_ge(S["chunk_free"], 8 * b + 8)
                    act.dma_start(c_parts[ds(b * P + NP, P), :], c_lo[:, :]).then_inc(S["c_stored"], 16)
                    a.activation(over_out[:, :], c_lo[:, :], ACT.Square, accum_out=over[:, ds(b, 1)]
                                 ).then_inc(S["over_ready"], 1)
                    act.wait_ge(S["over_ready"], b + 1)
                    act.wait_ge(S["c_stored"], 32 * b + 32)
                stage_end("act", act, None)
            if stages >= 2:
                stage_start("act", act)
                for k, half in enumerate((y, z)):
                    act.wait_ge(S["halves_psum"], k + 1)
                    a.activation(half[:, :], psum[:, 0:NP], ACT.Copy).then_inc(S["halves_taken"], 1)
                root_act(act, dsr[:, :], dsr[:, :], 0.0)
                root_act(act, q2[:, :], q2[:, :], 0.0)
                root_act(act, dd[:, :], dd[:, :], 0.0)
                stage_end("act", act, None)
            if stages >= 3:
                stage_start("act", act)
                root_act(act, vec[:, 3:4], vec[:, 3:4], eps1[:, 0:1])
                act.wait_ge(S["bn1_ready"], 1)

                def relu1(i, s):
                    after(act, h2_psum[3], 2 * i + s - 1)
                    after(act, r1_stored[s], 16 * i)
                    act.wait_ge(S["h1_psum"], 2 * i + s + 1)
                    a.activation(r1[:, s, :], psum[:, s * UE:(s + 1) * UE], ACT.Relu, scale=vec[:, 4:5],
                                 bias=vec[:, 5:6]).then_inc(S["r1_made"], 1)

                relu1(0, 0)
                relu1(0, 1)
                with act.Fori(1, NU // 2) as i:
                    relu1(i, 0)
                    relu1(i, 1)
                stage_end("act", act, None)
            if stages >= 4:
                stage_start("act", act)
                root_act(act, vec[:, 3:4], vec[:, 3:4], eps1[:, 0:1])
                act.wait_ge(S["w2_psum"], 1)
                a.activation(w2s[:, :], bank(6, P), ACT.Copy)
                for k in range(GE // P):
                    last = a.activation(row3[:, k * P:(k + 1) * P], bank(7)[0:3, 0:P], ACT.Copy)
                last.then_inc(S["bn2_ready"], 1)

                def relu2(i, s):
                    after(act, S["agg_done"], 2 * i + s - 1)
                    act.wait_ge(h2_psum[4], 2 * i + s + 1)
                    a.activation(u[:, s, :], psum[:, s * UE:(s + 1) * UE], ACT.Relu).then_inc(h2_taken[4], 1)

                relu2(0, 0)
                relu2(0, 1)
                with act.Fori(1, NU // 2) as i:
                    relu2(i, 0)
                    relu2(i, 1)
                norm_act(act)
                stage_end("act", act, None)

            def messages(q, width, scales):
                for b in range(NB):
                    act.wait_ge(S["node_psum"], q * NB + b + 1)
                    for m, (to, factor) in enumerate(scales):
                        o = (b % 4) * BANK + m * P
                        last = a.activation(to[:, b * P:(b + 1) * P], psum[:, o:o + P], ACT.Copy,
                                            scale=nd[:, factor, b:b + 1])
                    last.then_inc(S["node_taken"], 1)

            if stages >= 5:
                stage_start("act", act)
                act.wait_ge(S["nd_psum"], 1)
                a.activation(nd[:, :, :].rearrange("p j b -> p (j b)"), bank(7, 3 * NB), ACT.Copy
                             ).then_inc(S["nd_sb"], 1)
                act.wait_ge(S["nd_sb"], 1)
                messages(0, 2 * P, ((hn, 0), (hT, 1)))
                act.wait_ge(S["gcn_sum"], 1)
                a.activation(y[:, :], y[:, :], ACT.Relu, bias=vec[:, 8:9]).then_inc(S["gcn_relu"], 1)
                norm_act(act)
                stage_end("act", act, None)
            if stages >= 6:
                stage_start("act", act)
                act.wait_ge(S["weff_sum"], 1)
                a.activation(wtmp[:, 0, :], weff[:, :], ACT.Abs, accum_out=vec[:, 9:10]).then_inc(S["weff_abs"], 1)
                act.wait_ge(S["hT_psum"], 1)
                a.activation(hT[:, :], psum[:, 0:NP], ACT.Relu, bias=V["v_bi"][:, 0:1]).then_inc(S["hT_ready"], 1)
                for k in range(GNN_LAYERS):
                    act.wait_ge(S["asym_psum"], k + 1)
                    a.activation(y[:, :], psum[:, 0:NP], ACT.Relu).then_inc(S["asym_taken"], 1)
                    messages(1 + k, P, ((hn, 2),))
                    act.wait_ge(S["delta_ready"], k + 1)
                    a.activation(z[:, :], z[:, :], ACT.Tanh).then_inc(S["tanh_ready"], 1)
                norm_act(act)
                stage_end("act", act, None)

            if stages >= 7:
                stage_start("act", act)
                act.wait_ge(S["bq_ready"], 1)
                act.wait_ge(S["qk_psum"], 1)
                a.activation(y[:, :], psum[:, 0:NP], ACT.Identity, scale=HD ** -0.5, bias=vec[:, 10:11]
                             ).then_inc(S["qk_scaled"], 1)
                act.wait_ge(S["qk_psum"], 2)
                a.activation(z[:, :], psum[:, 0:NP], ACT.Identity, bias=V["v_bk"][:, 0:1]).then_inc(S["qk_scaled"], 1)
                stage_end("act", act, None)
                for quad in range(QUADS):
                    stage_start("act", act)
                    act.wait_ge(S["m_rows_psum"], quad + 1)
                    a.activation(m_rows[:, :], psum[0:HQ * 3, 0:NP], ACT.Copy).then_inc(S["m_rows_ready"], 1)
                    stage_end("act", act, None)
                    stage_start("act", act)
                    pairs = 2 * NB
                    if not quad:
                        act.sem_inc(S["ex_ready"], pairs)
                    with act.Fori(0, NC) as j:
                        for n in range(pairs):
                            act.wait_ge(S["sc_psum"], j * pairs + n + 1 + quad * NC * pairs)
                            act.wait_ge(S["pw_ready"], slot_again(pairs, 3, j, n) + quad * NC * pairs)
                            o = 2 * (n % 3) * BANK
                            a.activation(ex[:, n % 3, :].rearrange("p (h t) -> p h t", h=2),
                                         psum[:, o:o + 2 * BANK].rearrange("p (h t) -> p h t", h=2)[:, :, 0:CW],
                                         ACT.Exp).then_inc(S["ex_ready"], 1)
                        act.wait_ge(S["pw_free"], j * pairs + (2 + quad * NC) * pairs)
                        a.activation(o_sb[:, :], bank(6, CW), ACT.Copy).then_inc(S["o_ready"], 1)
                        hold("act", act, S["o_ready"], j + 1 + quad * NC)
                        act.sem_inc(S["pv_taken"], 1)
                        act.dma_start(head_sums[quad, :, ds(j * CW, CW)], o_sb[:, :]).then_inc(S["o_stored"], 16)
                        hold("act", act, S["o_stored"], 16 * j + 16 + 16 * quad * NC)
                    stage_end("act", act, None)
                stage_start("act", act)
                norm_act(act)
                stage_end("act", act, None)

        @block.vector
        def _(dve):
            v = nc.vector

            def do(i):
                stepped("dve", dve, i)

            def split_col(col):
                do(v.tensor_copy(col_b[:, 0:1], col))
                do(v.tensor_tensor(col_f[:, 4:5], col, col_b[:, 0:1], ALU.subtract))
                do(v.tensor_copy(col_b[:, 1:2], col_f[:, 4:5]))
                do(v.tensor_tensor(col_f[:, 5:6], col_f[:, 4:5], col_b[:, 1:2], ALU.subtract))
                do(v.tensor_copy(col_b[:, 2:3], col_f[:, 5:6]))
                do(v.tensor_copy(col_f[:, 0:3], col_b[:, 0:3]))

            def split(parts, whole):
                do(v.tensor_copy(parts[:, 0, :], whole))
                do(v.tensor_tensor(whole, whole, parts[:, 0, :], ALU.subtract))
                do(v.tensor_copy(parts[:, 1, :], whole))
                do(v.tensor_tensor(whole, whole, parts[:, 1, :], ALU.subtract))
                do(v.tensor_copy(parts[:, 2, :], whole))

            dve.wait_ge(loaded, 16 * len(ins))
            do(v.memset(x[:, N:NP], 0.0))
            do(v.memset(z[:, N:NP], 0.0))
            do(v.tensor_reduce(out=vec[:, 11:12], in_=x[:, 0:N], op=ALU.add, axis=AX.X))
            do(v.tensor_scalar(vec[:, 11:12], vec[:, 11:12], 1.0 / N, None, ALU.mult))
            do(v.tensor_scalar(z[:, 0:N], x[:, 0:N], vec[:, 11:12], None, ALU.subtract))
            dve.sem_inc(S["x_ready"], 1)
            v.tensor_scalar(src_c[:, :], src_i[:, :], float(-CENTER), None, ALU.add)
            v.tensor_scalar(dst_c[:, :], dst_i[:, :], float(-CENTER), None, ALU.add)
            for k, op in enumerate((ALU.min, ALU.max)):
                do(v.tensor_reduce(out=pair_lim[:, k, :], in_=edge_order[:, :].rearrange("p (g e) -> p g e", e=PE_EDGES),
                                   op=op, axis=AX.X))
                do(v.tensor_single_scalar(pair_lim[:, k, :], pair_lim[:, k, :], 7, op=ALU.arith_shift_right))
                do(v.tensor_reduce(out=unit_lim[:, k, :], in_=pair_lim[:, k, :].rearrange("p (g e) -> p g e", e=UE // PE_EDGES),
                                   op=op, axis=AX.X))
            dve.sem_inc(S["lims_ready"], 1)
            dve.wait_ge(S["rows_back"], 64)
            dve.wait_ge(S["consts_ready"], 1)
            do(v.tensor_scalar(win[:, 2, :], pair_bc[:, 0, :], nodeid[0:NB, 0:1], None, ALU.is_le))
            do(v.tensor_scalar(win[:, 3, :], pair_bc[:, 1, :], nodeid[0:NB, 0:1], None, ALU.is_ge))
            do(v.tensor_tensor(win[:, 2, :], win[:, 2, :], win[:, 3, :], ALU.mult))
            do(v.tensor_tensor(win[:, 4, :], win[:, 2, :], win[:, 0, :], ALU.mult))
            do(v.tensor_tensor(win[:, 5, :], win[:, 2, :], win[:, 1, :], ALU.mult))
            do(v.tensor_reduce(out=edge_w[:, 0:2], in_=win[:, 4:6, :], op=ALU.max, axis=AX.X))
            do(v.tensor_scalar(edge_w[:, 2:3], edge_w[:, 0:1], -1.0, float(NPAIR), ALU.mult, ALU.add))
            do(v.tensor_scalar(edge_w[:, 2:3], edge_w[:, 2:3], float(NPAIR - 2), None, ALU.min))
            do(v.tensor_scalar(edge_w[:, 4:5], edge_w[:, 2:3], 2.0, None, ALU.add))
            do(v.tensor_tensor(edge_w[:, 3:4], edge_w[:, 1:2], edge_w[:, 4:5], ALU.max))
            do(v.tensor_copy(lim_i[:, :], edge_w[:, 2:4]))
            dve.sem_inc(S["windows_ready"], 1)

            def visits(tab, n, start):
                do(v.memset(rowf[:, 0, 0:n], 1.0))
                do(v.tensor_tensor(rowf[:, 1, 0:n], tab[:, 1, :], tab[:, 0, :], ALU.subtract))
                do(v.tensor_tensor_scan(rowf[:, 2, 0:n], rowf[:, 0, 0:n], rowf[:, 1, 0:n], 0.0, ALU.mult, ALU.add))
                do(v.tensor_tensor(rowf[:, 3, 0:n], rowf[:, 2, 0:n], tab[:, 1, :], ALU.subtract))
                do(v.tensor_scalar(tab[:, 2, :], rowf[:, 3, 0:n], float(start), None, ALU.add))

            do(v.tensor_scalar(unit_tab[:, 1, :], unit_tab[:, 1, :], 1.0, None, ALU.add))
            visits(unit_tab, NU, VISIT0)
            do(v.scalar_tensor_tensor(rowf[:, 4, :], unit_tab[:, 2, :], 32.0, unit_tab[:, 1, :], ALU.mult, ALU.add))
            do(v.scalar_tensor_tensor(unit_tab[:, 3, :], rowf[:, 4, :], 32.0, unit_tab[:, 0, :], ALU.mult, ALU.add))
            dve.wait_ge(S["windows_back"], 16)
            visits(block_tab, NB, PAIR0)
            dve.wait_ge(S["ab_taken"], NB)
            split(b_parts, b_rows[:, :])
            stage_end("dve", dve, None)

            if stages >= 1:
                stage_start("dve", dve)
                dve.sem_inc(S["one_ready"], 2 * PAIR0)

                def one_hots(b, p, before):
                    for t in range(2):
                        dve.wait_ge(S["slot_free"], (before + p) * 2 + t + 1)
                        v.tensor_scalar(one_src[:, t, :], iota[:, :], src_c[:, ds(p * 2 + t, 1)], None, ALU.is_equal)
                        v.tensor_scalar(one_dst[:, t, :], iota[:, ds(b * P, P)], dst_c[:, ds(p * 2 + t, 1)], None,
                                        ALU.is_equal).then_inc(S["one_ready"], 1)

                def window(eng, b):
                    first = eng.value_load(block_tab[0:1, 0, ds(b, 1)], min_val=0, max_val=NPAIR - 2)
                    end = eng.value_load(block_tab[0:1, 1, ds(b, 1)], min_val=2, max_val=NPAIR)
                    before = eng.value_load(block_tab[0:1, 2, ds(b, 1)], min_val=PAIR0 - NPAIR, max_val=PAIR0 + NB * NPAIR)
                    return first, end, before

                def rest_of_counts(b):
                    for j in range(NC):
                        dve.wait_ge(S["c_made"], 8 * b + j + 1)
                        v.tensor_tensor(c_lo[:, j * CW:(j + 1) * CW], bank(j, CW), c_hi[:, j * CW:(j + 1) * CW],
                                        ALU.subtract).then_inc(S["chunk_free"], 1)

                def count_block(b):
                    first, end, before = window(dve, b)
                    one_hots(b, first, before)
                    if not isinstance(b, int):
                        rest_of_counts(b + -1)
                    with dve.Fori(first + 1, end) as p:
                        one_hots(b, p, before)

                count_block(0)
                with dve.Fori(1, NB) as b:
                    count_block(b)
                rest_of_counts(NB - 1)
                dve.wait_ge(S["over_ready"], NB)
                do(v.tensor_reduce(out=over1[:, :], in_=over[:, :], op=ALU.max, axis=AX.X))
                dve.sem_inc(S["over1_ready"], 1)
                dve.wait_ge(S["over_back"], 16)
                do(v.tensor_reduce(out=overrow[:, 0:1], in_=overrow[:, :], op=ALU.max, axis=AX.X))
                do(v.tensor_scalar(overrow[:, 0:1], overrow[:, 0:1], 0.0, 5.0, ALU.is_gt, ALU.mult))
                v.tensor_scalar(parts_tab[:, 0:1], overrow[:, 0:1], 5.0, None, ALU.add).then_inc(done["dve"], 1)
            def batch_norm(gain, shift, bias, to):
                root_dve(dve, vec[:, 3:4])
                do(v.tensor_tensor(vec[:, to:to + 1], vec[:, 3:4], gain, ALU.mult))
                do(v.tensor_tensor(vec[:, 2:3], vec[:, 2:3], bias, ALU.add))
                do(v.tensor_tensor(vec[:, 2:3], bias, vec[:, 2:3], ALU.subtract))
                do(v.tensor_tensor(vec[:, 2:3], vec[:, 2:3], vec[:, to:to + 1], ALU.mult))
                do(v.tensor_tensor(vec[:, to + 1:to + 2], shift, vec[:, 2:3], ALU.add))

            if stages >= 2:
                stage_start("dve", dve)

                def weigh(half, degrees, to):
                    do(v.tensor_tensor(hT[:, :], half[:, :], degrees[:, :], ALU.mult))
                    do(v.tensor_reduce(out=vec[:, to:to + 1], in_=hT[:, :], op=ALU.add, axis=AX.X))
                    do(v.tensor_tensor(hT[:, :], hT[:, :], half[:, :], ALU.mult))
                    do(v.tensor_reduce(out=vec[:, to + 1:to + 2], in_=hT[:, :], op=ALU.add, axis=AX.X))

                dve.wait_ge(S["halves_taken"], 2)
                dve.wait_ge(S["deg_psum"], 1)
                do(v.tensor_copy(dsr[:, :], psum[:, 0:NP]))
                dve.sem_inc(S["deg_taken"], 1)
                weigh(y, dsr, 12)
                dve.wait_ge(S["deg_psum"], 2)
                do(v.tensor_copy(dd[:, :], psum[:, 0:NP]))
                dve.sem_inc(S["deg_taken"], 1)
                weigh(z, dd, 14)
                do(v.tensor_scalar(dsr[:, :], dsr[:, :], 1.0, None, ALU.add))
                root_dve(dve, dsr[:, :])
                do(v.tensor_scalar(q2[:, :], dd[:, :], 1.0, None, ALU.max))
                root_dve(dve, q2[:, :])
                do(v.tensor_scalar(hT[:, :], dd[:, :], 0.0, None, ALU.is_gt))
                do(v.tensor_tensor(q2[:, :], q2[:, :], hT[:, :], ALU.mult))
                do(v.tensor_scalar(dd[:, :], dd[:, :], 1.0, None, ALU.add))
                root_dve(dve, dd[:, :])
                dve.wait_ge(S["deg_psum"], 3)
                do(v.tensor_tensor(hT[:, :], y[:, :], psum[:, 0:NP], ALU.mult))
                do(v.tensor_reduce(out=vec[:, 16:17], in_=hT[:, :], op=ALU.add, axis=AX.X))
                do(v.tensor_tensor(vec[:, 2:3], vec[:, 12:13], vec[:, 14:15], ALU.add))
                do(v.tensor_scalar(vec[:, 2:3], vec[:, 2:3], 1.0 / E, None, ALU.mult))
                do(v.tensor_tensor(vec[:, 3:4], vec[:, 13:14], vec[:, 15:16], ALU.add))
                do(v.tensor_tensor(vec[:, 3:4], vec[:, 3:4], vec[:, 16:17], ALU.add))
                do(v.tensor_tensor(vec[:, 3:4], vec[:, 3:4], vec[:, 16:17], ALU.add))
                do(v.tensor_scalar(vec[:, 3:4], vec[:, 3:4], 1.0 / E, None, ALU.mult))
                do(v.tensor_tensor(vec[:, 17:18], vec[:, 2:3], vec[:, 2:3], ALU.mult))
                do(v.tensor_tensor(vec[:, 3:4], vec[:, 3:4], vec[:, 17:18], ALU.subtract))
                do(v.tensor_scalar(vec[:, 3:4], vec[:, 3:4], 0.0, None, ALU.max))
                stage_end("dve", dve, None)

            if stages >= 3:
                stage_start("dve", dve)
                batch_norm(V["v_g1"][:, 0:1], V["v_be1"][:, 0:1], V["v_b1"][:, 0:1], 4)
                dve.sem_inc(S["bn1_ready"], 1)

                def count(g, k, s, last=GE):
                    dve.wait_ge(h2_psum[3], k + 1)
                    for half, n in ((0, GE), (1, last)):
                        i = v.bn_stats(stats[:, ds(2 * g + half, 1), :].rearrange("p o s -> p (o s)"),
                                       bank(4 + 2 * s + half, n))
                    i.then_inc(h2_taken[3], 1)

                def pass1(i):
                    for s in range(2):
                        g = 2 * i + s
                        first, end, before = unit(dve, g)
                        hold("dve", dve, dst_loaded[s], 16 * i + 16)
                        with dve.Fori(first, end) as b:
                            dve.wait_ge(S["visit_free"], before + b + 1)
                            v.tensor_scalar(oht[:, ds((before + b) & 1, 1), :].rearrange("p o e -> p (o e)"),
                                            dst_bc[:, s, :], nodeid[:, ds(b, 1)], None,
                                            ALU.is_equal).then_inc(S["visit_ready"], 1)
                        after(dve, dst_used[s], i)
                        v.memset(vec[:, 30 + s:31 + s], 0.0).then_inc(dst_used[s], 1)
                        if not isinstance(i, int):
                            count(2 * i + (s - 2), 2 * i + s - 2, s)

                dve.sem_inc(S["visit_ready"], VISIT0)
                pass1(0)
                with dve.Fori(1, NU // 2) as i:
                    pass1(i)
                count(NU - 2, NU - 2, 0)
                count(NU - 1, NU - 1, 1, LAST)
                stage_end("dve", dve, None)

            if stages >= 4:
                stage_start("dve", dve)
                dve.wait_ge(h2_taken[3], NU)
                do(v.bn_aggr(vec[:, 2:4], stats[:, :, :].rearrange("p g s -> p (g s)")))
                batch_norm(V["v_g2"][:, 0:1], V["v_be2"][:, 0:1], V["v_b2"][:, 0:1], 6)
                do(v.tensor_scalar(w2t[:, :], W["W2"][:, :], vec[:, 6:7], None, ALU.mult))
                split_col(vec[:, 7:8])
                do(v.memset(y[:, :], 0.0))
                dve.sem_inc(S["w2_ready"], 1)
                dve.sem_inc(S["agg_ready"], VISIT0)
                dve.sem_inc(S["agg_added"], VISIT0)

                def pass2(i):
                    for s in range(2):
                        g = 2 * i + s
                        first, end, before = unit(dve, g)
                        with dve.Fori(first, end) as b:
                            for k in range(UE // P):
                                last = v.tensor_scalar(ohd[:, s, k * P:(k + 1) * P], iota[:, ds(b * P, P)],
                                                       dst_c[:, ds(g * (UE // P) + k, 1)], None, ALU.is_equal)
                            last.then_inc(S["agg_ready"], 1)
                            dve.wait_ge(S["agg_psum"], before + b + 1)
                            v.tensor_tensor(y[:, ds(b * P, P)], y[:, ds(b * P, P)], bank(4 + s, P),
                                            ALU.add).then_inc(S["agg_added"], 1)
                            dve.wait_ge(S["agg_added"], before + b + 1)

                pass2(0)
                with dve.Fori(1, NU // 2) as i:
                    pass2(i)
                do(v.tensor_tensor(y[:, :], y[:, :], x[:, :], ALU.add))
                norm_dve(dve)
            if stages >= 5:
                stage_start("dve", dve)
                do(v.tensor_tensor(vec[:, 8:9], V["v_bf"][:, 0:1], V["v_bb"][:, 0:1], ALU.add))
                dve.wait_ge(S["node_taken"], NB)
                split(hp, hn[:, :])
                dve.sem_inc(S["h_parts"], 1)
                dve.wait_ge(S["agg_sum"], 1)
                do(v.tensor_tensor(y[:, :], psum[:, 0:NP], dd[:, :], ALU.mult))
                split(hp, hT[:, :])
                dve.sem_inc(S["h_parts"], 1)
                dve.wait_ge(S["agg_sum"], 2)
                do(v.tensor_tensor(z[:, :], psum[:, 0:NP], dsr[:, :], ALU.mult))
                do(v.tensor_tensor(y[:, :], y[:, :], z[:, :], ALU.add))
                dve.sem_inc(S["gcn_sum"], 1)
                dve.wait_ge(S["gcn_relu"], 1)
                do(v.tensor_tensor(y[:, :], y[:, :], x[:, :], ALU.add))
                norm_dve(dve)
            if stages >= 6:
                stage_start("dve", dve)
                do(v.tensor_tensor(weff[:, :], W["Wp"][:, :], W["WpT"][:, :], ALU.add))
                dve.sem_inc(S["weff_sum"], 1)
                do(v.tensor_tensor(W["WAT"][:, :], W["WAT"][:, :], W["WA"][:, :], ALU.subtract))
                dve.wait_ge(S["weff_abs"], 1)
                do(v.tensor_tensor(vec[:, 9:10], vec[:, 9:10], V["v_q"][:, 0:1], ALU.mult))
                do(v.tensor_tensor(vec[:, 9:10], vec[:, 9:10], V["v_r"][:, 0:1], ALU.add))
                do(v.tensor_scalar(wtmp[:, 1, :], identf[:, :], vec[:, 9:10], None, ALU.mult))
                do(v.tensor_tensor(weff[:, :], weff[:, :], wtmp[:, 1, :], ALU.add))
                dve.sem_inc(S["weff_ready"], 1)
                for k in range(GNN_LAYERS):
                    dve.wait_ge(S["node_taken"], (2 + k) * NB)
                    split(hp, hn[:, :])
                    dve.sem_inc(S["h_parts"], 1)
                    dve.wait_ge(S["agg_sum"], 3 + k)
                    do(v.tensor_tensor(z[:, :], psum[:, 0:NP], q2[:, :], ALU.mult))
                    do(v.tensor_tensor(z[:, :], z[:, :], y[:, :], ALU.subtract))
                    dve.sem_inc(S["delta_ready"], 1)
                    dve.wait_ge(S["tanh_ready"], k + 1)
                    do(v.scalar_tensor_tensor(hT[:, :], z[:, :], 0.0, hT[:, :], ALU.max, ALU.add))
                    dve.sem_inc(S["hT_next"], 1)
                do(v.tensor_tensor(y[:, :], hT[:, :], x[:, :], ALU.add))
                norm_dve(dve)
            if stages >= 7:
                stage_start("dve", dve)
                do(v.tensor_scalar(vec[:, 10:11], V["v_bq"][:, 0:1], HD ** -0.5, None, ALU.mult))
                dve.sem_inc(S["bq_ready"], 1)
                dve.wait_ge(S["qk_scaled"], 2)
                split(parts3, y[:, :])
                split(parts3k, z[:, :])
                dve.sem_inc(S["qk_parts_ready"], 1)
                dve.wait_ge(S["bv_back"], 16)
                dve.wait_ge(S["vaug_ready"], 1)
                for b in range(NB):
                    dve.wait_ge(S["node_psum"], (1 + GNN_LAYERS) * NB + b + 1)
                    last = v.tensor_tensor(vaug[:, b, :, 0:HD], bank(b % 4, P).rearrange("p (h d) -> p h d", h=H),
                                           bv_bc[:, :].rearrange("p (h d) -> p h d", h=H), ALU.add)
                    last.then_inc(S["node_taken"], 1)
                dve.wait_ge(S["node_taken"], (2 + GNN_LAYERS) * NB)
                stage_end("dve", dve, None)
                for quad in range(QUADS):
                    stage_start("dve", dve)
                    if not quad:
                        dve.sem_inc(S["mask_used"], RING)
                        dve.sem_inc(S["s_free"], 2)
                    halves = 2 * HQ
                    with dve.Fori(0, NB // RING) as i:
                        for r in range(RING):
                            hold("dve", dve, S["mask_ready"], i * RING + r + 1 + quad * NB)
                            for n in range(halves):
                                o = (n % 2) * 4 * BANK
                                hold("dve", dve, S["s_psum"], i * (RING * halves) + r * halves + n + 1 + quad * NB * halves)
                                v.tensor_tensor_reduce(
                                    out=masked[:, :].rearrange("p (c t) -> p c t", c=4),
                                    in0=psum[:, o:o + 4 * BANK].rearrange("p (c t) -> p c t", c=4)[:, :, 0:CW],
                                    in1=mask[:, r, (n % 2) * 4 * CW:(n % 2 + 1) * 4 * CW].rearrange("p (c t) -> p c t", c=4),
                                    scale=1.0, scalar=-3e38, op0=ALU.add, op1=ALU.max,
                                    accum_out=mx[:, n:n + 1]).then_inc(S["s_free"], 1)
                                hold("dve", dve, S["s_free"], i * (RING * halves) + r * halves + n + 3 + quad * NB * halves)
                            v.tensor_reduce(out=mxs[:, ds(i * RING + r, 1), :].rearrange("p o h -> p (o h)"),
                                            in_=mx[:, :].rearrange("p (h c) -> p h c", c=2), op=ALU.max,
                                            axis=AX.X).then_inc(S["mask_used"], 1)
                            hold("dve", dve, S["mask_used"], i * RING + r + 1 + RING + quad * NB)
                    do(v.tensor_scalar(mtmp[:, :, :], mxs[:, :, :], MASKED / 2, -1.0, ALU.is_gt, ALU.mult))
                    do(v.tensor_tensor(mxs[:, :, :], mxs[:, :, :], mtmp[:, :, :], ALU.mult))
                    for m in range(3):
                        do(v.tensor_copy(mb[:, :, :], mxs[:, :, :]))
                        do(v.tensor_copy(m_parts[:, :, :, m:m + 1].rearrange("p b h o -> p b (h o)"), mb[:, :, :]))
                        if m < 2:
                            do(v.tensor_tensor(mxs[:, :, :], mxs[:, :, :], mb[:, :, :], ALU.subtract))
                    dve.sem_inc(S["m_parts_ready"], 1)
                    stage_end("dve", dve, None)
                    stage_start("dve", dve)
                    pairs = 2 * NB
                    if not quad:
                        dve.sem_inc(S["pw_ready"], pairs)
                    with dve.Fori(0, NC) as j:
                        for n in range(pairs):
                            w = (n // 2) // SC
                            if n % (2 * SC) == 0:
                                dve.wait_ge(S["full_ready"], j * (NB // SC) + w + 1 + (quad * NC + 1) * (NB // SC))
                            dve.wait_ge(S["ex_ready"], j * pairs + n + 1 + (quad * NC + 1) * pairs)
                            dve.wait_ge(S["pw_free"], slot_again(pairs, 4, j, n) + quad * NC * pairs)
                            last = v.scalar_tensor_tensor(
                                pw[:, n % 4, :].rearrange("p (h t) -> p h t", h=2),
                                ex[:, n % 3, :].rearrange("p (h t) -> p h t", h=2), -MASKED,
                                c_full[:, w % 2, (n // 2) % SC:(n // 2) % SC + 1, :].broadcast_to([P, 2, CW]),
                                ALU.min, ALU.mult)
                            last.then_inc(S["pw_ready"], 1)
                    stage_end("dve", dve, None)
                stage_start("dve", dve)
                dve.wait_ge(S["sums_back"], 16 * 2 * H)
                do(v.tensor_scalar(z[0:H, :], z[0:H, :], 0.5, None, ALU.max))
                do(v.reciprocal(z[0:H, :], z[0:H, :]))
                dve.sem_inc(S["attn_ready"], 1)
                dve.wait_ge(S["attn_psum"], 1)
                do(v.tensor_tensor(y[:, :], y[:, :], psum[:, 0:NP], ALU.mult))
                dve.sem_inc(S["attn_ready"], 1)
                dve.wait_ge(S["wo_psum"], 1)
                do(v.scalar_tensor_tensor(y[:, :], psum[:, 0:NP], V["v_bo"][:, 0:1], x[:, :], ALU.add, ALU.add))
                norm_dve(dve)
            stage_start("dve", dve)
            for b in range(NB):
                dve.wait_ge(S["out_psum"], b + 1)
                v.tensor_copy(y[:, b * P:(b + 1) * P], bank(b % 4, P)).then_inc(S["out_sb"], 1)

        @block.tensor
        def _(pe):
            t = nc.tensor
            pe.wait_ge(loaded, 16 * len(ins))
            pe.wait_ge(S["x_ready"], 1)
            for b in range(NB):
                after(pe, S["ab_taken"], b - 3)
                o = (b % 4) * BANK
                t.matmul(psum[:, o:o + 2 * P], z[:, b * P:(b + 1) * P], W["W1"][:, :],
                         start=True, stop=True).then_inc(S["ab_ready"], 1)
            pe.wait_ge(S["consts_ready"], 1)
            stage_end("pe", pe, None)
            if stages >= 1:
                stage_start("pe", pe)
                pe.sem_inc(S["slot_free"], 2 * PAIR0 + 2)

                def window_pe(b):
                    first = pe.value_load(block_tab[0:1, 0, ds(b, 1)], min_val=0, max_val=NPAIR - 2)
                    end = pe.value_load(block_tab[0:1, 1, ds(b, 1)], min_val=2, max_val=NPAIR)
                    before = pe.value_load(block_tab[0:1, 2, ds(b, 1)], min_val=PAIR0 - NPAIR, max_val=PAIR0 + NB * NPAIR)
                    return first, end, before

                def count_pe(b):
                    first, end, before = window_pe(b)
                    for j in range(NC):
                        if not isinstance(b, int):
                            pe.wait_ge(S["chunk_free"], 8 * (b + -1) + j + 1)
                        t.matmul(bank(j, CW), zerosb[:, 0:P], zerosb[:, 0:CW], start=True, stop=True)
                    with pe.Fori(first, end) as p:
                        for s in range(2):
                            pe.wait_ge(S["one_ready"], (before + p) * 2 + s + 1)
                            for j in range(NC):
                                last = t.matmul(bank(j, CW), one_dst[:, s, :], one_src[:, s, j * CW:(j + 1) * CW],
                                                start=False, stop=True, skip_group_check=True)
                            last.then_inc(S["slot_free"], 1)

                count_pe(0)
                with pe.Fori(1, NB) as b:
                    count_pe(b)
                stage_end("pe", pe, None)

            def aggregate(q, parts):

                def chunk(i):
                    for r in range(RING):
                        pe.wait_ge(c_loaded[r], steps_pe * (16 * q) + (i * 16 + 16))
                        first = r * P if isinstance(i, int) else (i % RING) * (RING * P) + r * P
                        new = isinstance(i, int) and r == 0
                        for m in range(len(parts)):
                            weights = parts[m][:, ds(first, P)] if len(parts) > 1 else parts[m]
                            for c, w in CHUNKS:
                                last = t.matmul(psum[:, c:c + w], weights, c_ring[:, r, c:c + w],
                                                start=new and m == 0, stop=True, skip_group_check=not (new and m == 0))
                        last.then_inc(S["c_used"], 1)

                chunk(0)
                with pe.Fori(1, steps_pe) as i:
                    chunk(i)

            def node_rows(q, features, weights, width, taken):
                for b in range(NB):
                    after(pe, S["node_taken"], q * NB + b - 3 if b > 3 else 0)
                    o = (b % 4) * BANK
                    t.matmul(psum[:, o:o + width], features[:, b * P:(b + 1) * P], weights[:, 0:width],
                             start=True, stop=True).then_inc(S["node_psum"], 1)

            def feature_rows(weights, features, ready):
                for c, w in CHUNKS:
                    last = t.matmul(psum[:, c:c + w], weights[:, :], features[:, c:c + w], start=True, stop=True)
                last.then_inc(ready, 1)

            if stages >= 2:
                stage_start("pe", pe)
                for k in range(2):
                    after(pe, S["halves_taken"], k)
                    feature_rows(W["W1"][:, k * P:(k + 1) * P], z, S["halves_psum"])
                pe.wait_ge(S["halves_taken"], 2)
                steps_pe = pe.value_load(parts_tab[0:1, 0:1], min_val=RING, max_val=2 * RING)
                pe.sem_inc(S["c_used"], RING)
                for q in range(2):
                    after(pe, S["deg_taken"], q)
                    aggregate(q, [onesb[:, 0:P]])
                    pe.drain().then_inc(S["deg_psum"], 1)
                pe.wait_ge(S["deg_taken"], 2)
                aggregate(2, [b_parts[:, m, :] for m in range(3)])
                pe.drain().then_inc(S["deg_psum"], 1)
                stage_end("pe", pe, None)

            if stages >= 3:
                stage_start("pe", pe)
                pe.sem_inc(S["visit_free"], VISIT0 + 2)

                def layer1(i, s):
                    first, end, before = unit(pe, 2 * i + s)
                    after(pe, S["r1_made"], 2 * i + s - 1)
                    pe.wait_ge(a_loaded[s], 16 * i + 16)
                    for k in range(UE // P):
                        last = t.matmul(psum[:, s * UE + k * P:s * UE + (k + 1) * P], a_in[:, s, k * P:(k + 1) * P],
                                        identf[:, :], start=(k % (GE // P) == 0), stop=True, skip_group_check=True)
                    with pe.Fori(first, end) as b:
                        pe.wait_ge(S["visit_ready"], before + b + 1)
                        for m in range(3):
                            for half in range(2):
                                last = t.matmul(bank(2 * s + half), b_parts[:, m, ds(b * P, P)],
                                                oht[:, ds((before + b) & 1, 1), half * GE:(half + 1) * GE
                                                    ].rearrange("p o e -> p (o e)"),
                                                start=False, stop=True, skip_group_check=True)
                        last.then_inc(S["visit_free"], 1)
                    t.matmul(bank(2 * s, 1), zerosb[:, 0:P], zerosb[:, 0:1], start=False, stop=True,
                             skip_group_check=True).then_inc(S["h1_psum"], 1)

                def layer2(i, s):
                    pe.wait_ge(S["r1_made"], 2 * i + s + 1)
                    after(pe, h2_taken[3], 2 * i + s - 1)
                    for half in range(2):
                        last = t.matmul(bank(4 + 2 * s + half), W["W2T"][:, :], r1[:, s, half * GE:(half + 1) * GE],
                                        start=True, stop=True)
                    last.then_inc(h2_psum[3], 1)

                layer1(0, 0)
                layer1(0, 1)
                layer2(0, 0)
                with pe.Fori(1, NU // 2) as i:
                    layer1(i, 0)
                    layer2(i + -1, 1)
                    layer1(i, 1)
                    layer2(i, 0)
                layer2(NU // 2 - 1, 1)
                stage_end("pe", pe, None)
            if stages >= 4:
                stage_start("pe", pe)
                pe.wait_ge(S["w2_ready"], 1)
                t.transpose(bank(6, P), w2t[:, :], identf[:, :])
                t.transpose(bank(7)[0:3, 0:P], col_f[:, 0:3], identf[:, :]).then_inc(S["w2_psum"], 1)
                pe.wait_ge(S["bn2_ready"], 1)
                pe.sem_inc(S["agg_psum"], VISIT0)

                def layer2_rows(i, s):
                    pe.wait_ge(r1_loaded[s], 16 * i + 16)
                    after(pe, h2_taken[4], 2 * i + s - 1)
                    for half in range(2):
                        t.matmul(bank(2 * s + half), onesb[0:3, 0:P], row3[:, :], start=True, stop=True)
                    for k in range(UE // P):
                        last = t.matmul(psum[:, s * UE + k * P:s * UE + (k + 1) * P], a_in[:, s, k * P:(k + 1) * P],
                                        w2s[:, :], start=False, stop=True, skip_group_check=True)
                    last.then_inc(h2_psum[4], 1)

                def sum_edges(i, s):
                    first, end, before = unit(pe, 2 * i + s)
                    hold("pe", pe, h2_taken[4], 2 * i + s + 1)
                    with pe.Fori(first, end) as b:
                        pe.wait_ge(S["agg_ready"], before + b + 1)
                        for k in range(UE // P):
                            last = t.matmul(bank(4 + s, P), u[:, s, k * P:(k + 1) * P], ohd[:, s, k * P:(k + 1) * P],
                                            start=(k == 0), stop=(k == UE // P - 1))
                        last.then_inc(S["agg_psum"], 1)
                    t.matmul(bank(6, 1), zerosb[:, 0:P], zerosb[:, 0:1], start=True, stop=True
                             ).then_inc(S["agg_done"], 1)

                layer2_rows(0, 0)
                layer2_rows(0, 1)
                sum_edges(0, 0)
                with pe.Fori(1, NU // 2) as i:
                    layer2_rows(i, 0)
                    sum_edges(i + -1, 1)
                    layer2_rows(i, 1)
                    sum_edges(i, 0)
                sum_edges(NU // 2 - 1, 1)
                norm_pe(pe)
                stage_end("pe", pe, None)

            if stages >= 5:
                stage_start("pe", pe)
                for j, rows in enumerate((dd, dsr, q2)):
                    for b in range(NB):
                        last = t.matmul(bank(7)[:, j * NB + b:j * NB + b + 1], rows[0:1, b * P:(b + 1) * P],
                                        onesf[0:1, 0:1], start=True, stop=True)
                last.then_inc(S["nd_psum"], 1)
                node_rows(0, x, W["Wfb"], 2 * P, None)
                parts = [hp[:, m, :] for m in range(3)]
                for k, q in enumerate((3, 4)):
                    pe.wait_ge(S["h_parts"], k + 1)
                    if not k:
                        pe.wait_ge(S["node_taken"], NB)
                    aggregate(q, parts)
                    for b in range(NB):
                        for m in range(3):
                            last = t.matmul(psum[:, b * P:(b + 1) * P], hp[:, m, b * P:(b + 1) * P], identb[:, :],
                                            start=False, stop=True, skip_group_check=True)
                    last.then_inc(S["agg_sum"], 1)
                norm_pe(pe)
                stage_end("pe", pe, None)
            if stages >= 6:
                stage_start("pe", pe)
                feature_rows(W["WiT"], x, S["hT_psum"])
                pe.wait_ge(S["weff_ready"], 1)
                pe.wait_ge(S["hT_ready"], 1)
                for k in range(GNN_LAYERS):
                    after(pe, S["hT_next"], k)
                    feature_rows(W["WAT"], hT, S["asym_psum"])
                    pe.wait_ge(S["asym_taken"], k + 1)
                    node_rows(1 + k, hT, weff, P, None)
                    pe.wait_ge(S["h_parts"], 3 + k)
                    aggregate(5 + k, parts)
                    pe.drain().then_inc(S["agg_sum"], 1)
                norm_pe(pe)
                stage_end("pe", pe, None)
            if stages >= 7:
                stage_start("pe", pe)
                feature_rows(W["WqT"], x, S["qk_psum"])
                pe.wait_ge(S["qk_scaled"], 1)
                feature_rows(W["WkT"], x, S["qk_psum"])
                pe.wait_ge(S["qk_scaled"], 2)
                node_rows(1 + GNN_LAYERS, x, W["WvT"], P, None)
                stage_end("pe", pe, None)
                for quad in range(QUADS):
                    stage_start("pe", pe)
                    pe.wait_ge(packed, 16 * 2 * len(QK_SLOTS) * (quad + 1))
                    halves = 2 * HQ
                    with pe.Fori(0, NB) as b:
                        for n in range(halves):
                            hold("pe", pe, S["s_free"], b * halves + n + 1 + quad * NB * halves)
                            for c in range(4):
                                last = t.matmul(bank((n % 2) * 4 + c, CW), kp[0:KQK, n // 2, ds(b * P, P)],
                                                qp[0:KQK, n // 2, ((n % 2) * 4 + c) * CW:((n % 2) * 4 + c + 1) * CW],
                                                start=True, stop=True)
                            last.then_inc(S["s_psum"], 1)
                    pe.wait_ge(S["m_parts_ready"], quad + 1)
                    for b in range(NB):
                        last = t.transpose(psum[0:HQ * 3, b * P:(b + 1) * P],
                                           m_parts[:, b, :, :].rearrange("p h m -> p (h m)"), identf[:, :])
                    last.then_inc(S["m_rows_psum"], 1)
                    stage_end("pe", pe, None)
                    stage_start("pe", pe)
                    pairs = 2 * NB
                    if not quad:
                        pe.sem_inc(S["pw_free"], pairs)
                        pe.sem_inc(S["pv_taken"], 1)

                    def scores(j, n):
                        pe.wait_ge(S["ex_ready"], slot_again(pairs, 3, j, n) + quad * NC * pairs)
                        s0 = (n // 2) * P
                        for e in range(2):
                            hh = (n % 2) * 2 + e
                            last = t.matmul(bank(2 * (n % 3) + e, CW), qp[0:KQK + 3, hh, s0:s0 + P],
                                            kp[0:KQK + 3, hh, ds(j * CW, CW)], start=True, stop=True)
                        last.then_inc(S["sc_psum"], 1)

                    with pe.Fori(0, NC) as j:
                        scores(j, 0)
                        scores(j, 1)
                        for k in range(NB):
                            if k + 1 < NB:
                                scores(j, 2 * k + 2)
                                scores(j, 2 * k + 3)
                            if k == 0:
                                hold("pe", pe, S["pv_taken"], j + 1 + quad * NC)
                            pe.wait_ge(S["pw_ready"], j * pairs + 2 * k + 2 + (quad * NC + 1) * pairs)
                            for hh in range(HQ):
                                last = t.matmul(psum[hh * HW:(hh + 1) * HW, 6 * BANK:6 * BANK + CW],
                                                vaug[:, k, quad * HQ + hh, :],
                                                pw[:, (2 * k + hh // 2) % 4, (hh % 2) * CW:(hh % 2 + 1) * CW],
                                                start=(k == 0), stop=(k == NB - 1))
                            last.then_inc(S["pw_free"], 2)
                    stage_end("pe", pe, None)
                stage_start("pe", pe)
                pe.wait_ge(S["attn_ready"], 1)
                for c, w in CHUNKS:
                    last = t.matmul(psum[:, c:c + w], selh[:, :], z[0:H, c:c + w], start=True, stop=True)
                last.then_inc(S["attn_psum"], 1)
                pe.wait_ge(S["attn_ready"], 2)
                feature_rows(W["WoT"], y, S["wo_psum"])
                norm_pe(pe)
                stage_end("pe", pe, None)
            stage_start("pe", pe)
            for b in range(NB):
                after(pe, S["out_sb"], b - 3)
                t.transpose(bank(b % 4, P), x[:, b * P:(b + 1) * P], identf[:, :]).then_inc(S["out_psum"], 1)


_INS = ["x", "src", "dst", "L0_gnn_W1", "L0_gnn_b1", "L0_gnn_g1", "L0_gnn_be1", "L0_gnn_W2", "L0_gnn_b2", "L0_gnn_g2",
        "L0_gnn_be2", "L1_gnn_W_fwd", "L1_gnn_b_fwd", "L1_gnn_W_bwd", "L1_gnn_b_bwd", "L2_gnn_Wi", "L2_gnn_bi",
        "L2_gnn_A", "L2_gnn_Wp", "L3_gnn_Wq", "L3_gnn_bq", "L3_gnn_Wk", "L3_gnn_bk", "L3_gnn_Wv", "L3_gnn_bv",
        "L3_gnn_Wo", "L3_gnn_bo"]


def kernel(**inputs):
    import numpy as _np
    import concourse.bacc as _bacc
    from concourse import mybir as _mybir
    from concourse.bass_utils import run_bass_kernel_spmd as _run

    a = {n: _np.asarray(inputs[n]) for n in _INS}

    def edges(e):
        padded = _np.full((EP,), NP - 1, e.dtype)
        padded[:E] = e
        return padded

    src, dst = edges(a["src"]), edges(a["dst"])
    wp = a["L2_gnn_Wp"]
    laid = {
        "xT": a["x"].T,
        "src_cols": src.reshape(NT, P).T,
        "dst_cols": dst.reshape(NT, P).T,
        "dst_rows": dst.reshape(1, EP),
        "W1": a["L0_gnn_W1"].T.reshape(2, P, P).transpose(1, 0, 2).reshape(P, 2 * P),
        "W2": a["L0_gnn_W2"],
        "W2T": a["L0_gnn_W2"].T,
        "Wfb": _np.concatenate([a["L1_gnn_W_fwd"], a["L1_gnn_W_bwd"]], axis=1),
        "WiT": a["L2_gnn_Wi"].T,
        "WA": a["L2_gnn_A"],
        "WAT": a["L2_gnn_A"].T,
        "Wp": wp[:, :P],
        "WpT": wp[:, :P].T,
        "WqT": a["L3_gnn_Wq"].T,
        "WkT": a["L3_gnn_Wk"].T,
        "WvT": a["L3_gnn_Wv"].T,
        "WoT": a["L3_gnn_Wo"].T,
        "v_b1": a["L0_gnn_b1"].reshape(P, 1), "v_g1": a["L0_gnn_g1"].reshape(P, 1),
        "v_be1": a["L0_gnn_be1"].reshape(P, 1), "v_b2": a["L0_gnn_b2"].reshape(P, 1),
        "v_g2": a["L0_gnn_g2"].reshape(P, 1), "v_be2": a["L0_gnn_be2"].reshape(P, 1),
        "v_bf": a["L1_gnn_b_fwd"].reshape(P, 1), "v_bb": a["L1_gnn_b_bwd"].reshape(P, 1),
        "v_bi": a["L2_gnn_bi"].reshape(P, 1), "v_q": wp[:, P:P + 1], "v_r": wp[:, P + 1:P + 2],
        "v_bq": a["L3_gnn_bq"].reshape(P, 1), "v_bk": a["L3_gnn_bk"].reshape(P, 1),
        "v_bv": a["L3_gnn_bv"].reshape(P, 1), "v_bo": a["L3_gnn_bo"].reshape(P, 1),
    }
    nc = _bacc.Bacc("TRN2", target_bir_lowering=False, num_devices=1)
    arrays, ins = {}, {}
    for name, array in laid.items():
        array = _np.ascontiguousarray(array)
        arrays[f"in_{name}"] = array
        ins[name] = nc.dram_tensor(f"in_{name}", array.shape, _mybir.dt.from_np(array.dtype), kind="ExternalInput").ap()
    out = nc.dram_tensor("out_x", (N, P), _mybir.dt.float32, kind="ExternalOutput").ap()
    gnn(nc, ins, out, STAGES)
    r = _run(nc, [arrays], core_ids=[0])
    return r.results[0]["out_x"]
```

```python
import concourse.bass as bass
from concourse import mybir
from contextlib import ExitStack

P = 128
N = 3125
NB = -(-N // P)
NP = NB * P
E = 100000
GE = 512
NG = -(-E // GE)
EP = NG * GE
NT = EP // P
UE = 2 * GE
NU = EP // UE
PE_EDGES = 256
NPAIR = EP // PE_EDGES
WP = 98
LAST = E - (NG - 1) * GE
EPS = 1e-5
CENTER = NP // 2
CW = 400
NC = NP // CW
BANK = 512
CHUNKS = [(c, min(BANK, NP - c)) for c in range(0, NP, BANK)]
H = 8
HD = P // H
QUADS = 2
HQ = H // QUADS
HW = 32
QK_SLOTS = ((0, 0), (0, 1), (1, 0), (1, 1), (0, 2), (2, 0))
KQK = len(QK_SLOTS) * HD
MASKED = -1e30
HALVES = (slice(0, 3 * BANK), slice(3 * BANK, NP))
SC = 5
GNN_LAYERS = 4
PAIR0 = 512
VISIT0 = 64
RING = 5


def gnn(nc, ins, out):
    f32, bf16, f16, i32 = mybir.dt.float32, mybir.dt.bfloat16, mybir.dt.float16, mybir.dt.int32
    ALU = mybir.AluOpType
    ACT = mybir.ActivationFunctionType
    AX = mybir.AxisListType
    ds = bass.ds

    a_table = nc.dram_tensor("a_table", (NP, P), f32).ap()
    a_edges = nc.dram_tensor("a_edges", (NG, P, GE), f32).ap()
    r1_edges = nc.dram_tensor("r1_edges", (P, EP), f32).ap()
    c_parts = nc.dram_tensor("c_parts", (2 * NP, NP), bf16).ap()
    pair_rows = nc.dram_tensor("pair_rows", (2, WP, NPAIR // WP), i32).ap()
    unit_rows = nc.dram_tensor("unit_rows", (2, WP, NU // WP), i32).ap()
    block_rows = nc.dram_tensor("block_rows", (2, NB), i32).ap()
    qk_parts = nc.dram_tensor("qk_parts", (6, P, NP), bf16).ap()
    head_sums = nc.dram_tensor("head_sums", (QUADS, P, NP), f32).ap()
    flag_row = nc.dram_tensor("flag_row", (P, 1), f32).ap()
    pairs_flat = pair_rows.rearrange("a p g -> a (p g)")
    units_flat = unit_rows.rearrange("a p g -> a (p g)")

    ctx = ExitStack()
    with ctx:
        def sem(name):
            return ctx.enter_context(nc.semaphore(name))

        at = [-(-nc.sbuf_base // 64) * 64]
        size = {f32: 4, i32: 4, bf16: 2, f16: 2}

        def sb(name, shape, dt):
            n = size[dt]
            for s in shape[1:]:
                n *= s
            t = nc.alloc_sbuf_tensor_at(name, shape, dt, offset=at[0])
            at[0] += -(-n // 64) * 64
            assert at[0] <= nc.sbuf_usable_end, (name, at[0])
            return t

        x = sb("x", [P, NP], f32)
        y = sb("y", [P, NP], f32)
        z_at = at[0]
        z = sb("z", [P, NP], f32)
        W = {n: sb(n, [P, a.shape[1]], f32) for n, a in ins.items() if n[0] == "W"}
        V = {n: sb(n, [P, 1], f32) for n, a in ins.items() if n[0] == "v"}
        identf = sb("identf", [P, P], f32)
        identb = sb("identb", [P, P], bf16)
        meanf = sb("meanf", [P, P], f32)
        onesb = sb("onesb", [P, BANK], bf16)
        zerosb = sb("zerosb", [P, BANK], bf16)
        eps1 = sb("eps1", [P, 1], f32)
        rstd = sb("rstd", [P, NB], f32)
        iota = sb("iota", [P, NP], f16)
        nodeid = sb("nodeid", [P, NB], f32)
        src_i = sb("src_i", [P, NT], i32)
        dst_i = sb("dst_i", [P, NT], i32)
        src_c = sb("src_c", [P, NT], f32)
        dst_c = sb("dst_c", [P, NT], f32)
        unit_tab = sb("unit_tab", [1, 4, NU], i32)
        block_tab = sb("block_tab", [1, 4, NB], i32)
        parts_tab = sb("parts_tab", [1, 8], i32)
        vec = sb("vec", [P, 32], f32)
        col_b = sb("col_b", [P, 4], bf16)
        col_f = sb("col_f", [P, 8], f32)
        row3 = sb("row3", [3, GE], bf16)
        base = at[0]

        b_rows = sb("b_rows", [P, NP], f32)
        a_rows = sb("a_rows", [P, NP], f32)
        edge_order = sb("edge_order", [WP, EP // WP], i32)
        pair_lim = sb("pair_lim", [WP, 2, NPAIR // WP], i32)
        unit_lim = sb("unit_lim", [WP, 2, NU // WP], i32)
        pair_bc = sb("pair_bc", [NB, 2, NPAIR], i32)
        win = sb("win", [NB, 6, NPAIR], f32)
        edge_w = sb("edge_w", [NB, 8], f32)
        rowf = sb("rowf", [1, 5, NU], f32)
        lim_i = sb("lim_i", [NB, 2], i32)
        b_parts = sb("b_parts", [P, 3, NP], bf16)
        after_b = at[0]

        at[0] = base
        c_hi = sb("c_hi", [P, NP], bf16)
        c_lo = sb("c_lo", [P, NP], bf16)
        over = sb("over", [P, NB], f32)
        over_out = sb("over_out", [P, NP], bf16)
        over1 = sb("over1", [P, 1], f32)
        overrow = sb("overrow", [1, P], f32)
        gat = sb("gat", [P, 4, GE], f32)
        gidx = sb("gidx", [P, 4, 4], i32)
        assert at[0] <= after_b - 3 * NP * 2
        at[0] = after_b
        one_src = sb("one_src", [P, 2, 2, NP], bf16)
        one_dst = sb("one_dst", [P, 2, 2, P], bf16)

        at[0] = base
        a_in = sb("a_in", [P, 2, UE], f32)
        r1 = sb("r1", [P, 2, UE], f32)
        stats = sb("stats", [P, NG, 6], f32)
        w2s = sb("w2s", [P, P], f32)
        w2t = sb("w2t", [P, P], f32)
        shared = at[0]
        dst_bc = sb("dst_bc", [P, 2, UE], i32)
        oht = sb("oht", [P, 2, UE], bf16)
        assert at[0] <= after_b - 3 * NP * 2
        at[0] = shared
        u = sb("u", [P, 2, UE], f32)
        ohd = sb("ohd", [P, 2, UE], f32)
        visit_sum = sb("visit_sum", [P, P], f32)
        assert at[0] <= after_b

        at[0] = base
        c_ring = sb("c_ring", [P, RING, NP], bf16)
        c_ring_end = at[0]
        hp = sb("hp", [P, 3, NP], bf16)
        hn = sb("hn", [P, NP], f32)
        nd = sb("nd", [P, NB, 3], f32)
        weff = sb("weff", [P, P], f32)
        wtmp = sb("wtmp", [P, 4, P], f32)
        hT_start = at[0]
        hT = sb("hT", [P, NP], f32)
        assert c_ring_end <= after_b - 3 * NP * 2 and hT_start >= after_b
        dd = sb("dd", [P, NP], f32)
        dsr = sb("dsr", [P, NP], f32)
        q2 = sb("q2", [P, NP], f32)

        at[0] = base
        selh = sb("selh", [H, P], f32)
        bv_bc = sb("bv_bc", [P, P], f32)
        qp = sb("qp", [P, HQ, NP], bf16)
        kp = sb("kp", [P, HQ, NP], bf16)
        vaug = sb("vaug", [P, NB, H, HW], f32)
        attn = at[0]
        parts3 = sb("parts3", [P, 3, NP], bf16)
        parts3k = sb("parts3k", [P, 3, NP], bf16)
        at[0] = attn
        mask = sb("mask", [P, RING, NP], bf16)
        masked = sb("masked", [P, 2, 4 * CW], bf16)
        mx = sb("mx", [P, 2 * HQ], f32)
        mxs = sb("mxs", [P, NB, HQ], f32)
        mtmp = sb("mtmp", [P, NB, HQ], f32)
        mb = sb("mb", [P, NB, HQ], bf16)
        m_parts = sb("m_parts", [P, NB, HQ, 3], f32)
        m_rows = sb("m_rows", [HQ * 3, NP], bf16)
        at[0] = attn
        c_raw = sb("c_raw", [P, 2, 2, SC, CW], bf16)
        c_full = sb("c_full", [P, 3, SC, CW], f32)
        ex = sb("ex", [P, 3, 2 * CW], f32)
        o_sb = sb("o_sb", [P, CW], f32)
        assert 4 * 2 * CW <= NP
        at[0] = z_at
        pw = sb("pw", [P, 4, 2 * CW], f32)

        psum = ctx.enter_context(nc.psum_tensor("psum", [P, 8 * BANK], f32))

        def bank(j, n=BANK):
            return psum[:, j * BANK:j * BANK + n]

        done = {e: sem(f"{e}_stages") for e in ("sp", "pool", "act", "dve", "pe")}
        loaded = sem("loaded")
        step = {e: sem(f"{e}_steps") for e in ("act", "dve", "pe", "pool")}
        held = {e: sem(f"{e}_held") for e in ("act", "dve", "pe", "pool", "sp")}
        steps = dict.fromkeys(step, 0)
        passed = dict.fromkeys(done, 0)
        names = ("root_asked root_made ln_dve ln_psum ln_sq lims_ready lims_stored rows_back windows_ready "
                 "windows_stored windows_back ab_taken a_stored over1_ready over_stored over_back h1_psum bv_back "
                 "qk_parts_ready qk_stored mask_used m_rows_ready m_rows_stored full_ready sums_back out_sb "
                 "out_stored consts_ready row_sb r1_made bn2_ready agg_added agg_taken vaug_ready mask_ready "
                 "pw_ready ab_ready slot_free c_made c_stored chunk_free over_ready halves_psum halves_taken "
                 "bn1_ready w2_psum agg_done agg_psum node_psum node_taken nd_psum nd_sb gcn_sum gcn_relu "
                 "weff_sum weff_abs hT_psum hT_ready asym_psum asym_taken delta_ready tanh_ready bq_ready qk_psum "
                 "qk_scaled m_rows_psum ex_ready pw_free o_stored o_ready pv_taken sc_psum h_parts x_ready "
                 "one_ready deg_psum deg_taken visit_free visit_ready w2_ready agg_ready agg_sum weff_ready "
                 "hT_next s_free s_psum m_parts_ready attn_ready attn_psum wo_psum out_psum").split()
        S = {n: sem(n) for n in names}
        gathered = [sem(f"gathered{s}") for s in range(4)]
        a_staged = [sem(f"a_staged{s}") for s in range(4)]
        gat_free = [sem(f"gat_free{s}") for s in range(4)]
        a_loaded = [sem(f"a_loaded{s}") for s in range(2)]
        dst_loaded = [sem(f"dst_loaded{s}") for s in range(2)]
        dst_used = [sem(f"dst_used{s}") for s in range(2)]
        r1_stored = [sem(f"r1_stored{s}") for s in range(2)]
        r1_loaded = [sem(f"r1_loaded{s}") for s in range(2)]
        h2_psum = {n: sem(f"h2_psum{n}") for n in (3, 4)}
        h2_taken = {n: sem(f"h2_taken{n}") for n in (3, 4)}
        packed = sem("packed")
        mask_loaded = [sem(f"mask_loaded{r}") for r in range(RING)]
        raw_loaded = [sem(f"raw_loaded{r}") for r in range(2)]
        c_loaded = [sem(f"c_loaded{s}") for s in range(RING)]
        S["c_used"] = sem("c_used")

        def after(eng, s, n):
            if not (isinstance(n, int) and n <= 0):
                eng.wait_ge(s, n)

        def hold(name, eng, s, n):
            eng.wait_ge(s, n)
            eng.sem_inc(held[name], 1)

        def unit(eng, g):
            word = eng.value_load(unit_tab[0:1, 3, ds(g, 1)], min_val=0, max_val=(VISIT0 + NB * NU) * 1024)
            def number(value, least, most):
                return nc.s_assert_within(eng.snap(value), least, most)

            return (number(word & 31, 0, NB - 1), number((word >> 5) & 31, 1, NB),
                    number(word >> 10, 0, VISIT0 + NB * NU))

        def slot_again(n, slots, j, u):
            before = u - slots if u >= slots else max(w for w in range(n) if w % slots == u % slots) - n
            return j * n + (before + 1 + n)

        def stepped(name, eng, i):
            steps[name] += 1
            i.then_inc(step[name], 1)
            eng.wait_ge(step[name], steps[name])

        def stage_end(name, eng, last):
            if last is None:
                eng.sem_inc(done[name], 1)
            else:
                last.then_inc(done[name], 1)

        def stage_start(name, eng):
            passed[name] += 1
            for e in done:
                eng.wait_ge(done[e], passed[name])

        roots = dict(act=0, dve=0)

        def root_act(act, to, of, bias):
            n = roots["act"] = roots["act"] + 1
            act.wait_ge(S["root_asked"], n)
            nc.scalar.activation(to, of, ACT.Sqrt, bias=bias).then_inc(S["root_made"], 1)

        def root_dve(dve, to):
            n = roots["dve"] = roots["dve"] + 1
            dve.sem_inc(S["root_asked"], 1)
            dve.wait_ge(S["root_made"], n)
            stepped("dve", dve, nc.vector.reciprocal(to, to))

        norms = dict(pe=0, act=0, dve=0)

        def norm_pe(pe):
            n = norms["pe"] = norms["pe"] + 1
            pe.wait_ge(S["ln_dve"], 3 * n - 2)
            for c, w in CHUNKS:
                last = nc.tensor.matmul(psum[:, c:c + w], meanf[:, :], y[:, c:c + w], start=True, stop=True)
            last.then_inc(S["ln_psum"], 1)
            pe.wait_ge(S["ln_sq"], n)
            for b in range(NB):
                last = nc.tensor.matmul(bank(7)[:, b:b + 1], z[:, b * P:(b + 1) * P], meanf[:, 0:1],
                                        start=True, stop=True)
            last.then_inc(S["ln_psum"], 1)
            pe.wait_ge(S["ln_dve"], 3 * n)
            for b in range(NB):
                last = nc.tensor.matmul(psum[:, b * P:(b + 1) * P], rstd[:, b:b + 1].broadcast_to([P, P]), identf[:, :],
                                        start=True, stop=True)
            last.then_inc(S["ln_psum"], 1)

        def norm_act(act):
            n = norms["act"] = norms["act"] + 1
            act.wait_ge(S["ln_dve"], 3 * n - 1)
            nc.scalar.activation(z[:, :], y[:, :], ACT.Square).then_inc(S["ln_sq"], 1)
            act.wait_ge(S["ln_psum"], 3 * n - 1)
            root_act(act, rstd[:, :], bank(7, NB), eps1[:, 0:1])

        def norm_dve(dve):
            n = norms["dve"] = norms["dve"] + 1
            dve.sem_inc(S["ln_dve"], 1)
            dve.wait_ge(S["ln_psum"], 3 * n - 2)
            nc.vector.tensor_tensor(y[:, :], y[:, :], psum[:, 0:NP], ALU.subtract).then_inc(S["ln_dve"], 1)
            root_dve(dve, rstd[:, :])
            dve.sem_inc(S["ln_dve"], 1)
            dve.wait_ge(S["ln_psum"], 3 * n)
            nc.vector.tensor_tensor(x[:, :], y[:, :], psum[:, 0:NP], ALU.mult).then_inc(done["dve"], 1)

        block = ctx.enter_context(nc.Block())

        @block.sync
        def _(sp):
            sp.dma_start(x[:, 0:N], ins["xT"]).then_inc(loaded, 16)
            for name in list(W) + list(V):
                sp.dma_start((W if name in W else V)[name][:, :], ins[name]).then_inc(loaded, 16)
            sp.dma_start(src_i[:, :], ins["src_cols"]).then_inc(loaded, 16)
            sp.dma_start(dst_i[:, :], ins["dst_cols"]).then_inc(loaded, 16)
            sp.dma_start(edge_order[:, :], ins["dst_rows"].rearrange("a (p e) -> (a p) e", p=WP)).then_inc(loaded, 16)
            sp.wait_ge(S["lims_ready"], 1)
            for a in range(2):
                sp.dma_start(pair_rows[a], pair_lim[:, a, :]).then_inc(S["lims_stored"], 16)
                sp.dma_start(unit_rows[a], unit_lim[:, a, :]).then_inc(S["lims_stored"], 16)
            sp.wait_ge(S["lims_stored"], 64)
            for a in range(2):
                sp.dma_start(pair_bc[:, a, :],
                             pairs_flat[a:a + 1, :].broadcast_to([NB, NPAIR])).then_inc(S["rows_back"], 16)
                sp.dma_start(unit_tab[:, a, :], units_flat[a:a + 1, :]).then_inc(S["rows_back"], 16)
            sp.wait_ge(S["windows_ready"], 1)
            with nc.allow_non_contiguous_dma(reason="two columns of 25 numbers"):
                sp.dma_start(block_rows.rearrange("a b -> b a"), lim_i[:, :]).then_inc(S["windows_stored"], 16)
            sp.wait_ge(S["windows_stored"], 16)
            sp.dma_start(block_tab[:, 0:2, :], block_rows.rearrange("(o a) b -> o a b", o=1)).then_inc(S["windows_back"], 16)
            sp.wait_ge(S["ab_taken"], 25)
            sp.dma_start(a_table.rearrange("(b p) f -> p b f", p=P),
                         a_rows[:, :].rearrange("p (b f) -> p b f", f=P)).then_inc(S["a_stored"], 16)
            sp.wait_ge(S["a_stored"], 16)
            stage_end("sp", sp, None)

            stage_start("sp", sp)
            with sp.Fori(0, NG // 4) as i:
                for s in range(4):
                    sp.wait_ge(gathered[s], 64 * i + 64)
                    sp.dma_start(a_edges[ds(4 * i + s, 1)].rearrange("o p e -> (o p) e"),
                                 gat[:, s, :]).then_inc(a_staged[s], 16)
                    if s:
                        sp.wait_ge(a_staged[s - 1], 16 * i + 16)
                        sp.sem_inc(gat_free[s - 1], 1)
                sp.wait_ge(a_staged[3], 16 * i + 16)
                sp.sem_inc(gat_free[3], 1)
            sp.wait_ge(S["over1_ready"], 1)
            with nc.allow_non_contiguous_dma(reason="a column of 128 numbers"):
                sp.dma_start(flag_row, over1[:, :]).then_inc(S["over_stored"], 16)
            sp.wait_ge(S["over_stored"], 16)
            sp.dma_start(overrow[:, :], flag_row.rearrange("p o -> o p")).then_inc(S["over_back"], 16)
            stage_end("sp", sp, None)

            def load_counts(q, transposed):

                with sp.Fori(0, steps_sp) as i:
                    for r in range(RING):
                        hold("sp", sp, S["c_used"], steps_sp * (RING * q) + i * RING + (r + 1))
                        if transposed:
                            sp.dma_start_transpose(
                                c_ring[:, r, :],
                                c_parts[ds((i // RING) * NP, NP), ds((i % RING) * (RING * P) + r * P, P)]
                            ).then_inc(c_loaded[r], 16)
                        else:
                            sp.dma_start(c_ring[:, r, :], c_parts[ds(i * (RING * P) + r * P, P), :]
                                         ).then_inc(c_loaded[r], 16)

            stage_start("sp", sp)
            steps_sp = sp.value_load(parts_tab[0:1, 0:1], min_val=RING, max_val=2 * RING)
            load_counts(0, False)
            load_counts(1, True)
            load_counts(2, False)
            stage_end("sp", sp, None)

            stage_start("sp", sp)

            def fetch(i):
                for s in range(2):
                    after(sp, S["h1_psum"], 2 * i + s - 1)
                    sp.dma_start(a_in[:, s, :].rearrange("p (o e) -> p o e", o=2),
                                 a_edges[ds(4 * i + 2 * s, 2)].rearrange("o p e -> p o e")).then_inc(a_loaded[s], 16)
                    after(sp, dst_used[s], i)
                    sp.dma_start(dst_bc[:, s, :], ins["dst_rows"][:, ds((2 * i + s) * UE, UE)].broadcast_to([P, UE])
                                 ).then_inc(dst_loaded[s], 16)

            fetch(0)
            with sp.Fori(1, NU // 2) as i:
                fetch(i)
            stage_end("sp", sp, None)

            stage_start("sp", sp)

            def fetch_r1(i):
                for s in range(2):
                    after(sp, h2_psum[4], 2 * i + s - 1)
                    sp.dma_start(a_in[:, s, :], r1_edges[:, ds((2 * i + s) * UE, UE)]).then_inc(r1_loaded[s], 16)

            fetch_r1(0)
            with sp.Fori(1, NU // 2) as i:
                fetch_r1(i)
            stage_end("sp", sp, None)

            stage_start("sp", sp)
            load_counts(3, True)
            load_counts(4, False)
            stage_end("sp", sp, None)

            stage_start("sp", sp)
            for q in range(5, 5 + GNN_LAYERS):
                load_counts(q, True)
            stage_end("sp", sp, None)

            stage_start("sp", sp)
            sp.dma_start(bv_bc[:, :], ins["v_bv"].rearrange("p o -> o p").broadcast_to([P, P])).then_inc(S["bv_back"], 16)
            sp.wait_ge(S["qk_parts_ready"], 1)
            for m in range(3):
                sp.dma_start(qk_parts[m], parts3[:, m, :]).then_inc(S["qk_stored"], 16)
                sp.dma_start(qk_parts[3 + m], parts3k[:, m, :]).then_inc(S["qk_stored"], 16)
            sp.wait_ge(S["qk_stored"], 96)
            stage_end("sp", sp, None)

            for quad in range(QUADS):
                stage_start("sp", sp)
                with sp.Fori(0, NB // RING) as i:
                    for r in range(RING):
                        hold("sp", sp, S["mask_used"], i * RING + r + 1 + quad * NB)
                        sp.dma_start_transpose(mask[:, r, :], c_parts[0:NP, ds(i * (RING * P) + r * P, P)]
                                               ).then_inc(mask_loaded[r], 16)
                sp.wait_ge(S["m_rows_ready"], quad + 1)
                for hh in range(HQ):
                    sp.dma_start(kp[KQK:KQK + 3, hh, :], m_rows[3 * hh:3 * hh + 3, :]).then_inc(S["m_rows_stored"], 16)
                sp.wait_ge(S["m_rows_stored"], 16 * HQ * (quad + 1))
                stage_end("sp", sp, None)
                stage_start("sp", sp)
                with sp.Fori(0, NC) as j:
                    for w in range(NB // SC):
                        hold("sp", sp, S["full_ready"], slot_again(NB // SC, 2, j, w) + quad * NC * (NB // SC))
                        for part in range(2):
                            first = part * NP + w * SC * P
                            sp.dma_start(c_raw[:, w % 2, part, :, :],
                                         c_parts[first:first + SC * P, ds(j * CW, CW)].rearrange(
                                             "(k p) t -> p k t", p=P)).then_inc(raw_loaded[w % 2], 16)
                stage_end("sp", sp, None)
            stage_start("sp", sp)
            for h in range(H):
                quad, row = h // HQ, (h % HQ) * HW
                sp.dma_start(y[h * HD:(h + 1) * HD, :], head_sums[quad, row:row + HD, :]).then_inc(S["sums_back"], 16)
                sp.dma_start(z[h:h + 1, :], head_sums[quad, row + HD:row + HD + 1, :]).then_inc(S["sums_back"], 16)
            stage_end("sp", sp, None)

            stage_start("sp", sp)
            for b in range(NB):
                rows = min(P, N - b * P)
                sp.wait_ge(S["out_sb"], b + 1)
                sp.dma_start(out[b * P:b * P + rows, :], y[0:rows, b * P:(b + 1) * P]).then_inc(S["out_stored"], 16)
            sp.wait_ge(S["out_stored"], 16 * NB)

        @block.gpsimd
        def _(pool):
            g = nc.gpsimd
            stepped("pool", pool, g.memset(identf[:, :], 0.0))
            stepped("pool", pool, g.memset(identb[:, :], 0.0))
            for m in (identf, identb):
                g.affine_select(out=m[:, :], in_=m[:, :], compare_op=ALU.not_equal, fill=1.0, base=0,
                                pattern=[[-1, P]], channel_multiplier=1)
            pool.wait_ge(loaded, 16 * len(ins))
            for m, sign in ((W["Wp"], 1), (W["WpT"], -1)):
                g.affine_select(out=m[:, :], in_=m[:, :], compare_op=ALU.is_ge, fill=0.0, base=-1,
                                pattern=[[sign, P]], channel_multiplier=-sign)
            g.memset(meanf[:, :], 1.0 / P)
            g.memset(onesb[:, :], 1.0)
            g.memset(zerosb[:, :], 0.0)
            g.memset(eps1[:, :], EPS)
            g.iota(nodeid[:, :], pattern=[[P, NB]], base=0, channel_multiplier=1,
                   allow_small_or_imprecise_dtypes=True)
            g.iota(win[:, 0, :], pattern=[[-1, NPAIR]], base=NPAIR, channel_multiplier=0,
                   allow_small_or_imprecise_dtypes=True)
            g.iota(win[:, 1, :], pattern=[[1, NPAIR]], base=1, channel_multiplier=0,
                   allow_small_or_imprecise_dtypes=True)
            g.iota(iota[:, :], pattern=[[1, NP]], base=-CENTER, channel_multiplier=0,
                   allow_small_or_imprecise_dtypes=True).then_inc(S["consts_ready"], 1)
            stage_end("pool", pool, None)

            stage_start("pool", pool)

            def gather(i):
                for s in range(4):
                    after(pool, gat_free[s], i)
                    g.tensor_copy(gidx[:, s, :], src_i[:, ds(16 * i + 4 * s, 4)]).then_inc(S["row_sb"], 1)
                    hold("pool", pool, S["row_sb"], 4 * i + s + 1)
                    for k in range(4):
                        g.indirect_dma_start(gat[:, s, k * P:(k + 1) * P], None, a_table,
                                             bass.IndirectOffsetOnAxis(ap=gidx[:, s, k:k + 1], axis=0)
                                             ).then_inc(gathered[s], 16)

            gather(0)
            with pool.Fori(1, NG // 4) as i:
                gather(i)
            stage_end("pool", pool, None)

            for n in range(2, 7):
                stage_start("pool", pool)
                if n == 3:
                    def keep_r1(i):
                        for s in range(2):
                            hold("pool", pool, S["r1_made"], 2 * i + s + 1)
                            pool.dma_start(r1_edges[:, ds((2 * i + s) * UE, UE)], r1[:, s, :]).then_inc(r1_stored[s], 16)

                    with pool.Fori(0, NU // 2) as i:
                        keep_r1(i)
                    for s in range(2):
                        pool.wait_ge(r1_stored[s], 16 * (NU // 2))
                if n == 4:
                    pool.wait_ge(S["bn2_ready"], 1)
                    pool.sem_inc(S["agg_added"], VISIT0)

                    def add_sums(i):
                        for s in range(2):
                            first, end, before = unit(pool, 2 * i + s)
                            with pool.Fori(first, end) as b:
                                hold("pool", pool, S["agg_taken"], before + b + 1)
                                hold("pool", pool, S["agg_added"], before + b)
                                g.tensor_tensor(y[:, ds(b * P, P)], y[:, ds(b * P, P)], visit_sum[:, :], ALU.add
                                                ).then_inc(S["agg_added"], 1)

                    with pool.Fori(0, NU // 2) as i:
                        add_sums(i)
                stage_end("pool", pool, None)
            stage_start("pool", pool)
            stepped("pool", pool, g.memset(selh[:, :], 1.0))
            stepped("pool", pool, g.affine_select(out=selh[:, :], in_=selh[:, :], compare_op=ALU.is_ge, fill=0.0,
                                                  base=0, pattern=[[1, P]], channel_multiplier=-HD))
            stepped("pool", pool, g.affine_select(out=selh[:, :], in_=selh[:, :], compare_op=ALU.is_ge, fill=0.0,
                                                  base=HD - 1, pattern=[[-1, P]], channel_multiplier=HD))
            stepped("pool", pool, g.memset(qp[KQK:P, :, :], 1.0))
            stepped("pool", pool, g.memset(vaug[:, :, :, :], 0.0))
            g.memset(vaug[:, :, :, HD:HD + 1], 1.0).then_inc(S["vaug_ready"], 1)
            stage_end("pool", pool, None)

            for quad in range(QUADS):
                stage_start("pool", pool)
                with pool.Fori(0, NB // RING) as i:
                    for r in range(RING):
                        hold("pool", pool, mask_loaded[r], 16 * i + 16 + quad * (16 * NB // RING))
                        g.tensor_scalar(mask[:, r, :], mask[:, r, :], 0.0, MASKED, ALU.is_equal,
                                        ALU.mult).then_inc(S["mask_ready"], 1)
                stage_end("pool", pool, None)
                stage_start("pool", pool)
                if not quad:
                    pool.sem_inc(S["full_ready"], NB // SC)
                with pool.Fori(0, NC) as j:
                    for w in range(NB // SC):
                        uses = sum(1 for k in range(NB // SC) if k % 2 == w % 2)
                        hold("pool", pool, raw_loaded[w % 2], j * (32 * uses) + 32 * (w // 2 + 1) + quad * NC * 32 * uses)
                        hold("pool", pool, S["pw_ready"],
                             slot_again(NB // SC, 3, j, w) * (2 * SC) + quad * NC * 2 * NB)
                        g.tensor_tensor(c_full[:, w % 3, :, :], c_raw[:, w % 2, 0, :, :], c_raw[:, w % 2, 1, :, :],
                                        ALU.add).then_inc(S["full_ready"], 1)
                stage_end("pool", pool, None)
            stage_start("pool", pool)
            stage_end("pool", pool, None)

            stage_start("pool", pool)

        @block.scalar
        def _(act):
            a = nc.scalar
            for b in range(NB):
                act.wait_ge(S["ab_ready"], b + 1)
                o = (b % 4) * BANK
                a.activation(a_rows[:, b * P:(b + 1) * P], psum[:, o:o + P], ACT.Copy)
                last = a.activation(b_rows[:, b * P:(b + 1) * P], psum[:, o + P:o + 2 * P], ACT.Copy)
                last.then_inc(S["ab_taken"], 1)
            act.wait_ge(S["ab_taken"], NB)
            stage_end("act", act, None)

            stage_start("act", act)
            with act.Fori(0, NB) as b:
                before = act.value_load(block_tab[0:1, 2, ds(b, 1)], min_val=PAIR0 - NPAIR, max_val=PAIR0 + NB * NPAIR)
                end = act.value_load(block_tab[0:1, 1, ds(b, 1)], min_val=1, max_val=NPAIR)
                act.wait_ge(S["slot_free"], (before + end) * 2 + 4)
                for j in range(NC):
                    a.activation(c_hi[:, j * CW:(j + 1) * CW], bank(j, CW), ACT.Copy).then_inc(S["c_made"], 1)
                act.wait_ge(S["c_made"], 8 * b + 8)
                act.dma_start(c_parts[ds(b * P, P), :], c_hi[:, :]).then_inc(S["c_stored"], 16)
                act.wait_ge(S["chunk_free"], 8 * b + 8)
                act.dma_start(c_parts[ds(b * P + NP, P), :], c_lo[:, :]).then_inc(S["c_stored"], 16)
                a.activation(over_out[:, :], c_lo[:, :], ACT.Square, accum_out=over[:, ds(b, 1)]
                             ).then_inc(S["over_ready"], 1)
                act.wait_ge(S["over_ready"], b + 1)
                act.wait_ge(S["c_stored"], 32 * b + 32)
            stage_end("act", act, None)

            stage_start("act", act)
            for k, half in enumerate((y, z)):
                act.wait_ge(S["halves_psum"], k + 1)
                a.activation(half[:, :], psum[:, 0:NP], ACT.Copy).then_inc(S["halves_taken"], 1)
            root_act(act, dsr[:, :], dsr[:, :], 0.0)
            root_act(act, q2[:, :], q2[:, :], 0.0)
            root_act(act, dd[:, :], dd[:, :], 0.0)
            stage_end("act", act, None)

            stage_start("act", act)
            root_act(act, vec[:, 3:4], vec[:, 3:4], eps1[:, 0:1])
            act.wait_ge(S["bn1_ready"], 1)

            def relu1(i, s):
                after(act, h2_psum[3], 2 * i + s - 1)
                after(act, r1_stored[s], 16 * i)
                act.wait_ge(S["h1_psum"], 2 * i + s + 1)
                a.activation(r1[:, s, :], psum[:, s * UE:(s + 1) * UE], ACT.Relu, scale=vec[:, 4:5],
                             bias=vec[:, 5:6]).then_inc(S["r1_made"], 1)

            relu1(0, 0)
            relu1(0, 1)
            with act.Fori(1, NU // 2) as i:
                relu1(i, 0)
                relu1(i, 1)
            stage_end("act", act, None)

            stage_start("act", act)
            root_act(act, vec[:, 3:4], vec[:, 3:4], eps1[:, 0:1])
            act.wait_ge(S["w2_psum"], 1)
            a.activation(w2s[:, :], bank(6, P), ACT.Copy)
            for k in range(GE // P):
                last = a.activation(row3[:, k * P:(k + 1) * P], bank(7)[0:3, 0:P], ACT.Copy)
            last.then_inc(S["bn2_ready"], 1)

            def relu2(i, s):
                after(act, S["agg_done"], 2 * i + s - 1)
                act.wait_ge(h2_psum[4], 2 * i + s + 1)
                a.activation(u[:, s, :], psum[:, s * UE:(s + 1) * UE], ACT.Relu).then_inc(h2_taken[4], 1)

            def take_sums(i, s):
                first, end, before = unit(act, 2 * i + s)
                with act.Fori(first, end) as b:
                    act.wait_ge(S["agg_added"], before + b)
                    act.wait_ge(S["agg_psum"], before + b + 2)
                    a.activation(visit_sum[:, :], bank(4, P), ACT.Copy).then_inc(S["agg_taken"], 1)

            act.sem_inc(S["agg_taken"], VISIT0)
            relu2(0, 0)
            relu2(0, 1)
            take_sums(0, 0)
            with act.Fori(1, NU // 2) as i:
                relu2(i, 0)
                take_sums(i + -1, 1)
                relu2(i, 1)
                take_sums(i, 0)
            take_sums(NU // 2 - 1, 1)
            norm_act(act)
            stage_end("act", act, None)

            def messages(q, width, scales):
                for b in range(NB):
                    act.wait_ge(S["node_psum"], q * NB + b + 1)
                    for m, (to, factor) in enumerate(scales):
                        o = (b % 4) * BANK + m * P
                        last = a.activation(to[:, b * P:(b + 1) * P], psum[:, o:o + P], ACT.Copy,
                                            scale=nd[:, b, factor:factor + 1])
                    last.then_inc(S["node_taken"], 1)

            stage_start("act", act)
            act.wait_ge(S["nd_psum"], 1)
            a.activation(nd[:, :, :].rearrange("p b j -> p (b j)"), bank(7, 3 * NB), ACT.Copy
                         ).then_inc(S["nd_sb"], 1)
            act.wait_ge(S["nd_sb"], 1)
            messages(0, 2 * P, ((hn, 0), (hT, 1)))
            act.wait_ge(S["gcn_sum"], 1)
            a.activation(y[:, :], y[:, :], ACT.Relu, bias=vec[:, 8:9]).then_inc(S["gcn_relu"], 1)
            norm_act(act)
            stage_end("act", act, None)

            stage_start("act", act)
            act.wait_ge(S["weff_sum"], 1)
            a.activation(wtmp[:, 0, :], weff[:, :], ACT.Abs, accum_out=vec[:, 9:10]).then_inc(S["weff_abs"], 1)
            act.wait_ge(S["hT_psum"], 1)
            a.activation(hT[:, :], psum[:, 0:NP], ACT.Relu, bias=V["v_bi"][:, 0:1]).then_inc(S["hT_ready"], 1)
            for k in range(GNN_LAYERS):
                messages(1 + k, P, ((hn, 2),))
                act.wait_ge(S["asym_psum"], k + 1)
                a.activation(y[:, :], psum[:, 0:NP], ACT.Relu).then_inc(S["asym_taken"], 1)
                for n, half in enumerate(HALVES):
                    act.wait_ge(S["delta_ready"], 2 * k + n + 1)
                    a.activation(z[:, half], z[:, half], ACT.Tanh).then_inc(S["tanh_ready"], 1)
            norm_act(act)
            stage_end("act", act, None)

            stage_start("act", act)
            act.wait_ge(S["bq_ready"], 1)
            act.wait_ge(S["qk_psum"], 1)
            a.activation(y[:, :], psum[:, 0:NP], ACT.Identity, scale=HD ** -0.5, bias=vec[:, 10:11]
                         ).then_inc(S["qk_scaled"], 1)
            act.wait_ge(S["qk_psum"], 2)
            a.activation(z[:, :], psum[:, 0:NP], ACT.Identity, bias=V["v_bk"][:, 0:1]).then_inc(S["qk_scaled"], 1)
            stage_end("act", act, None)

            for quad in range(QUADS):
                stage_start("act", act)
                rows = slice(quad * HQ * HD, (quad + 1) * HQ * HD)
                for n, (mq, mk) in enumerate(QK_SLOTS):
                    for pack, m in ((qp, mq), (kp, 3 + mk)):
                        act.dma_start(pack[n * HD:(n + 1) * HD, :, :],
                                      qk_parts[m][rows, :].rearrange("(h d) n -> d h n", d=HD)).then_inc(packed, 16)
                act.wait_ge(S["m_rows_psum"], quad + 1)
                a.activation(m_rows[:, :], psum[0:HQ * 3, 0:NP], ACT.Copy).then_inc(S["m_rows_ready"], 1)
                stage_end("act", act, None)
                stage_start("act", act)
                pairs = 2 * NB
                if not quad:
                    act.sem_inc(S["ex_ready"], pairs)

                def sums_out(j):
                    act.wait_ge(S["pw_free"], j * pairs + (2 + quad * NC) * pairs)
                    after(act, S["o_stored"], 16 * (j + quad * NC))
                    a.activation(o_sb[:, :], bank(6, CW), ACT.Copy).then_inc(S["o_ready"], 1)
                    hold("act", act, S["o_ready"], j + 1 + quad * NC)
                    act.sem_inc(S["pv_taken"], 1)
                    act.dma_start(head_sums[quad, :, ds(j * CW, CW)], o_sb[:, :]).then_inc(S["o_stored"], 16)

                def exp_round(j):
                    for n in range(pairs):
                        if n == 3 and not (isinstance(j, int) and j == 0):
                            sums_out(j + -1)
                        act.wait_ge(S["sc_psum"], j * pairs + n + 1 + quad * NC * pairs)
                        act.wait_ge(S["pw_ready"], slot_again(pairs, 3, j, n) + quad * NC * pairs)
                        o = 2 * (n % 3) * BANK
                        a.activation(ex[:, n % 3, :].rearrange("p (h t) -> p h t", h=2),
                                     psum[:, o:o + 2 * BANK].rearrange("p (h t) -> p h t", h=2)[:, :, 0:CW],
                                     ACT.Exp).then_inc(S["ex_ready"], 1)

                exp_round(0)
                with act.Fori(1, NC) as j:
                    exp_round(j)
                sums_out(NC - 1)
                act.wait_ge(S["o_stored"], 16 * NC * (quad + 1))
                stage_end("act", act, None)
            stage_start("act", act)
            norm_act(act)
            stage_end("act", act, None)

        @block.vector
        def _(dve):
            v = nc.vector

            def do(i):
                stepped("dve", dve, i)

            def split_col(col):
                do(v.tensor_copy(col_b[:, 0:1], col))
                do(v.tensor_tensor(col_f[:, 4:5], col, col_b[:, 0:1], ALU.subtract))
                do(v.tensor_copy(col_b[:, 1:2], col_f[:, 4:5]))
                do(v.tensor_tensor(col_f[:, 5:6], col_f[:, 4:5], col_b[:, 1:2], ALU.subtract))
                do(v.tensor_copy(col_b[:, 2:3], col_f[:, 5:6]))
                do(v.tensor_copy(col_f[:, 0:3], col_b[:, 0:3]))

            def split(parts, whole, at=slice(0, NP)):
                do(v.tensor_copy(parts[:, 0, at], whole[:, at]))
                do(v.tensor_tensor(whole[:, at], whole[:, at], parts[:, 0, at], ALU.subtract))
                do(v.tensor_copy(parts[:, 1, at], whole[:, at]))
                do(v.tensor_tensor(whole[:, at], whole[:, at], parts[:, 1, at], ALU.subtract))
                do(v.tensor_copy(parts[:, 2, at], whole[:, at]))

            def split_messages(whole, taken):
                for i in range(NB // RING):
                    if taken is not None:
                        dve.wait_ge(S["node_taken"], taken + (i + 1) * RING)
                    split(hp, whole, slice(i * RING * P, (i + 1) * RING * P))
                    dve.sem_inc(S["h_parts"], 1)
                dve.sem_inc(S["h_parts"], NB // RING)

            dve.wait_ge(loaded, 16 * len(ins))
            do(v.memset(x[:, N:NP], 0.0))
            do(v.memset(z[:, N:NP], 0.0))
            do(v.tensor_reduce(out=vec[:, 11:12], in_=x[:, 0:N], op=ALU.add, axis=AX.X))
            do(v.tensor_scalar(vec[:, 11:12], vec[:, 11:12], 1.0 / N, None, ALU.mult))
            do(v.tensor_scalar(z[:, 0:N], x[:, 0:N], vec[:, 11:12], None, ALU.subtract))
            dve.sem_inc(S["x_ready"], 1)
            v.tensor_scalar(src_c[:, :], src_i[:, :], float(-CENTER), None, ALU.add)
            v.tensor_scalar(dst_c[:, :], dst_i[:, :], float(-CENTER), None, ALU.add)
            for k, op in enumerate((ALU.min, ALU.max)):
                do(v.tensor_reduce(out=pair_lim[:, k, :], in_=edge_order[:, :].rearrange("p (g e) -> p g e", e=PE_EDGES),
                                   op=op, axis=AX.X))
                do(v.tensor_single_scalar(pair_lim[:, k, :], pair_lim[:, k, :], 7, op=ALU.arith_shift_right))
                do(v.tensor_reduce(out=unit_lim[:, k, :], in_=pair_lim[:, k, :].rearrange(
                    "p (g e) -> p g e", e=UE // PE_EDGES),
                                   op=op, axis=AX.X))
            dve.sem_inc(S["lims_ready"], 1)
            dve.wait_ge(S["rows_back"], 64)
            dve.wait_ge(S["consts_ready"], 1)
            do(v.tensor_scalar(win[:, 2, :], pair_bc[:, 0, :], nodeid[0:NB, 0:1], None, ALU.is_le))
            do(v.tensor_scalar(win[:, 3, :], pair_bc[:, 1, :], nodeid[0:NB, 0:1], None, ALU.is_ge))
            do(v.tensor_tensor(win[:, 2, :], win[:, 2, :], win[:, 3, :], ALU.mult))
            do(v.tensor_tensor(win[:, 4, :], win[:, 2, :], win[:, 0, :], ALU.mult))
            do(v.tensor_tensor(win[:, 5, :], win[:, 2, :], win[:, 1, :], ALU.mult))
            do(v.tensor_reduce(out=edge_w[:, 0:2], in_=win[:, 4:6, :], op=ALU.max, axis=AX.X))
            do(v.tensor_scalar(edge_w[:, 2:3], edge_w[:, 0:1], -1.0, float(NPAIR), ALU.mult, ALU.add))
            do(v.tensor_scalar(edge_w[:, 2:3], edge_w[:, 2:3], float(NPAIR - 2), None, ALU.min))
            do(v.tensor_scalar(edge_w[:, 4:5], edge_w[:, 2:3], 2.0, None, ALU.add))
            do(v.tensor_tensor(edge_w[:, 3:4], edge_w[:, 1:2], edge_w[:, 4:5], ALU.max))
            do(v.tensor_copy(lim_i[:, :], edge_w[:, 2:4]))
            dve.sem_inc(S["windows_ready"], 1)

            def visits(tab, n, start):
                do(v.memset(rowf[:, 0, 0:n], 1.0))
                do(v.tensor_tensor(rowf[:, 1, 0:n], tab[:, 1, :], tab[:, 0, :], ALU.subtract))
                do(v.tensor_tensor_scan(rowf[:, 2, 0:n], rowf[:, 0, 0:n], rowf[:, 1, 0:n], 0.0, ALU.mult, ALU.add))
                do(v.tensor_tensor(rowf[:, 3, 0:n], rowf[:, 2, 0:n], tab[:, 1, :], ALU.subtract))
                do(v.tensor_scalar(tab[:, 2, :], rowf[:, 3, 0:n], float(start), None, ALU.add))

            do(v.tensor_scalar(unit_tab[:, 1, :], unit_tab[:, 1, :], 1.0, None, ALU.add))
            visits(unit_tab, NU, VISIT0)
            do(v.scalar_tensor_tensor(rowf[:, 4, :], unit_tab[:, 2, :], 32.0, unit_tab[:, 1, :], ALU.mult, ALU.add))
            do(v.scalar_tensor_tensor(unit_tab[:, 3, :], rowf[:, 4, :], 32.0, unit_tab[:, 0, :], ALU.mult, ALU.add))
            dve.wait_ge(S["windows_back"], 16)
            visits(block_tab, NB, PAIR0)
            dve.wait_ge(S["ab_taken"], NB)
            split(b_parts, b_rows)
            stage_end("dve", dve, None)

            stage_start("dve", dve)
            dve.sem_inc(S["one_ready"], 2 * PAIR0)

            def one_hots(b, p, before):
                slot = (before + p) & 1
                for t in range(2):
                    dve.wait_ge(S["slot_free"], (before + p) * 2 + t + 1)
                    v.tensor_scalar(one_src[:, ds(slot, 1), t, :].rearrange("p o n -> p (o n)"), iota[:, :],
                                    src_c[:, ds(p * 2 + t, 1)], None, ALU.is_equal)
                    v.tensor_scalar(one_dst[:, ds(slot, 1), t, :].rearrange("p o n -> p (o n)"),
                                    iota[:, ds(b * P, P)], dst_c[:, ds(p * 2 + t, 1)], None,
                                    ALU.is_equal).then_inc(S["one_ready"], 1)

            def window(eng, b):
                first = eng.value_load(block_tab[0:1, 0, ds(b, 1)], min_val=0, max_val=NPAIR - 2)
                end = eng.value_load(block_tab[0:1, 1, ds(b, 1)], min_val=2, max_val=NPAIR)
                before = eng.value_load(block_tab[0:1, 2, ds(b, 1)], min_val=PAIR0 - NPAIR, max_val=PAIR0 + NB * NPAIR)
                return first, end, before

            def rest_of_counts(b):
                for j in range(NC):
                    dve.wait_ge(S["c_made"], 8 * b + j + 1)
                    v.tensor_tensor(c_lo[:, j * CW:(j + 1) * CW], bank(j, CW), c_hi[:, j * CW:(j + 1) * CW],
                                    ALU.subtract).then_inc(S["chunk_free"], 1)

            def count_block(b):
                first, end, before = window(dve, b)
                one_hots(b, first, before)
                if not isinstance(b, int):
                    rest_of_counts(b + -1)
                with dve.Fori(first + 1, end) as p:
                    one_hots(b, p, before)

            count_block(0)
            with dve.Fori(1, NB) as b:
                count_block(b)
            rest_of_counts(NB - 1)
            dve.wait_ge(S["over_ready"], NB)
            do(v.tensor_reduce(out=over1[:, :], in_=over[:, :], op=ALU.max, axis=AX.X))
            dve.sem_inc(S["over1_ready"], 1)
            dve.wait_ge(S["over_back"], 16)
            do(v.tensor_reduce(out=overrow[:, 0:1], in_=overrow[:, :], op=ALU.max, axis=AX.X))
            do(v.tensor_scalar(overrow[:, 0:1], overrow[:, 0:1], 0.0, 5.0, ALU.is_gt, ALU.mult))
            v.tensor_scalar(parts_tab[:, 0:1], overrow[:, 0:1], 5.0, None, ALU.add).then_inc(done["dve"], 1)
            def batch_norm(gain, shift, bias, to):
                root_dve(dve, vec[:, 3:4])
                do(v.tensor_tensor(vec[:, to:to + 1], vec[:, 3:4], gain, ALU.mult))
                do(v.tensor_tensor(vec[:, 2:3], vec[:, 2:3], bias, ALU.add))
                do(v.tensor_tensor(vec[:, 2:3], bias, vec[:, 2:3], ALU.subtract))
                do(v.tensor_tensor(vec[:, 2:3], vec[:, 2:3], vec[:, to:to + 1], ALU.mult))
                do(v.tensor_tensor(vec[:, to + 1:to + 2], shift, vec[:, 2:3], ALU.add))

            stage_start("dve", dve)

            def weigh(half, degrees, to):
                do(v.tensor_tensor(hT[:, :], half[:, :], degrees[:, :], ALU.mult))
                do(v.tensor_reduce(out=vec[:, to:to + 1], in_=hT[:, :], op=ALU.add, axis=AX.X))
                do(v.tensor_tensor(hT[:, :], hT[:, :], half[:, :], ALU.mult))
                do(v.tensor_reduce(out=vec[:, to + 1:to + 2], in_=hT[:, :], op=ALU.add, axis=AX.X))

            dve.wait_ge(S["halves_taken"], 2)
            dve.wait_ge(S["deg_psum"], 1)
            do(v.tensor_copy(dsr[:, :], psum[:, 0:NP]))
            dve.sem_inc(S["deg_taken"], 1)
            weigh(y, dsr, 12)
            dve.wait_ge(S["deg_psum"], 2)
            do(v.tensor_copy(dd[:, :], psum[:, 0:NP]))
            dve.sem_inc(S["deg_taken"], 1)
            weigh(z, dd, 14)
            do(v.tensor_scalar(dsr[:, :], dsr[:, :], 1.0, None, ALU.add))
            root_dve(dve, dsr[:, :])
            do(v.tensor_scalar(q2[:, :], dd[:, :], 1.0, None, ALU.max))
            root_dve(dve, q2[:, :])
            do(v.tensor_scalar(hT[:, :], dd[:, :], 0.0, None, ALU.is_gt))
            do(v.tensor_tensor(q2[:, :], q2[:, :], hT[:, :], ALU.mult))
            do(v.tensor_scalar(dd[:, :], dd[:, :], 1.0, None, ALU.add))
            root_dve(dve, dd[:, :])
            do(v.tensor_scalar(hT[:, :], dd[:, :], identf[:, 0:1], None, ALU.mult))
            for j, factor in ((1, dsr), (2, q2)):
                do(v.scalar_tensor_tensor(hT[:, :], factor[:, :], identf[:, j:j + 1], hT[:, :], ALU.mult, ALU.add))
            dve.wait_ge(S["deg_psum"], 3)
            do(v.tensor_tensor(z[:, :], y[:, :], psum[:, 0:NP], ALU.mult))
            do(v.tensor_reduce(out=vec[:, 16:17], in_=z[:, :], op=ALU.add, axis=AX.X))
            do(v.tensor_tensor(vec[:, 2:3], vec[:, 12:13], vec[:, 14:15], ALU.add))
            do(v.tensor_scalar(vec[:, 2:3], vec[:, 2:3], 1.0 / E, None, ALU.mult))
            do(v.tensor_tensor(vec[:, 3:4], vec[:, 13:14], vec[:, 15:16], ALU.add))
            do(v.tensor_tensor(vec[:, 3:4], vec[:, 3:4], vec[:, 16:17], ALU.add))
            do(v.tensor_tensor(vec[:, 3:4], vec[:, 3:4], vec[:, 16:17], ALU.add))
            do(v.tensor_scalar(vec[:, 3:4], vec[:, 3:4], 1.0 / E, None, ALU.mult))
            do(v.tensor_tensor(vec[:, 17:18], vec[:, 2:3], vec[:, 2:3], ALU.mult))
            do(v.tensor_tensor(vec[:, 3:4], vec[:, 3:4], vec[:, 17:18], ALU.subtract))
            do(v.tensor_scalar(vec[:, 3:4], vec[:, 3:4], 0.0, None, ALU.max))
            stage_end("dve", dve, None)

            stage_start("dve", dve)
            batch_norm(V["v_g1"][:, 0:1], V["v_be1"][:, 0:1], V["v_b1"][:, 0:1], 4)
            dve.sem_inc(S["bn1_ready"], 1)

            def count(g, k, s, last=GE):
                dve.wait_ge(h2_psum[3], k + 1)
                for half, n in ((0, GE), (1, last)):
                    i = v.bn_stats(stats[:, ds(2 * g + half, 1), :].rearrange("p o s -> p (o s)"),
                                   bank(4 + 2 * s + half, n))
                i.then_inc(h2_taken[3], 1)

            def pass1(i):
                for s in range(2):
                    g = 2 * i + s
                    first, end, before = unit(dve, g)
                    hold("dve", dve, dst_loaded[s], 16 * i + 16)
                    with dve.Fori(first, end) as b:
                        dve.wait_ge(S["visit_free"], before + b + 1)
                        v.tensor_scalar(oht[:, ds((before + b) & 1, 1), :].rearrange("p o e -> p (o e)"),
                                        dst_bc[:, s, :], nodeid[:, ds(b, 1)], None,
                                        ALU.is_equal).then_inc(S["visit_ready"], 1)
                    after(dve, dst_used[s], i)
                    v.memset(vec[:, 30 + s:31 + s], 0.0).then_inc(dst_used[s], 1)
                    if not isinstance(i, int):
                        count(2 * i + (s - 2), 2 * i + s - 2, s)

            dve.sem_inc(S["visit_ready"], VISIT0)
            pass1(0)
            with dve.Fori(1, NU // 2) as i:
                pass1(i)
            count(NU - 2, NU - 2, 0)
            count(NU - 1, NU - 1, 1, LAST)
            stage_end("dve", dve, None)

            stage_start("dve", dve)
            dve.wait_ge(h2_taken[3], NU)
            do(v.bn_aggr(vec[:, 2:4], stats[:, :, :].rearrange("p g s -> p (g s)")))
            batch_norm(V["v_g2"][:, 0:1], V["v_be2"][:, 0:1], V["v_b2"][:, 0:1], 6)
            do(v.tensor_scalar(w2t[:, :], W["W2"][:, :], vec[:, 6:7], None, ALU.mult))
            split_col(vec[:, 7:8])
            do(v.memset(y[:, :], 0.0))
            dve.sem_inc(S["w2_ready"], 1)
            dve.sem_inc(S["agg_ready"], VISIT0)

            def pass2(i):
                for s in range(2):
                    g = 2 * i + s
                    first, end, before = unit(dve, g)
                    with dve.Fori(first, end) as b:
                        dve.wait_ge(S["agg_psum"], before + b)
                        for k in range(UE // P):
                            last = v.tensor_scalar(ohd[:, ds((before + b) & 1, 1), k * P:(k + 1) * P
                                                       ].rearrange("p o e -> p (o e)"), iota[:, ds(b * P, P)],
                                                   dst_c[:, ds(g * (UE // P) + k, 1)], None, ALU.is_equal)
                        last.then_inc(S["agg_ready"], 1)

            pass2(0)
            with dve.Fori(1, NU // 2) as i:
                pass2(i)
            first, end, before = unit(dve, NU - 1)
            dve.wait_ge(S["agg_added"], before + end)
            do(v.tensor_tensor(y[:, :], y[:, :], x[:, :], ALU.add))
            norm_dve(dve)
            stage_start("dve", dve)
            do(v.tensor_tensor(vec[:, 8:9], V["v_bf"][:, 0:1], V["v_bb"][:, 0:1], ALU.add))
            split_messages(hn, 0)
            dve.wait_ge(S["agg_sum"], 1)
            do(v.tensor_tensor(y[:, :], psum[:, 0:NP], dd[:, :], ALU.mult))
            split_messages(hT, None)
            dve.wait_ge(S["agg_sum"], 2)
            do(v.tensor_tensor(z[:, :], psum[:, 0:NP], dsr[:, :], ALU.mult))
            do(v.tensor_tensor(y[:, :], y[:, :], z[:, :], ALU.add))
            dve.sem_inc(S["gcn_sum"], 1)
            dve.wait_ge(S["gcn_relu"], 1)
            do(v.tensor_tensor(y[:, :], y[:, :], x[:, :], ALU.add))
            norm_dve(dve)
            stage_start("dve", dve)
            do(v.tensor_tensor(weff[:, :], W["Wp"][:, :], W["WpT"][:, :], ALU.add))
            dve.sem_inc(S["weff_sum"], 1)
            do(v.tensor_tensor(W["WAT"][:, :], W["WAT"][:, :], W["WA"][:, :], ALU.subtract))
            dve.wait_ge(S["weff_abs"], 1)
            do(v.tensor_tensor(vec[:, 9:10], vec[:, 9:10], V["v_q"][:, 0:1], ALU.mult))
            do(v.tensor_tensor(vec[:, 9:10], vec[:, 9:10], V["v_r"][:, 0:1], ALU.add))
            do(v.tensor_scalar(wtmp[:, 1, :], identf[:, :], vec[:, 9:10], None, ALU.mult))
            do(v.tensor_tensor(weff[:, :], weff[:, :], wtmp[:, 1, :], ALU.add))
            dve.sem_inc(S["weff_ready"], 1)
            for k in range(GNN_LAYERS):
                split_messages(hn, (1 + k) * NB)
                dve.wait_ge(S["agg_sum"], 3 + k)
                for half in HALVES:
                    do(v.tensor_tensor(z[:, half], psum[:, half], q2[:, half], ALU.mult))
                    do(v.tensor_tensor(z[:, half], z[:, half], y[:, half], ALU.subtract))
                    dve.sem_inc(S["delta_ready"], 1)
                for n, half in enumerate(HALVES):
                    dve.wait_ge(S["tanh_ready"], 2 * k + n + 1)
                    do(v.scalar_tensor_tensor(hT[:, half], z[:, half], 0.0, hT[:, half], ALU.max, ALU.add))
                    dve.sem_inc(S["hT_next"], 1)
            do(v.tensor_tensor(y[:, :], hT[:, :], x[:, :], ALU.add))
            norm_dve(dve)
            stage_start("dve", dve)
            do(v.tensor_scalar(vec[:, 10:11], V["v_bq"][:, 0:1], HD ** -0.5, None, ALU.mult))
            dve.sem_inc(S["bq_ready"], 1)
            dve.wait_ge(S["qk_scaled"], 1)
            split(parts3, y)
            dve.wait_ge(S["qk_scaled"], 2)
            split(parts3k, z)
            dve.sem_inc(S["qk_parts_ready"], 1)
            dve.wait_ge(S["bv_back"], 16)
            dve.wait_ge(S["vaug_ready"], 1)
            for b in range(NB):
                dve.wait_ge(S["node_psum"], (1 + GNN_LAYERS) * NB + b + 1)
                last = v.tensor_tensor(vaug[:, b, :, 0:HD], bank(b % 4, P).rearrange("p (h d) -> p h d", h=H),
                                       bv_bc[:, :].rearrange("p (h d) -> p h d", h=H), ALU.add)
                last.then_inc(S["node_taken"], 1)
            dve.wait_ge(S["node_taken"], (2 + GNN_LAYERS) * NB)
            stage_end("dve", dve, None)

            for quad in range(QUADS):
                stage_start("dve", dve)
                if not quad:
                    dve.sem_inc(S["mask_used"], RING)
                    dve.sem_inc(S["s_free"], 2)
                halves = 2 * HQ
                with dve.Fori(0, NB // RING) as i:
                    for r in range(RING):
                        hold("dve", dve, S["mask_ready"], i * RING + r + 1 + quad * NB)
                        for n in range(halves):
                            o = (n % 2) * 4 * BANK
                            hold("dve", dve, S["s_free"], i * (RING * halves) + r * halves + n + 1 + quad * NB * halves)
                            hold("dve", dve, S["s_psum"], i * (RING * halves) + r * halves + n + 1 + quad * NB * halves)
                            v.tensor_tensor_reduce(
                                out=masked[:, n % 2, :].rearrange("p (c t) -> p c t", c=4),
                                in0=psum[:, o:o + 4 * BANK].rearrange("p (c t) -> p c t", c=4)[:, :, 0:CW],
                                in1=mask[:, r, (n % 2) * 4 * CW:(n % 2 + 1) * 4 * CW].rearrange("p (c t) -> p c t", c=4),
                                scale=1.0, scalar=-3e38, op0=ALU.add, op1=ALU.max,
                                accum_out=mx[:, n:n + 1]).then_inc(S["s_free"], 1)
                        hold("dve", dve, S["s_free"], i * (RING * halves) + (r + 1) * halves + 2 + quad * NB * halves)
                        v.tensor_reduce(out=mxs[:, ds(i * RING + r, 1), :].rearrange("p o h -> p (o h)"),
                                        in_=mx[:, :].rearrange("p (h c) -> p h c", c=2), op=ALU.max,
                                        axis=AX.X).then_inc(S["mask_used"], 1)
                        hold("dve", dve, S["mask_used"], i * RING + r + 1 + RING + quad * NB)
                do(v.tensor_scalar(mtmp[:, :, :], mxs[:, :, :], MASKED / 2, -1.0, ALU.is_gt, ALU.mult))
                do(v.tensor_tensor(mxs[:, :, :], mxs[:, :, :], mtmp[:, :, :], ALU.mult))
                for m in range(3):
                    do(v.tensor_copy(mb[:, :, :], mxs[:, :, :]))
                    do(v.tensor_copy(m_parts[:, :, :, m:m + 1].rearrange("p b h o -> p b (h o)"), mb[:, :, :]))
                    if m < 2:
                        do(v.tensor_tensor(mxs[:, :, :], mxs[:, :, :], mb[:, :, :], ALU.subtract))
                dve.sem_inc(S["m_parts_ready"], 1)
                stage_end("dve", dve, None)
                stage_start("dve", dve)
                pairs = 2 * NB
                if not quad:
                    dve.sem_inc(S["pw_ready"], pairs)
                with dve.Fori(0, NC) as j:
                    for n in range(pairs):
                        w = (n // 2) // SC
                        if n % (2 * SC) == 0:
                            dve.wait_ge(S["full_ready"], j * (NB // SC) + w + 1 + (quad * NC + 1) * (NB // SC))
                        dve.wait_ge(S["ex_ready"], j * pairs + n + 1 + (quad * NC + 1) * pairs)
                        dve.wait_ge(S["pw_free"], slot_again(pairs, 4, j, n) + quad * NC * pairs)
                        last = v.scalar_tensor_tensor(
                            pw[:, n % 4, :].rearrange("p (h t) -> p h t", h=2),
                            ex[:, n % 3, :].rearrange("p (h t) -> p h t", h=2), -MASKED,
                            c_full[:, w % 3, (n // 2) % SC:(n // 2) % SC + 1, :].broadcast_to([P, 2, CW]),
                            ALU.min, ALU.mult)
                        last.then_inc(S["pw_ready"], 1)
                stage_end("dve", dve, None)
            stage_start("dve", dve)
            dve.wait_ge(S["sums_back"], 16 * 2 * H)
            do(v.tensor_scalar(z[0:H, :], z[0:H, :], 0.5, None, ALU.max))
            do(v.reciprocal(z[0:H, :], z[0:H, :]))
            dve.sem_inc(S["attn_ready"], 1)
            dve.wait_ge(S["attn_psum"], 1)
            do(v.tensor_tensor(y[:, :], y[:, :], psum[:, 0:NP], ALU.mult))
            dve.sem_inc(S["attn_ready"], 1)
            dve.wait_ge(S["wo_psum"], 1)
            do(v.scalar_tensor_tensor(y[:, :], psum[:, 0:NP], V["v_bo"][:, 0:1], x[:, :], ALU.add, ALU.add))
            norm_dve(dve)
            stage_start("dve", dve)
            for b in range(NB):
                dve.wait_ge(S["out_psum"], b + 1)
                v.tensor_copy(y[:, b * P:(b + 1) * P], bank(b % 4, P)).then_inc(S["out_sb"], 1)

        @block.tensor
        def _(pe):
            t = nc.tensor
            pe.wait_ge(loaded, 16 * len(ins))
            pe.wait_ge(S["x_ready"], 1)
            for b in range(NB):
                after(pe, S["ab_taken"], b - 3)
                o = (b % 4) * BANK
                t.matmul(psum[:, o:o + 2 * P], z[:, b * P:(b + 1) * P], W["W1"][:, :],
                         start=True, stop=True).then_inc(S["ab_ready"], 1)
            pe.wait_ge(S["consts_ready"], 1)
            stage_end("pe", pe, None)

            stage_start("pe", pe)
            pe.sem_inc(S["slot_free"], 2 * PAIR0 + 4)

            def window_pe(b):
                first = pe.value_load(block_tab[0:1, 0, ds(b, 1)], min_val=0, max_val=NPAIR - 2)
                end = pe.value_load(block_tab[0:1, 1, ds(b, 1)], min_val=2, max_val=NPAIR)
                before = pe.value_load(block_tab[0:1, 2, ds(b, 1)], min_val=PAIR0 - NPAIR, max_val=PAIR0 + NB * NPAIR)
                return first, end, before

            def count_tile(slot, s, j, start):
                return t.matmul(bank(j, CW), one_dst[:, ds(slot, 1), s, :].rearrange("p o n -> p (o n)"),
                                one_src[:, ds(slot, 1), s, j * CW:(j + 1) * CW].rearrange("p o n -> p (o n)"),
                                start=start, stop=True, skip_group_check=True)

            def count_pe(b):
                first, end, before = window_pe(b)
                slot = (before + first) & 1
                pe.wait_ge(S["one_ready"], (before + first) * 2 + 2)
                for j in range(NC):
                    if not isinstance(b, int):
                        pe.wait_ge(S["chunk_free"], 8 * (b + -1) + j + 1)
                    for s in range(2):
                        last = count_tile(slot, s, j, s == 0)
                last.then_inc(S["slot_free"], 2)
                with pe.Fori(first + 1, end) as p:
                    slot = (before + p) & 1
                    for s in range(2):
                        pe.wait_ge(S["one_ready"], (before + p) * 2 + s + 1)
                        for j in range(NC):
                            last = count_tile(slot, s, j, False)
                        last.then_inc(S["slot_free"], 1)

            count_pe(0)
            with pe.Fori(1, NB) as b:
                count_pe(b)
            stage_end("pe", pe, None)

            def aggregate(q, parts, messages=None):

                def chunk(i):
                    if messages is not None:
                        pe.wait_ge(S["h_parts"], i + (1 + messages * (2 * NB // RING)))
                    for r in range(RING):
                        pe.wait_ge(c_loaded[r], steps_pe * (16 * q) + (i * 16 + 16))
                        first = r * P if isinstance(i, int) else (i % RING) * (RING * P) + r * P
                        new = isinstance(i, int) and r == 0
                        for m in range(len(parts)):
                            weights = parts[m][:, ds(first, P)] if len(parts) > 1 else parts[m]
                            for c, w in CHUNKS:
                                last = t.matmul(psum[:, c:c + w], weights, c_ring[:, r, c:c + w],
                                                start=new and m == 0, stop=True, skip_group_check=not (new and m == 0))
                        last.then_inc(S["c_used"], 1)

                chunk(0)
                with pe.Fori(1, steps_pe) as i:
                    chunk(i)

            def node_rows(q, features, weights, width, halves=None):
                for b in range(NB):
                    for n, half in enumerate(HALVES):
                        if halves and b * P == half.start:
                            after(pe, halves[0], halves[1] and halves[1] + n - 1)
                    after(pe, S["node_taken"], q * NB + b - 3 if b > 3 else 0)
                    o = (b % 4) * BANK
                    t.matmul(psum[:, o:o + width], features[:, b * P:(b + 1) * P], weights[:, 0:width],
                             start=True, stop=True).then_inc(S["node_psum"], 1)

            def feature_rows(weights, features, ready):
                for c, w in CHUNKS:
                    last = t.matmul(psum[:, c:c + w], weights[:, :], features[:, c:c + w], start=True, stop=True)
                last.then_inc(ready, 1)

            stage_start("pe", pe)
            for k in range(2):
                after(pe, S["halves_taken"], k)
                feature_rows(W["W1"][:, k * P:(k + 1) * P], z, S["halves_psum"])
            pe.wait_ge(S["halves_taken"], 2)
            steps_pe = pe.value_load(parts_tab[0:1, 0:1], min_val=RING, max_val=2 * RING)
            pe.sem_inc(S["c_used"], RING)
            for q in range(2):
                after(pe, S["deg_taken"], q)
                aggregate(q, [onesb[:, 0:P]])
                pe.drain().then_inc(S["deg_psum"], 1)
            pe.wait_ge(S["deg_taken"], 2)
            aggregate(2, [b_parts[:, m, :] for m in range(3)])
            pe.drain().then_inc(S["deg_psum"], 1)
            stage_end("pe", pe, None)

            stage_start("pe", pe)
            pe.sem_inc(S["visit_free"], VISIT0 + 2)

            def layer1(i, s):
                first, end, before = unit(pe, 2 * i + s)
                after(pe, S["r1_made"], 2 * i + s - 1)
                pe.wait_ge(a_loaded[s], 16 * i + 16)
                for k in range(UE // P):
                    last = t.matmul(psum[:, s * UE + k * P:s * UE + (k + 1) * P], a_in[:, s, k * P:(k + 1) * P],
                                    identf[:, :], start=(k % (GE // P) == 0), stop=True, skip_group_check=True)
                with pe.Fori(first, end) as b:
                    pe.wait_ge(S["visit_ready"], before + b + 1)
                    for m in range(3):
                        for half in range(2):
                            last = t.matmul(bank(2 * s + half), b_parts[:, m, ds(b * P, P)],
                                            oht[:, ds((before + b) & 1, 1), half * GE:(half + 1) * GE
                                                ].rearrange("p o e -> p (o e)"),
                                            start=False, stop=True, skip_group_check=True)
                    last.then_inc(S["visit_free"], 1)
                t.matmul(bank(2 * s, 1), zerosb[:, 0:P], zerosb[:, 0:1], start=False, stop=True,
                         skip_group_check=True).then_inc(S["h1_psum"], 1)

            def layer2(i, s):
                pe.wait_ge(S["r1_made"], 2 * i + s + 1)
                after(pe, h2_taken[3], 2 * i + s - 1)
                for half in range(2):
                    last = t.matmul(bank(4 + 2 * s + half), W["W2T"][:, :], r1[:, s, half * GE:(half + 1) * GE],
                                    start=True, stop=True)
                last.then_inc(h2_psum[3], 1)

            layer1(0, 0)
            layer1(0, 1)
            layer2(0, 0)
            with pe.Fori(1, NU // 2) as i:
                layer1(i, 0)
                layer2(i + -1, 1)
                layer1(i, 1)
                layer2(i, 0)
            layer2(NU // 2 - 1, 1)
            stage_end("pe", pe, None)

            stage_start("pe", pe)
            pe.wait_ge(S["w2_ready"], 1)
            t.transpose(bank(6, P), w2t[:, :], identf[:, :])
            t.transpose(bank(7)[0:3, 0:P], col_f[:, 0:3], identf[:, :]).then_inc(S["w2_psum"], 1)
            pe.wait_ge(S["bn2_ready"], 1)
            pe.sem_inc(S["agg_psum"], VISIT0 + 1)

            def layer2_rows(i, s):
                pe.wait_ge(r1_loaded[s], 16 * i + 16)
                after(pe, h2_taken[4], 2 * i + s - 1)
                for half in range(2):
                    t.matmul(bank(2 * s + half), onesb[0:3, 0:P], row3[:, :], start=True, stop=True)
                for k in range(UE // P):
                    last = t.matmul(psum[:, s * UE + k * P:s * UE + (k + 1) * P], a_in[:, s, k * P:(k + 1) * P],
                                    w2s[:, :], start=False, stop=True, skip_group_check=True)
                last.then_inc(h2_psum[4], 1)

            def sum_edges(i, s):
                first, end, before = unit(pe, 2 * i + s)
                hold("pe", pe, h2_taken[4], 2 * i + s + 1)
                with pe.Fori(first, end) as b:
                    pe.wait_ge(S["agg_taken"], before + b)
                    pe.wait_ge(S["agg_ready"], before + b + 1)
                    for k in range(UE // P):
                        last = t.matmul(bank(4, P), u[:, s, k * P:(k + 1) * P],
                                        ohd[:, ds((before + b) & 1, 1), k * P:(k + 1) * P
                                            ].rearrange("p o e -> p (o e)"),
                                        start=(k == 0), stop=(k == UE // P - 1))
                    last.then_inc(S["agg_psum"], 1)
                t.matmul(bank(6, 1), zerosb[:, 0:P], zerosb[:, 0:1], start=True, stop=True
                         ).then_inc(S["agg_done"], 1)

            layer2_rows(0, 0)
            layer2_rows(0, 1)
            sum_edges(0, 0)
            with pe.Fori(1, NU // 2) as i:
                layer2_rows(i, 0)
                sum_edges(i + -1, 1)
                layer2_rows(i, 1)
                sum_edges(i, 0)
            sum_edges(NU // 2 - 1, 1)
            norm_pe(pe)
            stage_end("pe", pe, None)

            stage_start("pe", pe)
            for b in range(NB):
                last = t.matmul(bank(7)[:, 3 * b:3 * b + 3], hT[:, b * P:(b + 1) * P], identf[:, 0:3],
                                start=True, stop=True)
            last.then_inc(S["nd_psum"], 1)
            node_rows(0, x, W["Wfb"], 2 * P)
            parts = [hp[:, m, :] for m in range(3)]
            for k, q in enumerate((3, 4)):
                if not k:
                    pe.wait_ge(S["node_taken"], NB)
                aggregate(q, parts, k)
                for b in range(NB):
                    for m in range(3):
                        last = t.matmul(psum[:, b * P:(b + 1) * P], hp[:, m, b * P:(b + 1) * P], identb[:, :],
                                        start=False, stop=True, skip_group_check=True)
                last.then_inc(S["agg_sum"], 1)
            norm_pe(pe)
            stage_end("pe", pe, None)

            stage_start("pe", pe)
            feature_rows(W["WiT"], x, S["hT_psum"])
            pe.wait_ge(S["weff_ready"], 1)
            pe.wait_ge(S["hT_ready"], 1)
            for k in range(GNN_LAYERS):
                node_rows(1 + k, hT, weff, P, (S["hT_next"], 2 * k))
                pe.wait_ge(S["node_taken"], (2 + k) * NB)
                feature_rows(W["WAT"], hT, S["asym_psum"])
                pe.wait_ge(S["asym_taken"], k + 1)
                aggregate(5 + k, parts, 2 + k)
                pe.drain().then_inc(S["agg_sum"], 1)
            norm_pe(pe)
            stage_end("pe", pe, None)

            stage_start("pe", pe)
            feature_rows(W["WqT"], x, S["qk_psum"])
            pe.wait_ge(S["qk_scaled"], 1)
            feature_rows(W["WkT"], x, S["qk_psum"])
            pe.wait_ge(S["qk_scaled"], 2)
            node_rows(1 + GNN_LAYERS, x, W["WvT"], P)
            stage_end("pe", pe, None)

            for quad in range(QUADS):
                stage_start("pe", pe)
                pe.wait_ge(packed, 16 * 2 * len(QK_SLOTS) * (quad + 1))
                halves = 2 * HQ
                with pe.Fori(0, NB) as b:
                    for n in range(halves):
                        hold("pe", pe, S["s_free"], b * halves + n + 1 + quad * NB * halves)
                        for c in range(4):
                            last = t.matmul(bank((n % 2) * 4 + c, CW), kp[0:KQK, n // 2, ds(b * P, P)],
                                            qp[0:KQK, n // 2, ((n % 2) * 4 + c) * CW:((n % 2) * 4 + c + 1) * CW],
                                            start=True, stop=True)
                        last.then_inc(S["s_psum"], 1)
                pe.wait_ge(S["m_parts_ready"], quad + 1)
                for b in range(NB):
                    last = t.transpose(psum[0:HQ * 3, b * P:(b + 1) * P],
                                       m_parts[:, b, :, :].rearrange("p h m -> p (h m)"), identf[:, :])
                last.then_inc(S["m_rows_psum"], 1)
                stage_end("pe", pe, None)
                stage_start("pe", pe)
                pairs = 2 * NB
                if not quad:
                    pe.sem_inc(S["pw_free"], pairs)
                    pe.sem_inc(S["pv_taken"], 1)

                def scores(j, n):
                    pe.wait_ge(S["ex_ready"], slot_again(pairs, 3, j, n) + quad * NC * pairs)
                    s0 = (n // 2) * P
                    for e in range(2):
                        hh = (n % 2) * 2 + e
                        last = t.matmul(bank(2 * (n % 3) + e, CW), qp[0:KQK + 3, hh, s0:s0 + P],
                                        kp[0:KQK + 3, hh, ds(j * CW, CW)], start=True, stop=True)
                    last.then_inc(S["sc_psum"], 1)

                with pe.Fori(0, NC) as j:
                    for n in range(3):
                        scores(j, n)
                    for k in range(NB):
                        for n in (2 * k + 3, 2 * k + 4):
                            if n < pairs:
                                scores(j, n)
                        if k == 0:
                            hold("pe", pe, S["pv_taken"], j + 1 + quad * NC)
                        pe.wait_ge(S["pw_ready"], j * pairs + 2 * k + 2 + (quad * NC + 1) * pairs)
                        for hh in range(HQ):
                            last = t.matmul(psum[hh * HW:(hh + 1) * HW, 6 * BANK:6 * BANK + CW],
                                            vaug[:, k, quad * HQ + hh, :],
                                            pw[:, (2 * k + hh // 2) % 4, (hh % 2) * CW:(hh % 2 + 1) * CW],
                                            start=(k == 0), stop=(k == NB - 1))
                        last.then_inc(S["pw_free"], 2)
                stage_end("pe", pe, None)
            stage_start("pe", pe)
            pe.wait_ge(S["attn_ready"], 1)
            for c, w in CHUNKS:
                last = t.matmul(psum[:, c:c + w], selh[:, :], z[0:H, c:c + w], start=True, stop=True)
            last.then_inc(S["attn_psum"], 1)
            pe.wait_ge(S["attn_ready"], 2)
            feature_rows(W["WoT"], y, S["wo_psum"])
            norm_pe(pe)
            stage_end("pe", pe, None)

            stage_start("pe", pe)
            for b in range(NB):
                after(pe, S["out_sb"], b - 3)
                t.transpose(bank(b % 4, P), x[:, b * P:(b + 1) * P], identf[:, :]).then_inc(S["out_psum"], 1)


_INS = ["x", "src", "dst", "L0_gnn_W1", "L0_gnn_b1", "L0_gnn_g1", "L0_gnn_be1", "L0_gnn_W2", "L0_gnn_b2", "L0_gnn_g2",
        "L0_gnn_be2", "L1_gnn_W_fwd", "L1_gnn_b_fwd", "L1_gnn_W_bwd", "L1_gnn_b_bwd", "L2_gnn_Wi", "L2_gnn_bi",
        "L2_gnn_A", "L2_gnn_Wp", "L3_gnn_Wq", "L3_gnn_bq", "L3_gnn_Wk", "L3_gnn_bk", "L3_gnn_Wv", "L3_gnn_bv",
        "L3_gnn_Wo", "L3_gnn_bo"]


def kernel(**inputs):
    import numpy as _np
    import concourse.bacc as _bacc
    from concourse import mybir as _mybir
    from concourse.bass_utils import run_bass_kernel_spmd as _run

    a = {n: _np.asarray(inputs[n]) for n in _INS}

    def edges(e):
        padded = _np.full((EP,), NP - 1, e.dtype)
        padded[:E] = e
        return padded

    src, dst = edges(a["src"]), edges(a["dst"])
    wp = a["L2_gnn_Wp"]
    laid = {
        "xT": a["x"].T,
        "src_cols": src.reshape(NT, P).T,
        "dst_cols": dst.reshape(NT, P).T,
        "dst_rows": dst.reshape(1, EP),
        "W1": a["L0_gnn_W1"].T.reshape(2, P, P).transpose(1, 0, 2).reshape(P, 2 * P),
        "W2": a["L0_gnn_W2"],
        "W2T": a["L0_gnn_W2"].T,
        "Wfb": _np.concatenate([a["L1_gnn_W_fwd"], a["L1_gnn_W_bwd"]], axis=1),
        "WiT": a["L2_gnn_Wi"].T,
        "WA": a["L2_gnn_A"],
        "WAT": a["L2_gnn_A"].T,
        "Wp": wp[:, :P],
        "WpT": wp[:, :P].T,
        "WqT": a["L3_gnn_Wq"].T,
        "WkT": a["L3_gnn_Wk"].T,
        "WvT": a["L3_gnn_Wv"].T,
        "WoT": a["L3_gnn_Wo"].T,
        "v_b1": a["L0_gnn_b1"].reshape(P, 1), "v_g1": a["L0_gnn_g1"].reshape(P, 1),
        "v_be1": a["L0_gnn_be1"].reshape(P, 1), "v_b2": a["L0_gnn_b2"].reshape(P, 1),
        "v_g2": a["L0_gnn_g2"].reshape(P, 1), "v_be2": a["L0_gnn_be2"].reshape(P, 1),
        "v_bf": a["L1_gnn_b_fwd"].reshape(P, 1), "v_bb": a["L1_gnn_b_bwd"].reshape(P, 1),
        "v_bi": a["L2_gnn_bi"].reshape(P, 1), "v_q": wp[:, P:P + 1], "v_r": wp[:, P + 1:P + 2],
        "v_bq": a["L3_gnn_bq"].reshape(P, 1), "v_bk": a["L3_gnn_bk"].reshape(P, 1),
        "v_bv": a["L3_gnn_bv"].reshape(P, 1), "v_bo": a["L3_gnn_bo"].reshape(P, 1),
    }
    nc = _bacc.Bacc("TRN2", target_bir_lowering=False, num_devices=1)
    arrays, ins = {}, {}
    for name, array in laid.items():
        array = _np.ascontiguousarray(array)
        arrays[f"in_{name}"] = array
        ins[name] = nc.dram_tensor(f"in_{name}", array.shape, _mybir.dt.from_np(array.dtype), kind="ExternalInput").ap()
    out = nc.dram_tensor("out_x", (N, P), _mybir.dt.float32, kind="ExternalOutput").ap()
    gnn(nc, ins, out)
    r = _run(nc, [arrays], core_ids=[0])
    return r.results[0]["out_x"]
```
